# Optimizing a Trainium2 kernel written in Bass

```python
import numpy as np
import jax
import jax.numpy as jnp

def _softmax(x, axis=-1):
    return jax.nn.softmax(x, axis=axis)

def _gelu(x):
    return jax.nn.gelu(x, approximate=True)

def _silu(x):
    return jax.nn.silu(x)

def _sigmoid(x):
    return jax.nn.sigmoid(x)

def _layernorm(x, axis=-1, eps=1e-05):
    m = jnp.mean(x, axis=axis, keepdims=True)
    v = jnp.var(x, axis=axis, keepdims=True)
    return (x - m) / jnp.sqrt(v + eps)

def _scatter_add(tgt, idx, src, axis=0):
    return tgt.at[idx].add(src)

def _segment_sum(src, seg, n):
    return jax.ops.segment_sum(src, seg, n)
kernel_name = 'mk_adaln_d4_jaxref_r8_2134bb'

def setup_inputs(seed: int=0):
    np.random.seed(seed)
    _w = jnp.asarray

    def _L0_attn_setup():
        import jax, jax.numpy as jnp
        import numpy as np
        B, L, D = (8, 512, 128)
        K = 32
        key = jax.random.key(seed)
        kx, kw, kb = jax.random.split(key, 3)
        x = jax.random.normal(kx, (B, L, D), dtype=jnp.float32)
        W = jax.random.normal(kw, (K, D), dtype=jnp.float32) * 0.02
        b = jax.random.normal(kb, (K,), dtype=jnp.float32) * 0.02
        return {'x': x, 'W': W, 'b': b}
    _L0_attn_in = _L0_attn_setup()

    def _L0_ffn_setup():
        import jax, jax.numpy as jnp
        import numpy as np
        D_MODEL, D_FF, RANK = (128, 512, 32)
        B, S = (4, 512)
        key = jax.random.key(seed)
        ks = jax.random.split(key, 7)
        return {'x': jax.random.normal(ks[0], (B, S, D_MODEL), dtype=jnp.float32), 'U1': jax.random.normal(ks[1], (D_MODEL, RANK), dtype=jnp.float32) * 0.02, 'V1': jax.random.normal(ks[2], (RANK, D_FF), dtype=jnp.float32) * 0.02, 'b1': jnp.zeros((D_FF,), dtype=jnp.float32), 'U2': jax.random.normal(ks[3], (D_FF, RANK), dtype=jnp.float32) * 0.02, 'V2': jax.random.normal(ks[4], (RANK, D_MODEL), dtype=jnp.float32) * 0.02, 'b2': jnp.zeros((D_MODEL,), dtype=jnp.float32)}
    _L0_ffn_in = _L0_ffn_setup()
    _L0_c = _w((lambda *s: np.random.randn(*s).astype(np.float32) * 0.05)(4, 128))
    _L0_wmod = _w((lambda *s: np.random.randn(*s).astype(np.float32) * 0.05)(128, 6 * 128) * 128 ** (-0.5))

    def _L1_attn_setup():
        import jax, jax.numpy as jnp
        import numpy as np
        key = jax.random.key(seed)
        ks = jax.random.split(key, 4)
        B, S, D = (4, 512, 128)
        scale = 1.0 / np.sqrt(D)
        return {'inputs': jax.random.normal(ks[0], (B, S, D), dtype=jnp.float32), 'Wa': jax.random.normal(ks[1], (D, D), dtype=jnp.float32) * scale, 'ba': jnp.zeros((D,), dtype=jnp.float32), 'Wb': jax.random.normal(ks[2], (D, D), dtype=jnp.float32) * scale, 'bb': jnp.zeros((D,), dtype=jnp.float32), 'Wc': jax.random.normal(ks[3], (D, D), dtype=jnp.float32) * scale, 'bc': jnp.zeros((D,), dtype=jnp.float32)}
    _L1_attn_in = _L1_attn_setup()

    def _L1_ffn_setup():
        import jax, jax.numpy as jnp
        import numpy as np
        E, G, TOPK = (32, 16, 2)
        HID, INTER, A_INTER = (128, 256, 128)
        CAP_FACTOR = 1.25
        SCALE = 0.05

        def _stats(x):
            mean = x.mean(-1, keepdims=True)
            std = jnp.std(x, axis=-1, keepdims=True, ddof=1)
            mn = x.min(-1, keepdims=True)
            mx = x.max(-1, keepdims=True)
            l2 = jnp.linalg.norm(x, axis=-1, keepdims=True)
            sp = (jnp.abs(x) < 1e-06).astype(x.dtype).mean(-1, keepdims=True)
            return jnp.concatenate([mean, std, mn, mx, l2, sp], -1)
        key = jax.random.key(seed)
        ks = jax.random.split(key, 8)
        B, N = (4, 128)
        s = lambda k, shape, sc: jax.random.normal(k, shape, jnp.float32) * sc
        return {'x': jax.random.normal(ks[0], (B, N, HID), jnp.float32), 'r1_w': s(ks[1], (HID // 2, HID + 6), 0.02), 'r1_b': jnp.zeros((HID // 2,), jnp.float32), 'r2_w': s(ks[2], (E, HID // 2), 0.02), 'w_up': s(ks[3], (E, 2 * INTER, HID), 0.02), 'w_down': s(ks[4], (E, HID, INTER), 0.02), 'a_up': s(ks[5], (G, 2 * A_INTER, HID), 0.02), 'a_down': s(ks[6], (G, HID, A_INTER), 0.02)}
    _L1_ffn_in = _L1_ffn_setup()
    _L1_c = _w((lambda *s: np.random.randn(*s).astype(np.float32) * 0.05)(4, 128))
    _L1_wmod = _w((lambda *s: np.random.randn(*s).astype(np.float32) * 0.05)(128, 6 * 128) * 128 ** (-0.5))

    def _L2_attn_setup():
        import jax, jax.numpy as jnp
        import numpy as np
        HEADS = 16
        DIM_HEAD = 64
        B, T, C = (4, 256, 128)

        def apply_rope(x):
            d = x.shape[-1]
            seq_len = x.shape[1]
            inv_freq = 1.0 / 10000.0 ** (jnp.arange(0, d, 2, dtype=jnp.float32) / d)
            pos = jnp.arange(seq_len, dtype=jnp.float32)
            ang = pos[:, None] * inv_freq[None, :]
            sin = jnp.sin(ang)[None]
            cos = jnp.cos(ang)[None]
            x1, x2 = (x[..., 0::2], x[..., 1::2])
            rot = jnp.stack([x1 * cos - x2 * sin, x1 * sin + x2 * cos], axis=-1)
            return rot.reshape(x.shape)
        key = jax.random.key(seed)
        ks = jax.random.split(key, 6)
        inner = HEADS * DIM_HEAD
        w = 0.02
        return {'x': jax.random.normal(ks[0], (B, T, C), dtype=jnp.float32), 'Wq': jax.random.normal(ks[1], (C, inner), dtype=jnp.float32) * w, 'Wk': jax.random.normal(ks[2], (C, inner), dtype=jnp.float32) * w, 'Wv': jax.random.normal(ks[3], (C, inner), dtype=jnp.float32) * w, 'Wo': jax.random.normal(ks[4], (inner, C), dtype=jnp.float32) * w, 'bo': jnp.zeros((C,), dtype=jnp.float32)}
    _L2_attn_in = _L2_attn_setup()

    def _L2_ffn_setup():
        import jax, jax.numpy as jnp
        import numpy as np
        DIM = 128

        def _reference_tuple_inner(x, W_r, W_k, W_v, mu_r, mu_k):
            B, T, C = x.shape
            x_prev = jnp.concatenate([jnp.zeros((B, 1, C), x.dtype), x[:, :-1, :]], axis=1)
            xr = mu_r * x + (1.0 - mu_r) * x_prev
            xk = mu_k * x + (1.0 - mu_k) * x_prev
            r = jax.nn.sigmoid(jnp.einsum('btc,dc->btd', xr, W_r))
            k = jnp.einsum('btc,dc->btd', xk, W_k)
            k_act = jnp.square(jax.nn.relu(k))
            out = r * jnp.einsum('btc,dc->btd', k_act, W_v)
            new_state = x[:, -1, :]
            return (out, new_state)
        key = jax.random.key(seed)
        ks = jax.random.split(key, 6)
        B, T, C = (8, 256, DIM)
        x = jax.random.normal(ks[0], (B, T, C), dtype=jnp.float32)
        s = 1.0 / np.sqrt(C)
        W_r = jax.random.uniform(ks[1], (C, C), jnp.float32, -s, s)
        W_k = jax.random.uniform(ks[2], (C, C), jnp.float32, -s, s)
        W_v = jax.random.uniform(ks[3], (C, C), jnp.float32, -s, s)
        mu_r = jax.random.uniform(ks[4], (C,), jnp.float32)
        mu_k = jax.random.uniform(ks[5], (C,), jnp.float32)
        return {'x': x, 'W_r': W_r, 'W_k': W_k, 'W_v': W_v, 'mu_r': mu_r, 'mu_k': mu_k}
    _L2_ffn_in = _L2_ffn_setup()
    _L2_c = _w((lambda *s: np.random.randn(*s).astype(np.float32) * 0.05)(4, 128))
    _L2_wmod = _w((lambda *s: np.random.randn(*s).astype(np.float32) * 0.05)(128, 6 * 128) * 128 ** (-0.5))

    def _L3_attn_setup():
        import math
        import jax, jax.numpy as jnp
        import numpy as np
        N_HEADS = 16
        N_KV_HEADS = 4
        HEAD_DIM = 64
        DIM = 128
        WINDOW = 16
        EPS = 0.01

        def _alibi_slopes(n_heads):
            closest = 2 ** math.floor(math.log2(n_heads))
            base = 2.0 ** (-2.0 ** (-(math.log2(closest) - 3)))
            slopes = base ** np.arange(1, closest + 1, dtype=np.float32)
            if closest < n_heads:
                eb = 2.0 ** (-2.0 ** (-(math.log2(2 * closest) - 3)))
                extra = eb ** np.arange(1, 2 * (n_heads - closest) + 1, 2, dtype=np.float32)
                slopes = np.concatenate([slopes, extra])
            return jnp.asarray(slopes[:n_heads])

        def _rmsnorm(x, w):
            xf = x.astype(jnp.float32)
            norm = jax.lax.rsqrt(jnp.mean(xf * xf, axis=-1, keepdims=True) + EPS)
            return (xf * norm).astype(x.dtype) * w
        key = jax.random.key(seed)
        ks = jax.random.split(key, 6)
        B, L = (2, 256)
        s = 1.0 / math.sqrt(DIM)
        return {'x': jax.random.normal(ks[0], (B, L, DIM), jnp.float32), 'wq': jax.random.normal(ks[1], (N_HEADS * HEAD_DIM, DIM), jnp.float32) * s, 'wk': jax.random.normal(ks[2], (N_KV_HEADS * HEAD_DIM, DIM), jnp.float32) * s, 'wv': jax.random.normal(ks[3], (N_KV_HEADS * HEAD_DIM, DIM), jnp.float32) * s, 'wo': jax.random.normal(ks[4], (DIM, N_HEADS * HEAD_DIM), jnp.float32) * s, 'q_norm_w': jnp.ones((HEAD_DIM,), jnp.float32), 'k_norm_w': jnp.ones((HEAD_DIM,), jnp.float32)}
    _L3_attn_in = _L3_attn_setup()

    def _L3_ffn_setup():
        import jax, jax.numpy as jnp
        import numpy as np
        DIM = 128
        DEPTH = 2
        HEADS = 8
        DIM_HEAD = 64
        WINDOW = 64
        INNER = HEADS * DIM_HEAD
        HID = int(DIM * 4 * 2 / 3)
        B, N = (2, 1024)
        QK_SCALE = 8.0

        def shift_token(t):
            t1, t2 = jnp.split(t, 2, axis=-1)
            t2 = jnp.pad(t2, ((0, 0), (1, 0), (0, 0)))[:, :-1]
            return jnp.concatenate([t1, t2], axis=-1)

        def l2norm(t):
            return t / jnp.clip(jnp.linalg.norm(t, axis=-1, keepdims=True), 1e-12)

        def rotate_half(x):
            x1, x2 = jnp.split(x, 2, axis=-1)
            return jnp.concatenate([-x2, x1], axis=-1)

        def rotary_xpos(q, k):
            n = q.shape[-2]
            half_idx = jnp.arange(0, DIM_HEAD, 2, dtype=jnp.float32)
            inv_freq = 1.0 / 10000.0 ** (half_idx / DIM_HEAD)
            t = jnp.arange(n, dtype=jnp.float32)
            freqs = t[:, None] * inv_freq[None, :]
            freqs = jnp.concatenate([freqs, freqs], axis=-1)
            base = (half_idx + 0.4 * DIM_HEAD) / (1.4 * DIM_HEAD)
            power = (t - n // 2) / float(WINDOW // 2)
            scale = base[None, :] ** power[:, None]
            scale = jnp.concatenate([scale, scale], axis=-1)
            cos, sin = (jnp.cos(freqs), jnp.sin(freqs))
            q = q * cos * scale + rotate_half(q) * sin * scale
            k = k * cos / scale + rotate_half(k) * sin / scale
            return (q, k)

        def local_attention(q, k, v):
            b, h, n, d = q.shape
            w = n // WINDOW
            bq = q.reshape(b, h, w, WINDOW, d) * QK_SCALE
            bk = k.reshape(b, h, w, WINDOW, d)
            bv = v.reshape(b, h, w, WINDOW, d)

            def look_around(t):
                p = jnp.pad(t, ((0, 0), (0, 0), (1, 0), (0, 0), (0, 0)))
                return jnp.concatenate([p[:, :, :w], p[:, :, 1:]], axis=3)
            bk, bv = (look_around(bk), look_around(bv))
            bt = jnp.arange(n).reshape(w, WINDOW)
            btp = jnp.pad(bt, ((1, 0), (0, 0)), constant_values=-1)
            btk = jnp.concatenate([btp[:w], btp[1:]], axis=1)
            sim = jnp.einsum('bhwid,bhwjd->bhwij', bq, bk)
            i = bt[:, :, None]
            j = btk[:, None, :]
            mask = (i < j) | (i > j + WINDOW) | (j == -1)
            sim = jnp.where(mask, -jnp.finfo(sim.dtype).max, sim)
            attn = jax.nn.softmax(sim, axis=-1)
            out = jnp.einsum('bhwij,bhwjd->bhwid', attn, bv)
            return out.reshape(b, h, n, d)

        def _layer(x, wqkv, qs, ksc, wo, lg, lb, w1, b1, w2, b2):
            b, n, _ = x.shape
            h = shift_token(x)
            qkv = h @ wqkv
            q, k, v = jnp.split(qkv, 3, axis=-1)
            to_heads = lambda t: t.reshape(b, n, HEADS, DIM_HEAD).transpose(0, 2, 1, 3)
            q, k, v = (to_heads(q), to_heads(k), to_heads(v))
            q = l2norm(q) * qs
            k = l2norm(k) * ksc
            q, k = rotary_xpos(q, k)
            o = local_attention(q, k, v)
            o = o.transpose(0, 2, 1, 3).reshape(b, n, INNER)
            x = x + o @ wo
            h = shift_token(x)
            mu = h.mean(-1, keepdims=True)
            var = h.var(-1, keepdims=True)
            h = (h - mu) / jnp.sqrt(var + 1e-05) * lg + lb
            h = h @ w1 + b1
            a, g = jnp.split(h, 2, axis=-1)
            h = a * jax.nn.gelu(g, approximate=False)
            x = x + h @ w2 + b2
            return x
        key = jax.random.key(seed)
        ks = jax.random.split(key, 6)
        return {'x': jax.random.normal(ks[0], (B, N, DIM), jnp.float32), 'wqkv': jax.random.normal(ks[1], (DEPTH, DIM, 3 * INNER), jnp.float32) * 0.02, 'q_scale': jnp.ones((DEPTH, DIM_HEAD), jnp.float32), 'k_scale': jnp.ones((DEPTH, DIM_HEAD), jnp.float32), 'wo': jax.random.normal(ks[2], (DEPTH, INNER, DIM), jnp.float32) * 0.02, 'ln_g': jnp.ones((DEPTH, DIM), jnp.float32), 'ln_b': jnp.zeros((DEPTH, DIM), jnp.float32), 'w1': jax.random.normal(ks[3], (DEPTH, DIM, 2 * HID), jnp.float32) * 0.02, 'b1': jnp.zeros((DEPTH, 2 * HID), jnp.float32), 'w2': jax.random.normal(ks[4], (DEPTH, HID, DIM), jnp.float32) * 0.02, 'b2': jnp.zeros((DEPTH, DIM), jnp.float32)}
    _L3_ffn_in = _L3_ffn_setup()
    _L3_c = _w((lambda *s: np.random.randn(*s).astype(np.float32) * 0.05)(4, 128))
    _L3_wmod = _w((lambda *s: np.random.randn(*s).astype(np.float32) * 0.05)(128, 6 * 128) * 128 ** (-0.5))
    _d = {'L0_attn_x': _L0_attn_in['x'], 'L0_attn_W': _L0_attn_in['W'], 'L0_attn_b': _L0_attn_in['b'], 'L0_ffn_U1': _L0_ffn_in['U1'], 'L0_ffn_V1': _L0_ffn_in['V1'], 'L0_ffn_b1': _L0_ffn_in['b1'], 'L0_ffn_U2': _L0_ffn_in['U2'], 'L0_ffn_V2': _L0_ffn_in['V2'], 'L0_ffn_b2': _L0_ffn_in['b2'], 'L0_c': _L0_c, 'L0_wmod': _L0_wmod, 'L1_attn_Wa': _L1_attn_in['Wa'], 'L1_attn_ba': _L1_attn_in['ba'], 'L1_attn_Wb': _L1_attn_in['Wb'], 'L1_attn_bb': _L1_attn_in['bb'], 'L1_attn_Wc': _L1_attn_in['Wc'], 'L1_attn_bc': _L1_attn_in['bc'], 'L1_ffn_r1_w': _L1_ffn_in['r1_w'], 'L1_ffn_r1_b': _L1_ffn_in['r1_b'], 'L1_ffn_r2_w': _L1_ffn_in['r2_w'], 'L1_ffn_w_up': _L1_ffn_in['w_up'], 'L1_ffn_w_down': _L1_ffn_in['w_down'], 'L1_ffn_a_up': _L1_ffn_in['a_up'], 'L1_ffn_a_down': _L1_ffn_in['a_down'], 'L1_c': _L1_c, 'L1_wmod': _L1_wmod, 'L2_attn_Wq': _L2_attn_in['Wq'], 'L2_attn_Wk': _L2_attn_in['Wk'], 'L2_attn_Wv': _L2_attn_in['Wv'], 'L2_attn_Wo': _L2_attn_in['Wo'], 'L2_attn_bo': _L2_attn_in['bo'], 'L2_ffn_W_r': _L2_ffn_in['W_r'], 'L2_ffn_W_k': _L2_ffn_in['W_k'], 'L2_ffn_W_v': _L2_ffn_in['W_v'], 'L2_ffn_mu_r': _L2_ffn_in['mu_r'], 'L2_ffn_mu_k': _L2_ffn_in['mu_k'], 'L2_c': _L2_c, 'L2_wmod': _L2_wmod, 'L3_attn_wq': _L3_attn_in['wq'], 'L3_attn_wk': _L3_attn_in['wk'], 'L3_attn_wv': _L3_attn_in['wv'], 'L3_attn_wo': _L3_attn_in['wo'], 'L3_attn_q_norm_w': _L3_attn_in['q_norm_w'], 'L3_attn_k_norm_w': _L3_attn_in['k_norm_w'], 'L3_ffn_wqkv': _L3_ffn_in['wqkv'], 'L3_ffn_q_scale': _L3_ffn_in['q_scale'], 'L3_ffn_k_scale': _L3_ffn_in['k_scale'], 'L3_ffn_wo': _L3_ffn_in['wo'], 'L3_ffn_ln_g': _L3_ffn_in['ln_g'], 'L3_ffn_ln_b': _L3_ffn_in['ln_b'], 'L3_ffn_w1': _L3_ffn_in['w1'], 'L3_ffn_b1': _L3_ffn_in['b1'], 'L3_ffn_w2': _L3_ffn_in['w2'], 'L3_ffn_b2': _L3_ffn_in['b2'], 'L3_c': _L3_c, 'L3_wmod': _L3_wmod}
    _x0 = _d['L0_attn_x']
    _d['L0_attn_x'] = jax.random.normal(jax.random.fold_in(jax.random.key(seed), 1), (4, 512, 128), dtype=_x0.dtype)
    del _x0
    return _d

def reference(L0_attn_x, L0_attn_W, L0_attn_b, L0_ffn_U1, L0_ffn_V1, L0_ffn_b1, L0_ffn_U2, L0_ffn_V2, L0_ffn_b2, L0_c, L0_wmod, L1_attn_Wa, L1_attn_ba, L1_attn_Wb, L1_attn_bb, L1_attn_Wc, L1_attn_bc, L1_ffn_r1_w, L1_ffn_r1_b, L1_ffn_r2_w, L1_ffn_w_up, L1_ffn_w_down, L1_ffn_a_up, L1_ffn_a_down, L1_c, L1_wmod, L2_attn_Wq, L2_attn_Wk, L2_attn_Wv, L2_attn_Wo, L2_attn_bo, L2_ffn_W_r, L2_ffn_W_k, L2_ffn_W_v, L2_ffn_mu_r, L2_ffn_mu_k, L2_c, L2_wmod, L3_attn_wq, L3_attn_wk, L3_attn_wv, L3_attn_wo, L3_attn_q_norm_w, L3_attn_k_norm_w, L3_ffn_wqkv, L3_ffn_q_scale, L3_ffn_k_scale, L3_ffn_wo, L3_ffn_ln_g, L3_ffn_ln_b, L3_ffn_w1, L3_ffn_b1, L3_ffn_w2, L3_ffn_b2, L3_c, L3_wmod):

    def _L0_attn_ref(x, W, b):
        import jax, jax.numpy as jnp
        import numpy as np
        B, L, D = (8, 512, 128)
        K = 32
        logits = jnp.einsum('bld,kd->blk', x, W) + b
        w = jax.nn.softmax(logits, axis=-1)
        Bn, Ln, Dn = x.shape
        Kn = w.shape[-1]
        xp = jnp.pad(x, ((0, 0), (0, Kn - 1), (0, 0)))
        out = jnp.zeros_like(x)
        for d in range(Kn):
            out = out + w[:, :, d:d + 1] * xp[:, d:d + Ln]
        return out

    def _L0_ffn_ref(x, U1, V1, b1, U2, V2, b2):
        import jax, jax.numpy as jnp
        import numpy as np
        D_MODEL, D_FF, RANK = (128, 512, 32)
        B, S = (4, 512)
        P = jnp.einsum('bsd,dr->bsr', x, U1)
        H = jax.nn.gelu(jnp.einsum('bsr,rf->bsf', P, V1) + b1)
        Q = jnp.einsum('bsf,fr->bsr', H, U2)
        return jnp.einsum('bsr,rd->bsd', Q, V2) + b2

    def _L1_attn_ref(inputs, Wa, ba, Wb, bb, Wc, bc):
        import jax, jax.numpy as jnp
        import numpy as np
        a = jax.nn.sigmoid(jnp.einsum('bsd,ed->bse', inputs, Wa) + ba)
        b = jnp.tanh(jnp.einsum('bsd,ed->bse', inputs, Wb) + bb)
        c = jax.nn.sigmoid(jnp.einsum('bsd,ed->bse', inputs, Wc) + bc)
        B, S, D = inputs.shape

        def step(state, abc):
            a_t, b_t, c_t = abc
            state = a_t * state + (1.0 - a_t) * b_t
            return (state, c_t * state)
        abc = (jnp.swapaxes(a, 0, 1), jnp.swapaxes(b, 0, 1), jnp.swapaxes(c, 0, 1))
        init = jnp.zeros((B, D), dtype=inputs.dtype)
        _, ys = jax.lax.scan(step, init, abc)
        return jnp.swapaxes(ys, 0, 1)

    def _L1_ffn_ref(x, r1_w, r1_b, r2_w, w_up, w_down, a_up, a_down):
        import jax, jax.numpy as jnp
        import numpy as np
        E, G, TOPK = (32, 16, 2)
        HID, INTER, A_INTER = (128, 256, 128)
        CAP_FACTOR = 1.25
        SCALE = 0.05

        def _stats(x):
            mean = x.mean(-1, keepdims=True)
            std = jnp.std(x, axis=-1, keepdims=True, ddof=1)
            mn = x.min(-1, keepdims=True)
            mx = x.max(-1, keepdims=True)
            l2 = jnp.linalg.norm(x, axis=-1, keepdims=True)
            sp = (jnp.abs(x) < 1e-06).astype(x.dtype).mean(-1, keepdims=True)
            return jnp.concatenate([mean, std, mn, mx, l2, sp], -1)
        B, N, C = x.shape
        xf = x.reshape(-1, C)
        T = xf.shape[0]
        cap = int(CAP_FACTOR * T / E)
        ri = jnp.concatenate([xf, _stats(xf)], -1)
        h = jax.nn.gelu(ri @ r1_w.T + r1_b, approximate=False)
        probs = jax.nn.softmax(h @ r2_w.T, -1)
        topp, topi = jax.lax.top_k(probs, TOPK)
        wnorm = topp / topp.sum(-1, keepdims=True)
        eids = jnp.arange(E)
        hit = topi[..., None] == eids
        routed = hit.any(1)
        Wc = jnp.where(hit, wnorm[..., None], 0.0).sum(1)
        score = jnp.where(routed, probs, -jnp.inf)
        idx = jnp.argsort(-score, axis=0)[:cap].T
        valid = jnp.take_along_axis(routed.T, idx, 1)
        w = jnp.take_along_axis(Wc.T, idx, 1) * valid
        xe = xf[idx]
        up = jnp.einsum('eci,eji->ecj', xe, w_up)
        gate, upv = jnp.split(up, 2, axis=-1)
        hact = jax.nn.silu(gate) * upv
        ye = jnp.einsum('ecj,eoj->eco', hact, w_down)
        out = jnp.zeros((T, C), xf.dtype).at[idx.reshape(-1)].add((w[..., None] * ye).reshape(-1, C))
        Wmask = jnp.zeros((T, E), xf.dtype).at[idx, eids[:, None]].add(w)
        gw = SCALE * Wmask.reshape(T, G, E // G).sum(-1)
        aup = jnp.einsum('tc,gjc->tgj', xf, a_up)
        ag, av = jnp.split(aup, 2, axis=-1)
        ah = jax.nn.silu(ag) * av
        ay = jnp.einsum('tgj,goj->tgo', ah, a_down)
        out = out + jnp.einsum('tg,tgo->to', gw, ay)
        return out.reshape(B, N, C)

    def _L2_attn_ref(x, Wq, Wk, Wv, Wo, bo):
        import jax, jax.numpy as jnp
        import numpy as np
        HEADS = 16
        DIM_HEAD = 64
        B, T, C = (4, 256, 128)

        def apply_rope(x):
            d = x.shape[-1]
            seq_len = x.shape[1]
            inv_freq = 1.0 / 10000.0 ** (jnp.arange(0, d, 2, dtype=jnp.float32) / d)
            pos = jnp.arange(seq_len, dtype=jnp.float32)
            ang = pos[:, None] * inv_freq[None, :]
            sin = jnp.sin(ang)[None]
            cos = jnp.cos(ang)[None]
            x1, x2 = (x[..., 0::2], x[..., 1::2])
            rot = jnp.stack([x1 * cos - x2 * sin, x1 * sin + x2 * cos], axis=-1)
            return rot.reshape(x.shape)
        b, t, c = x.shape
        h, d = (HEADS, DIM_HEAD)
        scale = d ** (-0.5)

        def split_heads(z):
            return z.reshape(b, t, h, d).transpose(0, 2, 1, 3).reshape(b * h, t, d)
        q = split_heads(x @ Wq)
        k = split_heads(x @ Wk)
        v = split_heads(x @ Wv)
        q = apply_rope(q)
        k = apply_rope(k)
        sim = jnp.einsum('bid,bjd->bij', q, k) * scale
        causal = jnp.tril(jnp.ones((t, t), dtype=bool))
        sim = jnp.where(causal[None], sim, -jnp.inf)
        attn = jax.nn.softmax(sim, axis=-1)
        out = jnp.einsum('bij,bjd->bid', attn, v)
        out = out.reshape(b, h, t, d).transpose(0, 2, 1, 3).reshape(b, t, h * d)
        return out @ Wo + bo

    def _L2_ffn_ref(x, W_r, W_k, W_v, mu_r, mu_k):
        import jax, jax.numpy as jnp
        import numpy as np
        DIM = 128

        def _reference_tuple_inner(x, W_r, W_k, W_v, mu_r, mu_k):
            B, T, C = x.shape
            x_prev = jnp.concatenate([jnp.zeros((B, 1, C), x.dtype), x[:, :-1, :]], axis=1)
            xr = mu_r * x + (1.0 - mu_r) * x_prev
            xk = mu_k * x + (1.0 - mu_k) * x_prev
            r = jax.nn.sigmoid(jnp.einsum('btc,dc->btd', xr, W_r))
            k = jnp.einsum('btc,dc->btd', xk, W_k)
            k_act = jnp.square(jax.nn.relu(k))
            out = r * jnp.einsum('btc,dc->btd', k_act, W_v)
            new_state = x[:, -1, :]
            return (out, new_state)
        return _reference_tuple_inner(x, W_r, W_k, W_v, mu_r, mu_k)[0]

    def _L3_attn_ref(x, wq, wk, wv, wo, q_norm_w, k_norm_w):
        import math
        import jax, jax.numpy as jnp
        import numpy as np
        N_HEADS = 16
        N_KV_HEADS = 4
        HEAD_DIM = 64
        DIM = 128
        WINDOW = 16
        EPS = 0.01

        def _alibi_slopes(n_heads):
            closest = 2 ** math.floor(math.log2(n_heads))
            base = 2.0 ** (-2.0 ** (-(math.log2(closest) - 3)))
            slopes = base ** np.arange(1, closest + 1, dtype=np.float32)
            if closest < n_heads:
                eb = 2.0 ** (-2.0 ** (-(math.log2(2 * closest) - 3)))
                extra = eb ** np.arange(1, 2 * (n_heads - closest) + 1, 2, dtype=np.float32)
                slopes = np.concatenate([slopes, extra])
            return jnp.asarray(slopes[:n_heads])

        def _rmsnorm(x, w):
            xf = x.astype(jnp.float32)
            norm = jax.lax.rsqrt(jnp.mean(xf * xf, axis=-1, keepdims=True) + EPS)
            return (xf * norm).astype(x.dtype) * w
        B, L, _ = x.shape
        n_rep = N_HEADS // N_KV_HEADS
        q = (x @ wq.T).reshape(B, L, N_HEADS, HEAD_DIM)
        k = (x @ wk.T).reshape(B, L, N_KV_HEADS, HEAD_DIM)
        v = (x @ wv.T).reshape(B, L, N_KV_HEADS, HEAD_DIM)
        q = _rmsnorm(q, q_norm_w)
        k = _rmsnorm(k, k_norm_w)
        k = jnp.broadcast_to(k[:, :, None], (B, L, n_rep, N_KV_HEADS, HEAD_DIM)).reshape(B, L, N_HEADS, HEAD_DIM)
        v = jnp.broadcast_to(v[:, :, None], (B, L, n_rep, N_KV_HEADS, HEAD_DIM)).reshape(B, L, N_HEADS, HEAD_DIM)
        pos = jnp.arange(L)
        rel = pos[None, :] - pos[:, None]
        slopes = _alibi_slopes(N_HEADS)
        bias = slopes[:, None, None] * rel[None].astype(jnp.float32)
        masked = (rel > 0) | (rel < -WINDOW)
        bias = jnp.where(masked[None], -jnp.inf, bias)
        scale = 1.0 / math.sqrt(HEAD_DIM)
        attn = jnp.einsum('bqhd,bkhd->bhqk', q, k) * scale + bias[None]
        attn = jax.nn.softmax(attn, axis=-1)
        out = jnp.einsum('bhqk,bkhd->bqhd', attn, v).reshape(B, L, N_HEADS * HEAD_DIM)
        return out @ wo.T

    def _L3_ffn_ref(x, wqkv, q_scale, k_scale, wo, ln_g, ln_b, w1, b1, w2, b2):
        import jax, jax.numpy as jnp
        import numpy as np
        DIM = 128
        DEPTH = 2
        HEADS = 8
        DIM_HEAD = 64
        WINDOW = 64
        INNER = HEADS * DIM_HEAD
        HID = int(DIM * 4 * 2 / 3)
        B, N = (2, 1024)
        QK_SCALE = 8.0

        def shift_token(t):
            t1, t2 = jnp.split(t, 2, axis=-1)
            t2 = jnp.pad(t2, ((0, 0), (1, 0), (0, 0)))[:, :-1]
            return jnp.concatenate([t1, t2], axis=-1)

        def l2norm(t):
            return t / jnp.clip(jnp.linalg.norm(t, axis=-1, keepdims=True), 1e-12)

        def rotate_half(x):
            x1, x2 = jnp.split(x, 2, axis=-1)
            return jnp.concatenate([-x2, x1], axis=-1)

        def rotary_xpos(q, k):
            n = q.shape[-2]
            half_idx = jnp.arange(0, DIM_HEAD, 2, dtype=jnp.float32)
            inv_freq = 1.0 / 10000.0 ** (half_idx / DIM_HEAD)
            t = jnp.arange(n, dtype=jnp.float32)
            freqs = t[:, None] * inv_freq[None, :]
            freqs = jnp.concatenate([freqs, freqs], axis=-1)
            base = (half_idx + 0.4 * DIM_HEAD) / (1.4 * DIM_HEAD)
            power = (t - n // 2) / float(WINDOW // 2)
            scale = base[None, :] ** power[:, None]
            scale = jnp.concatenate([scale, scale], axis=-1)
            cos, sin = (jnp.cos(freqs), jnp.sin(freqs))
            q = q * cos * scale + rotate_half(q) * sin * scale
            k = k * cos / scale + rotate_half(k) * sin / scale
            return (q, k)

        def local_attention(q, k, v):
            b, h, n, d = q.shape
            w = n // WINDOW
            bq = q.reshape(b, h, w, WINDOW, d) * QK_SCALE
            bk = k.reshape(b, h, w, WINDOW, d)
            bv = v.reshape(b, h, w, WINDOW, d)

            def look_around(t):
                p = jnp.pad(t, ((0, 0), (0, 0), (1, 0), (0, 0), (0, 0)))
                return jnp.concatenate([p[:, :, :w], p[:, :, 1:]], axis=3)
            bk, bv = (look_around(bk), look_around(bv))
            bt = jnp.arange(n).reshape(w, WINDOW)
            btp = jnp.pad(bt, ((1, 0), (0, 0)), constant_values=-1)
            btk = jnp.concatenate([btp[:w], btp[1:]], axis=1)
            sim = jnp.einsum('bhwid,bhwjd->bhwij', bq, bk)
            i = bt[:, :, None]
            j = btk[:, None, :]
            mask = (i < j) | (i > j + WINDOW) | (j == -1)
            sim = jnp.where(mask, -jnp.finfo(sim.dtype).max, sim)
            attn = jax.nn.softmax(sim, axis=-1)
            out = jnp.einsum('bhwij,bhwjd->bhwid', attn, bv)
            return out.reshape(b, h, n, d)

        def _layer(x, wqkv, qs, ksc, wo, lg, lb, w1, b1, w2, b2):
            b, n, _ = x.shape
            h = shift_token(x)
            qkv = h @ wqkv
            q, k, v = jnp.split(qkv, 3, axis=-1)
            to_heads = lambda t: t.reshape(b, n, HEADS, DIM_HEAD).transpose(0, 2, 1, 3)
            q, k, v = (to_heads(q), to_heads(k), to_heads(v))
            q = l2norm(q) * qs
            k = l2norm(k) * ksc
            q, k = rotary_xpos(q, k)
            o = local_attention(q, k, v)
            o = o.transpose(0, 2, 1, 3).reshape(b, n, INNER)
            x = x + o @ wo
            h = shift_token(x)
            mu = h.mean(-1, keepdims=True)
            var = h.var(-1, keepdims=True)
            h = (h - mu) / jnp.sqrt(var + 1e-05) * lg + lb
            h = h @ w1 + b1
            a, g = jnp.split(h, 2, axis=-1)
            h = a * jax.nn.gelu(g, approximate=False)
            x = x + h @ w2 + b2
            return x
        for l in range(DEPTH):
            x = _layer(x, wqkv[l], q_scale[l], k_scale[l], wo[l], ln_g[l], ln_b[l], w1[l], b1[l], w2[l], b2[l])
        return x
    x = L0_attn_x
    mod = (_silu(L0_c) @ L0_wmod).reshape(L0_c.shape[0], 6, 1, -1)
    sa, ca, ga, sb, cb, gb = (mod[:, 0], mod[:, 1], mod[:, 2], mod[:, 3], mod[:, 4], mod[:, 5])
    ga = (2 * (ga >= 0) - 1) * jnp.maximum(jnp.abs(ga), 0.25)
    gb = (2 * (gb >= 0) - 1) * jnp.maximum(jnp.abs(gb), 0.25)
    h = _layernorm(x, axis=-1) * (1 + ca) + sa
    x = x + ga * _L0_attn_ref(h, L0_attn_W, L0_attn_b)
    h = _layernorm(x, axis=-1) * (1 + cb) + sb
    x = x + gb * _L0_ffn_ref(h, L0_ffn_U1, L0_ffn_V1, L0_ffn_b1, L0_ffn_U2, L0_ffn_V2, L0_ffn_b2)
    mod = (_silu(L1_c) @ L1_wmod).reshape(L1_c.shape[0], 6, 1, -1)
    sa, ca, ga, sb, cb, gb = (mod[:, 0], mod[:, 1], mod[:, 2], mod[:, 3], mod[:, 4], mod[:, 5])
    ga = (2 * (ga >= 0) - 1) * jnp.maximum(jnp.abs(ga), 0.25)
    gb = (2 * (gb >= 0) - 1) * jnp.maximum(jnp.abs(gb), 0.25)
    h = _layernorm(x, axis=-1) * (1 + ca) + sa
    x = x + ga * _L1_attn_ref(h, L1_attn_Wa, L1_attn_ba, L1_attn_Wb, L1_attn_bb, L1_attn_Wc, L1_attn_bc)
    h = _layernorm(x, axis=-1) * (1 + cb) + sb
    x = x + gb * _L1_ffn_ref(h, L1_ffn_r1_w, L1_ffn_r1_b, L1_ffn_r2_w, L1_ffn_w_up, L1_ffn_w_down, L1_ffn_a_up, L1_ffn_a_down)
    mod = (_silu(L2_c) @ L2_wmod).reshape(L2_c.shape[0], 6, 1, -1)
    sa, ca, ga, sb, cb, gb = (mod[:, 0], mod[:, 1], mod[:, 2], mod[:, 3], mod[:, 4], mod[:, 5])
    ga = (2 * (ga >= 0) - 1) * jnp.maximum(jnp.abs(ga), 0.25)
    gb = (2 * (gb >= 0) - 1) * jnp.maximum(jnp.abs(gb), 0.25)
    h = _layernorm(x, axis=-1) * (1 + ca) + sa
    x = x + ga * _L2_attn_ref(h, L2_attn_Wq, L2_attn_Wk, L2_attn_Wv, L2_attn_Wo, L2_attn_bo)
    h = _layernorm(x, axis=-1) * (1 + cb) + sb
    x = x + gb * _L2_ffn_ref(h, L2_ffn_W_r, L2_ffn_W_k, L2_ffn_W_v, L2_ffn_mu_r, L2_ffn_mu_k)
    mod = (_silu(L3_c) @ L3_wmod).reshape(L3_c.shape[0], 6, 1, -1)
    sa, ca, ga, sb, cb, gb = (mod[:, 0], mod[:, 1], mod[:, 2], mod[:, 3], mod[:, 4], mod[:, 5])
    ga = (2 * (ga >= 0) - 1) * jnp.maximum(jnp.abs(ga), 0.25)
    gb = (2 * (gb >= 0) - 1) * jnp.maximum(jnp.abs(gb), 0.25)
    h = _layernorm(x, axis=-1) * (1 + ca) + sa
    x = x + ga * _L3_attn_ref(h, L3_attn_wq, L3_attn_wk, L3_attn_wv, L3_attn_wo, L3_attn_q_norm_w, L3_attn_k_norm_w)
    h = _layernorm(x, axis=-1) * (1 + cb) + sb
    x = x + gb * _L3_ffn_ref(h, L3_ffn_wqkv, L3_ffn_q_scale, L3_ffn_k_scale, L3_ffn_wo, L3_ffn_ln_g, L3_ffn_ln_b, L3_ffn_w1, L3_ffn_b1, L3_ffn_w2, L3_ffn_b2)
    return x

_drawn_inputs = setup_inputs


def setup_inputs(seed=0):
    import zlib

    import numpy as np

    out = dict(_drawn_inputs(seed))
    spreads = {'L0_ffn_b1': (0.0, 0.8),
     'L0_ffn_b2': (0.0, 0.1),
     'L1_attn_ba': (0.0, 0.8),
     'L1_attn_bb': (0.0, 0.789),
     'L1_attn_bc': (0.0, 0.8),
     'L1_ffn_r1_b': (0.0, 0.8),
     'L2_attn_bo': (0.0, 0.353),
     'L3_attn_q_norm_w': (1.0, 0.6),
     'L3_attn_k_norm_w': (1.0, 0.6),
     'L3_ffn_q_scale': (1.0, 0.6),
     'L3_ffn_k_scale': (1.0, 0.6),
     'L3_ffn_ln_g': (1.0, 0.6),
     'L3_ffn_ln_b': (0.0, 0.8),
     'L3_ffn_b1': (0.0, 0.8),
     'L3_ffn_b2': (0.0, 0.8)}
    factors = {'L0_attn_W': 4.673,
     'L0_attn_b': 8.0,
     'L0_ffn_U1': 8.0,
     'L0_ffn_V1': 8.0,
     'L0_ffn_U2': 8.0,
     'L0_ffn_V2': 8.0,
     'L1_ffn_r1_w': 8.0,
     'L1_ffn_r2_w': 8.0,
     'L1_ffn_w_up': 8.0,
     'L1_ffn_w_down': 8.0,
     'L1_ffn_a_up': 8.0,
     'L1_ffn_a_down': 8.0,
     'L2_attn_Wq': 8.0,
     'L2_attn_Wk': 8.0,
     'L2_attn_Wv': 8.0,
     'L2_attn_Wo': 8.0,
     'L2_ffn_W_r': 8.0,
     'L2_ffn_W_k': 2.815,
     'L2_ffn_mu_r': 8.0,
     'L2_ffn_mu_k': 4.466,
     'L3_ffn_wqkv': 7.271,
     'L3_ffn_wo': 7.297,
     'L3_ffn_w1': 8.0,
     'L3_ffn_w2': 8.0}
    for name, (base, spread) in spreads.items():
        noise = np.random.default_rng([zlib.crc32(name.encode()), seed]).standard_normal(out[name].shape)
        drawn = base * np.exp(spread * noise) if base else spread * noise
        out[name] = jnp.asarray(drawn.astype(out[name].dtype))
    for name, factor in factors.items():
        out[name] = (out[name] * factor).astype(out[name].dtype)
    return out
```

```python
from contextlib import ExitStack

import numpy as np

import concourse.bass as bass
from concourse import mybir

F32 = mybir.dt.float32
U32 = mybir.dt.uint32
ALU = mybir.AluOpType
ACT = mybir.ActivationFunctionType
AX_X = mybir.AxisListType.X

C = 128
B = 4
T = 512
N = B * T
PAD = 64
TP = PAD + T
TILES = N // 128
TB = T // 128
EPS = 1e-5
LN2 = 0.6931471805599453

K = 32
R = 32
FB = 4
E = 32
CAP = int(1.25 * N / E)
G = 16
SLOTS = E * CAP
DUMP = SLOTS
ROUNDS = CAP // 8
WG = 2 * 512 + 2 * 256 + 256 + 128
NB128 = SLOTS // 128

NBLK = T // 64
PAIRS = 8
GROUPS = [[7], [6, 0], [5, 1], [4, 2], [3]]
GCUM = [1, 3, 5, 7, 8]
PCH = [j // 2 + 1 for j in range(NBLK)]
POFF = [128 * sum(PCH[:j]) for j in range(NBLK)]
PW = 128 * sum(PCH)
CHUNKS = [(jc, j) for jc in range(TB) for j in range(NBLK) if j // 2 >= jc]
NFILL = len(CHUNKS) // 4

HID = int(C * 4 * 2 / 3)

VEC = {}
for _name, _n in (("ffn0_b1", 4), ("ffn0_b2", 1), ("scan_ba", 1), ("scan_bb", 1), ("scan_bc", 1),
                  ("r1_b", 1), ("attn2_bo", 1), ("mu_r", 1), ("mu_k", 1), ("qn_w", 1), ("kn_w", 1),
                  ("q_scale", 2), ("k_scale", 2), ("q_scale_rot", 2), ("k_scale_rot", 2),
                  ("ln_g", 2), ("ln_b", 2), ("b2", 2), ("b1a", 6), ("b1g", 6), ("slope", 8)):
    VEC[_name] = (sum(n for _, n in VEC.values()), _n)
NVEC = sum(n for _, n in VEC.values())


def adaln_blocks(nc, d, out):
    ctx = ExitStack()
    with ctx:
        def sb(name, shape, dt=F32):
            return ctx.enter_context(nc.sbuf_tensor(name, shape, dt))

        scope = [ExitStack()]

        def tmp_sb(name, shape, dt=F32):
            return scope[0].enter_context(nc.sbuf_tensor(name, shape, dt))

        def next_block():
            scope[0].close()
            scope[0] = ExitStack()

        sems = {}

        def sem(name):
            if name not in sems:
                sems[name] = ctx.enter_context(nc.semaphore(name))
            return sems[name]

        bank = [ctx.enter_context(nc.psum_tensor(f"bank{i}", [128, 512], F32)) for i in range(8)]

        x = sb("x", [C, B, T])
        h = sb("h", [C, B, TP])
        ident = sb("ident", [128, 128])
        centre = sb("centre", [128, 128])
        mean = sb("mean", [128, 128])
        vec = sb("vec", [128, NVEC])
        cond = sb("cond", [C, 16])
        cond_silu = sb("cond_silu", [C, 16])
        mod = sb("mod", [C, 4, 6, B])
        
        gate_sign = sb("gate_sign", [C, 4, 2, B])
        gate_abs = sb("gate_abs", [C, 4, 2, B])
        eps_col = sb("eps_col", [128, 1])
        rms_eps = sb("rms_eps", [128, 1])
        ln_clip = sb("ln_clip", [128, 1])
        head_sum = sb("head_sum", [128, 128])
        ln_square = sb("ln_square", [C, 2, T])
        ln_log = sb("ln_log", [C, 2, T])
        ln_rstd = sb("ln_rstd", [C, 2, T])
        ln_norm = sb("ln_norm", [C, 2, T])

        lr_u1 = sb("lr_u1", [C, R])
        lr_v1 = sb("lr_v1", [R, FB * 128])
        lr_u2 = sb("lr_u2", [128, FB, R])
        lr_v2 = sb("lr_v2", [R, C])
        scan_w = sb("scan_w", [C, 3, C])
        moe_w = [sb(f"moe_w{u}", [128, WG]) for u in range(2)]
        r1_c = sb("r1_c", [C, 64])
        r1_s = sb("r1_s", [6, 64])
        r2_w = sb("r2_w", [64, E])
        iota_e = sb("iota_e", [128, E])
        chunk_sum = sb("chunk_sum", [128, 128])
        zeros = sb("zeros", [128, 4 * C])
        htok = sb("htok", [128, TILES, C])

        ctx.callback(lambda: scope[0].close())

        def v(name, i=0):
            at, n = VEC[name]
            assert i < n
            return vec[:, at + i:at + i + 1]

        def gate(k, b):
            return mod[:, k // 2, 3 * (k % 2) + 2, b:b + 1]

        def scale1(k, b):
            return mod[:, k // 2, 3 * (k % 2) + 1, b:b + 1]

        def shift(k, b):
            return mod[:, k // 2, 3 * (k % 2), b:b + 1]

        def hb(b):
            return h[:, b, PAD:TP]

        def hh(b, lo, n):
            return h[:, b, PAD + lo:PAD + lo + n]

        steps = {"dve": 0, "act": 0, "pool": 0}

        def link(eng, name, ins):
            steps[name] += 1
            ins.then_inc(sem(name + "_step"), 1)
            eng.wait_ge(sem(name + "_step"), steps[name])

        LAST = 4 * 5
        block = ctx.enter_context(nc.Block())

        def x_written(k):
            if k == 4:
                return "pair_added", B * PAIRS
            if k == 6:
                return "pair_added", 2 * B * PAIRS
            return "x_ready", 4 * (k if k < 4 else k - 1)

        def ln_pe(pe, k, after_all=False):
            def centred(b):
                n = 4 * k + b
                src = x[:, b, :]
                if k == 0:
                    pe.wait_ge(sem(f"x_loaded{b}"), 16)
                else:
                    name, base = ("shifted", 8 * (k - 8) + 4) if k >= 8 else x_written(k - 1)
                    pe.wait_ge(sem(name), base + (B if after_all else b + 1))
                if k >= 8:
                    src = shifted[:, b, PAD:TP]
                if n >= 2:
                    pe.wait_ge(sem("ln_normed"), n - 1)
                pe.matmul(bank[n % 2][:, :], centre[:, :], src, start=True, stop=True) \
                  .then_inc(sem("ln_centred"), 1)

            def variance(b):
                n = 4 * k + b
                pe.wait_ge(sem("ln_squared"), n + 1)
                pe.matmul(bank[2 + n % 2][:, :], mean[:, :], ln_square[:, n % 2, :], start=True, stop=True) \
                  .then_inc(sem("ln_variance"), 1)

            centred(0)
            for b in range(B):
                if b + 1 < B:
                    centred(b + 1)
                variance(b)

        def ln_act(act, k):
            nc.scalar.preload_act_table_set("natural_log_exp_and_others")
            for b in range(B):
                n = 4 * k + b
                act.wait_ge(sem("ln_centred"), n + 1)
                if n >= 2:
                    act.wait_ge(sem("ln_variance"), n - 1)
                nc.scalar.activation(ln_square[:, n % 2, :], bank[n % 2][:, :], ACT.Square) \
                  .then_inc(sem("ln_squared"), 1)
                act.wait_ge(sem("ln_variance"), n + 1)
                if n == 0:
                    act.wait_ge(sem("filled"), 1)
                nc.scalar.activation(ln_log[:, n % 2, :], bank[2 + n % 2][:, :], ACT.Ln,
                                     bias=eps_col[:, 0:1]).then_inc(sem("ln_log"), 1)
                act.wait_ge(sem("ln_log"), n + 1)
                if n >= 2:
                    act.wait_ge(sem("ln_normed"), n - 1)
                nc.scalar.activation(ln_rstd[:, n % 2, :], ln_log[:, n % 2, :], ACT.Exp, scale=-0.5) \
                  .then_inc(sem("ln_rstd"), 1)

        def ln_dve(dve, k):
            for b in range(B):
                n = 4 * k + b
                dve.wait_ge(sem("ln_rstd"), n + 1)
                if n >= 2:
                    dve.wait_ge(sem("h_ready"), n - 1)
                nc.vector.tensor_tensor(ln_norm[:, n % 2, :], bank[n % 2][:, :], ln_rstd[:, n % 2, :],
                                        ALU.mult).then_inc(sem("ln_normed"), 1)

        def ln_pool(pool, k):
            for b in range(B):
                n = 4 * k + b
                if k == 0 and b == 0:
                    pool.wait_ge(sem("mod_ready"), 4)
                pool.wait_ge(sem("ln_normed"), n + 1)
                dst = conv_h[:, T * b:T * b + T] if k == 0 else hb(b)
                scale, bias = (scale1(k, b), shift(k, b)) if k < 8 else (v("ln_g", k - 8), v("ln_b", k - 8))
                if k >= 8:
                    dst = mlp_in[b]
                nc.gpsimd.tensor_scalar(dst, ln_norm[:, n % 2, :], scale, bias,
                                        ALU.mult, ALU.add).then_inc(sem("h_ready"), 1)

        def mod_act(act):
            act.wait_ge(sem("cond_loaded"), 16)
            nc.scalar.activation(cond_silu[:, :], cond[:, :], ACT.Silu).then_inc(sem("cond_ready"), 1)

        def mod_pe(pe):
            pe.wait_ge(sem("cond_ready"), 1)
            pe.wait_ge(sem("wmod_loaded"), 16)
            for l in range(4):
                for j in range(6):
                    at = (6 * l + j) * B
                    last = pe.matmul(bank[7][:, at:at + B], wmod[:, l, j * C:(j + 1) * C],
                                     cond_silu[:, B * l:B * l + B], start=True, stop=True)
            last.then_inc(sem("mod_raw"), 1)

        def mod_dve(dve):
            dve.wait_ge(sem("mod_raw"), 1)
            raw = bank[7][:, 0:96].rearrange("p (l j b) -> p l j b", l=4, j=6)
            for i in range(2):
                s, c, g = (mod[:, :, 3 * i + j, :] for j in range(3))
                nc.vector.tensor_copy(s, raw[:, :, 3 * i, :]).then_inc(sem("mod_ready"), 1)
                nc.vector.tensor_scalar(c, raw[:, :, 3 * i + 1, :], 1.0, None, ALU.add) \
                  .then_inc(sem("mod_ready"), 1)
                r = raw[:, :, 3 * i + 2, :]
                link(dve, "dve", nc.vector.tensor_scalar(gate_sign[:, :, i, :], r, 0.0, 2.0, ALU.is_ge, ALU.mult))
                link(dve, "dve", nc.vector.tensor_scalar(gate_abs[:, :, i, :], r, -1.0, None, ALU.mult))
                link(dve, "dve", nc.vector.tensor_tensor(gate_abs[:, :, i, :], gate_abs[:, :, i, :], r, ALU.max))
                link(dve, "dve", nc.vector.tensor_scalar(gate_abs[:, :, i, :], gate_abs[:, :, i, :], 0.25, None,
                                                         ALU.max))
                link(dve, "dve", nc.vector.scalar_tensor_tensor(g, gate_sign[:, :, i, :], -1.0,
                                                                gate_abs[:, :, i, :], ALU.add, ALU.mult))

        wmod = tmp_sb("wmod", [C, 4, 6 * C])
        conv_h = tmp_sb("conv_h", [C, N])
        conv_w = tmp_sb("conv_w", [C, 2 * K])
        conv_bias = tmp_sb("conv_bias", [128, 16, K])
        conv_mask = tmp_sb("conv_mask", [128, TB, K])
        conv_edge = tmp_sb("conv_edge", [K, K])
        logit = tmp_sb("logit", [128, 16, K])
        row_max = tmp_sb("row_max", [128, 16])
        row_sum = tmp_sb("row_sum", [128, 16])
        row_inv = tmp_sb("row_inv", [128, 16])
        prob4 = tmp_sb("prob4", [128, 16, 4, K])
        band = tmp_sb("band", [128, TILES, 128])
        edge = tmp_sb("edge", [K, TILES, K])

        def htok_pe(pe, banks, tokens):
            for b in range(B):
                for i in range(TB):
                    last = pe.transpose(banks[b][:, 128 * i:128 * i + 128], tokens(b, i), ident[:, :])
                last.then_inc(sem("htok_raw"), 1)

        def conv_pe(pe):
            pe.wait_ge(sem("h_ready"), 4)
            for r in range(K):
                half = 64 * (r % 2)
                last = pe.matmul(bank[4][half:half + 64, K * (r // 2):K * (r // 2) + K],
                                 conv_h[:, r:N:K], conv_w[:, K - r:2 * K - r], start=True, stop=True)
            last.then_inc(sem("conv_logits"), 1)
            pe.wait_ge(sem("ln_normed"), 4)
            htok_pe(pe, bank[0:4], lambda b, i: conv_h[:, T * b + 128 * i:T * b + 128 * i + 128])
            pe.wait_ge(sem("conv_prob"), 1)
            for g in range(4):
                for i in range(4):
                    last = pe.transpose(bank[4 + g][:, 128 * i:128 * i + 128],
                                        prob4[:, 4 * g + i, :, :].rearrange("p a b -> p (a b)"), ident[:, :])
                last.then_inc(sem("conv_probT"), 1)
            pe.wait_ge(sem("conv_band"), 8)
            for b in range(B):
                pe.wait_ge(sem("htok_ready"), b + 1)
                if b + 1 < B:
                    pe.wait_ge(sem("htok_ready"), b + 2)
                for i in range(TB):
                    t = TB * b + i
                    last = pe.matmul(bank[b][:, 128 * i:128 * i + 128], htok[:, t, :], band[:, t, :],
                                     start=True, stop=(i == TB - 1))
                    if i < TB - 1:
                        last = pe.matmul(bank[b][:, 128 * i + 96:128 * i + 128], htok[0:K, t + 1, :],
                                         edge[:, t, :], start=False, stop=True)
                last.then_inc(sem("pv_raw"), 1)

        def htok_act(act, base):
            for b in range(B):
                act.wait_ge(sem("htok_raw"), base + b + 1)
                nc.scalar.activation(htok[:, TB * b:TB * b + TB, :],
                                     bank[b][:, :].rearrange("p (i c) -> p i c", i=TB), ACT.Copy) \
                  .then_inc(sem("htok_ready"), 1)

        def conv_act(act):
            act.wait_ge(sem("conv_shifted"), 1)
            nc.scalar.activation(logit[:, :, :], logit[:, :, :], ACT.Exp).then_inc(sem("conv_exp"), 1)
            htok_act(act, 0)

        def conv_dve(dve):
            dve.wait_ge(sem("conv_logits"), 1)
            dve.wait_ge(sem("conv_tables"), 64)
            link(dve, "dve", nc.vector.tensor_tensor(
                logit[:, :, :], bank[4][:, :].rearrange("p (r j) -> p r j", j=K), conv_bias[:, :, :], ALU.add))
            link(dve, "dve", nc.vector.tensor_reduce(row_max[:, :], logit[:, :, :], AX_X, ALU.max))
            nc.vector.tensor_tensor(logit[:, :, :], logit[:, :, :],
                                    row_max[:, :].unsqueeze(2).to_broadcast([128, 16, K]), ALU.subtract) \
              .then_inc(sem("conv_shifted"), 1)
            dve.wait_ge(sem("conv_exp"), 1)
            link(dve, "dve", nc.vector.tensor_reduce(row_sum[:, :], logit[:, :, :], AX_X, ALU.add))
            link(dve, "dve", nc.vector.reciprocal(row_inv[:, :], row_sum[:, :]))
            for a in range(4):
                last = nc.vector.tensor_tensor(prob4[:, :, a, :], logit[:, :, :],
                                               row_inv[:, :].unsqueeze(2).to_broadcast([128, 16, K]), ALU.mult)
            last.then_inc(sem("conv_prob"), 1)
            bandv = band[:, :, :].rearrange("s t (q r) -> s t q r", r=K)
            for g in range(4):
                dve.wait_ge(sem("conv_probT"), g + 1)
                p = bank[4 + g][:, :].rearrange("s (r t q) -> s t q r", r=8, q=TB)
                m = conv_mask[:, :, 8 * g:8 * g + 8].unsqueeze(1).to_broadcast([128, TILES, TB, 8])
                nc.vector.tensor_tensor(bandv[:, :, :, 8 * g:8 * g + 8], p, m, ALU.mult) \
                  .then_inc(sem("conv_band"), 1)
                m = conv_edge[:, 8 * g:8 * g + 8].unsqueeze(1).to_broadcast([K, TILES, 8])
                nc.vector.tensor_tensor(edge[:, :, 8 * g:8 * g + 8], p[0:K, :, TB - 1, :], m, ALU.mult) \
                  .then_inc(sem("conv_band"), 1)
            for b in range(B):
                dve.wait_ge(sem("pv_raw"), b + 1)
                nc.vector.scalar_tensor_tensor(x[:, b, :], bank[b][:, :], gate(0, b), x[:, b, :],
                                               ALU.mult, ALU.add).then_inc(sem("x_ready"), 1)

        next_block()
        lr_p = tmp_sb("lr_p", [R, 2, T])
        lr_h = tmp_sb("lr_h", [128, 2, FB, T])
        lr_q = tmp_sb("lr_q", [R, 2, T])
        tmp = tmp_sb("tmp", [C, 2, T])

        def lr_pe(pe):
            def up(b):
                pe.wait_ge(sem("h_ready"), 4 + b + 1)
                if b:
                    pe.wait_ge(sem("lr_out_read"), b - 1) if b > 1 else None
                    pe.wait_ge(sem("lr_p_ready"), b)
                else:
                    pe.wait_ge(sem("early_loaded"), 80)
                pe.matmul(bank[4][0:R, :], lr_u1[:, :], hb(b), start=True, stop=True) \
                  .then_inc(sem("lr_p_raw"), 1)
                pe.wait_ge(sem("lr_p_ready"), b + 1)
                for f in range(FB):
                    n = FB * b + f
                    if n >= 2:
                        pe.wait_ge(sem("up_acted"), n - 1)
                    pe.matmul(bank[5 + n % 2][:, :], lr_v1[:, 128 * f:128 * f + 128], lr_p[:, b % 2, :],
                              start=True, stop=True).then_inc(sem("up_raw"), 1)

            def down(b):
                pe.wait_ge(sem("up_acted"), FB * b + FB)
                if b:
                    pe.wait_ge(sem("lr_out_read"), b)
                for f in range(FB):
                    last = pe.matmul(bank[7][0:R, :], lr_u2[:, f, :], lr_h[:, b % 2, f, :],
                                     start=(f == 0), stop=(f == FB - 1))
                last.then_inc(sem("lr_q_raw"), 1)
                pe.wait_ge(sem("lr_q_ready"), b + 1)
                pe.matmul(bank[7][:, :], lr_v2[:, :], lr_q[:, b % 2, :], start=True, stop=True) \
                  .then_inc(sem("lr_out"), 1)

            up(0)
            for b in range(B):
                if b + 1 < B:
                    up(b + 1)
                down(b)

        def lr_act(act):
            for b in range(B):
                for f in range(FB):
                    n = FB * b + f
                    act.wait_ge(sem("up_raw"), n + 1)
                    if b >= 2 and f == 0:
                        act.wait_ge(sem("lr_q_raw"), b - 1)
                    nc.scalar.activation(lr_h[:, b % 2, f, :], bank[5 + n % 2][:, :], ACT.Gelu_apprx_tanh,
                                         bias=v("ffn0_b1", f)).then_inc(sem("up_acted"), 1)

        def lr_dve(dve):
            def p(b):
                dve.wait_ge(sem("lr_p_raw"), b + 1)
                if b >= 2:
                    dve.wait_ge(sem("up_raw"), FB * (b - 1))
                nc.vector.tensor_copy(lr_p[:, b % 2, :], bank[4][0:R, :]).then_inc(sem("lr_p_ready"), 1)

            p(0)
            for b in range(B):
                if b + 1 < B:
                    p(b + 1)
                dve.wait_ge(sem("lr_q_raw"), b + 1)
                if b >= 2:
                    dve.wait_ge(sem("lr_out"), b - 1)
                nc.vector.tensor_copy(lr_q[:, b % 2, :], bank[7][0:R, :]).then_inc(sem("lr_q_ready"), 1)
                dve.wait_ge(sem("lr_out"), b + 1)
                if b >= 2:
                    dve.wait_ge(sem("x_ready"), 4 + b - 1)
                nc.vector.tensor_scalar(tmp[:, b % 2, :], bank[7][:, :], v("ffn0_b2"), gate(1, b),
                                        ALU.add, ALU.mult).then_inc(sem("lr_out_read"), 1)
                dve.wait_ge(sem("lr_out_read"), b + 1)
                nc.vector.tensor_tensor(x[:, b, :], x[:, b, :], tmp[:, b % 2, :], ALU.add) \
                  .then_inc(sem("x_ready"), 1)

        next_block()
        scan_a = tmp_sb("scan_a", [C, 2, T])
        scan_b = tmp_sb("scan_b", [C, 2, T])
        scan_c = tmp_sb("scan_c", [C, 2, T])
        scan_1a = tmp_sb("scan_1a", [C, 2, T])

        def scan_banks(b):
            return (bank[4], bank[5], bank[6]) if b % 2 == 0 else (bank[7], bank[0], bank[1])

        def scan_pe(pe):
            pe.wait_ge(sem("ln_normed"), 12)
            for b in range(B):
                pe.wait_ge(sem("h_ready"), 8 + b + 1)
                if b >= 2:
                    pe.wait_ge(sem("scan_gates"), 3 * (b - 1))
                for i in range(3):
                    pe.matmul(scan_banks(b)[i][:, :], scan_w[:, i, :], hb(b), start=True, stop=True) \
                      .then_inc(sem("scan_raw"), 1)

        def scan_act(act):
            for b in range(B):
                if b >= 2:
                    act.wait_ge(sem("x_ready"), 8 + b - 1)
                for i, (dst, f, bias) in enumerate(((scan_a, ACT.Sigmoid, "scan_ba"), (scan_b, ACT.Tanh, "scan_bb"),
                                                    (scan_c, ACT.Sigmoid, "scan_bc"))):
                    act.wait_ge(sem("scan_raw"), 3 * b + i + 1)
                    nc.scalar.activation(dst[:, b % 2, :], scan_banks(b)[i][:, :], f, bias=v(bias)) \
                      .then_inc(sem("scan_gates"), 1)

        def scan_pool(pool):
            for b in range(B):
                pool.wait_ge(sem("scan_gates"), 3 * b + 1)
                if b >= 2:
                    pool.wait_ge(sem("scan_in"), b - 1)
                nc.gpsimd.tensor_scalar(scan_1a[:, b % 2, :], scan_a[:, b % 2, :], -1.0, 1.0,
                                        ALU.mult, ALU.add).then_inc(sem("scan_1a_ready"), 1)

        def scan_dve(dve):
            for b in range(B):
                i = b % 2
                dve.wait_ge(sem("scan_gates"), 3 * b + 3)
                dve.wait_ge(sem("scan_1a_ready"), b + 1)
                nc.vector.tensor_tensor(scan_b[:, i, :], scan_1a[:, i, :], scan_b[:, i, :], ALU.mult) \
                  .then_inc(sem("scan_in"), 1)
                dve.wait_ge(sem("scan_in"), b + 1)
                link(dve, "dve", nc.vector.tensor_tensor_scan(scan_1a[:, i, :], scan_a[:, i, :], scan_b[:, i, :],
                                                              0.0, ALU.mult, ALU.add))
                link(dve, "dve", nc.vector.tensor_tensor(scan_c[:, i, :], scan_c[:, i, :], scan_1a[:, i, :], ALU.mult))
                nc.vector.scalar_tensor_tensor(x[:, b, :], scan_c[:, i, :], gate(2, b), x[:, b, :],
                                               ALU.mult, ALU.add).then_inc(sem("x_ready"), 1)

        next_block()
        bn = tmp_sb("bn", [128, TILES, 6])
        mv = tmp_sb("mv", [128, TILES, 2])
        stat = tmp_sb("stat", [128, TILES, 6])
        small = tmp_sb("small", [128, TILES, C])
        statT = tmp_sb("statT", [6, B, T])
        r_hid = tmp_sb("r_hid", [64, B, T])
        prob = tmp_sb("prob", [128, TILES, E])
        r_max = tmp_sb("r_max", [128, TILES])
        r_sum = tmp_sb("r_sum", [128, TILES])
        r_inv = tmp_sb("r_inv", [128, TILES])
        top8 = tmp_sb("top8", [128, TILES, 8])
        top8_at = tmp_sb("top8_at", [128, TILES, 8], U32)
        pick = tmp_sb("pick", [128, 2, TILES])
        onehot = tmp_sb("onehot", [128, 2, TILES, E])
        hit = tmp_sb("hit", [128, TILES, E])
        score = tmp_sb("score", [128, 4, B, E])
        scoreT = tmp_sb("scoreT", [128, T])
        rest = [tmp_sb(f"rest{i}", [128, T]) for i in range(2)]
        best = tmp_sb("best", [128, CAP])
        cand = [tmp_sb(f"cand{i}", [E, B, CAP]) for i in range(2)]
        best_all = tmp_sb("best_all", [E, CAP])
        above_last = tmp_sb("above_last", [E, CAP])
        cut = tmp_sb("cut", [E, 2])
        cut4 = tmp_sb("cut4", [128, 2])
        ones = tmp_sb("ones", [128, T])
        is_gt = tmp_sb("is_gt", [128, T])
        is_eq = tmp_sb("is_eq", [128, T])
        cum_gt = tmp_sb("cum_gt", [128, T])
        cum_eq = tmp_sb("cum_eq", [128, T])
        totals = tmp_sb("totals", [128, 2])
        offset = tmp_sb("offset", [128, 2])
        looked = tmp_sb("looked", [128, 2, TILES, E])
        place = tmp_sb("place", [128, 2, TILES])
        valid = tmp_sb("valid", [128, 2, TILES])
        slot = tmp_sb("slot", [128, 2, TILES])
        slot_u = tmp_sb("slot_u", [128, 2, TILES], U32)
        weight = tmp_sb("weight", [128, 2, TILES])
        xg = tmp_sb("xg", [128, SLOTS // 128, C])
        xgT = tmp_sb("xgT", [C, SLOTS + 128 - CAP])
        moe_silu = [tmp_sb(f"moe_silu{u}", [128, 3, 2 * CAP]) for u in range(2)]
        moe_act = [tmp_sb(f"moe_act{u}", [128, 3, 2 * CAP]) for u in range(2)]
        y_slot = [tmp_sb(f"y_slot{u}", [CAP, 2, C]) for u in range(2)]

        def up(u, q, j):
            return bank[2 * u + q][:, :].rearrange("p (j c) -> p j c", c=128)[:, j:j + 2, 0:CAP]

        y_tok = tmp_sb("y_tok", [128, 2, TILES, C])
        y_sum = tmp_sb("y_sum", [128, TILES, C])
        xg_dram = nc.dram_tensor("xg_dram", (SLOTS, C), F32, kind="Internal").ap()
        y_dram = nc.dram_tensor("y_dram", (SLOTS + 1, C), F32, kind="Internal").ap()

        def moe_pe(pe):
            pe.wait_ge(sem("h_ready"), 16)
            pe.wait_ge(sem("ln_normed"), 16)
            pe.wait_ge(sem("x_ready"), 12)
            htok_pe(pe, bank[0:4], lambda b, i: hh(b, 128 * i, 128))
            pe.wait_ge(sem("moe_stats"), 1)
            for b in range(B):
                for i in range(TB):
                    last = pe.transpose(bank[4 + b][0:6, 128 * i:128 * i + 128], stat[:, TB * b + i, :], ident[:, :])
                last.then_inc(sem("moe_statT_raw"), 1)
            pe.wait_ge(sem("moe_loaded"), 80)
            for b in range(B):
                pe.wait_ge(sem("htok_ready"), B + b + 1)
                pe.matmul(bank[b][0:64, :], r1_c[:, :], hb(b), start=True, stop=False)
                pe.wait_ge(sem("moe_statT_ready"), b + 1)
                pe.matmul(bank[b][0:64, :], r1_s[:, :], statT[:, b, :], start=False, stop=True) \
                  .then_inc(sem("moe_hid_raw"), 1)
            for b in range(B):
                pe.wait_ge(sem("moe_hid_ready"), b + 1)
                for i in range(TB):
                    t = TB * b + i
                    last = pe.matmul(bank[4][:, E * t:E * t + E], r_hid[:, b, 128 * i:128 * i + 128], r2_w[:, :],
                                     start=True, stop=True)
            last.then_inc(sem("moe_logits"), 1)
            pe.wait_ge(sem("moe_scored"), 1)
            for g in range(4):
                last = pe.transpose(bank[5][:, 128 * g:128 * g + 128],
                                    score[:, g, :, :].rearrange("p j e -> p (j e)"), ident[:, :])
            last.then_inc(sem("moe_scoreT_raw"), 1)
            pe.wait_ge(sem("moe_totals"), 2)
            pe.matmul(bank[6][:, 0:2], chunk_sum[:, :], totals[:, :], start=True, stop=True) \
              .then_inc(sem("moe_offset_raw"), 1)
            pe.wait_ge(sem("moe_placed"), 1)
            for g in range(4):
                last = pe.transpose(bank[7][:, 128 * g:128 * g + 128], cum_gt[:, 128 * g:128 * g + 128], ident[:, :])
            last.then_inc(sem("moe_placeT"), 1)
            pe.wait_ge(sem("xg_loaded"), 16)
            for s in range(NB128 // 4):
                for i in range(4):
                    last = pe.transpose(bank[s][:, 128 * i:128 * i + 128], xg[:, 4 * s + i, :], ident[:, :])
                last.then_inc(sem("xgT_raw"), 1)
            pe.wait_ge(sem("xgT_ready"), NB128 // 4)

            with pe.Fori(0, G // 2) as i:
                for u in range(2):
                    w = moe_w[u]
                    pe.wait_ge(sem(f"moe_w_loaded{u}"), i * 16 + 16)
                    for q in range(2):
                        for j in range(4):
                            last = pe.matmul(bank[2 * u + q][:, 128 * j:128 * j + 128],
                                             w[:, 512 * q + 128 * j:512 * q + 128 * j + 128],
                                             xgT[:, bass.ds(i * (4 * CAP) + (2 * u + q) * CAP, 128)],
                                             start=True, stop=True)
                        last.then_inc(sem(f"moe_up{u}"), 1)
                    for j in range(2):
                        last = pe.matmul(bank[4 + u][:, 2 * CAP * j:2 * CAP * j + 2 * CAP],
                                         w[:, 1536 + 128 * j:1536 + 128 * j + 128],
                                         xgT[:, bass.ds(i * (4 * CAP) + 2 * u * CAP, 2 * CAP)],
                                         start=True, stop=True)
                    last.then_inc(sem(f"moe_up{u}"), 1)
                for u in range(2):
                    w = moe_w[u]
                    pe.wait_ge(sem(f"moe_acted{u}"), i * 3 + 3)
                    for q in range(2):
                        y = bank[6 + u][0:CAP, C * q:C * q + C]
                        for j in range(2):
                            pe.matmul(y, moe_act[u][:, q, CAP * j:CAP * j + CAP],
                                      w[:, 1024 + 256 * q + 128 * j:1024 + 256 * q + 128 * j + 128],
                                      start=(j == 0), stop=False)
                        last = pe.matmul(y, moe_act[u][:, 2, CAP * q:CAP * q + CAP], w[:, 1792:1920],
                                         start=False, stop=True)
                    last.then_inc(sem(f"moe_y{u}"), 1)

            for b in range(B):
                pe.wait_ge(sem("y_summed"), b + 1)
                for i in range(TB):
                    last = pe.transpose(bank[b][:, 128 * i:128 * i + 128], y_sum[:, TB * b + i, :], ident[:, :])
                last.then_inc(sem("moe_out"), 1)

        def moe_act_engine(act):
            htok_act(act, B)
            act.wait_ge(sem("moe_moments"), 2)
            nc.scalar.activation(stat[:, :, 1], stat[:, :, 1], ACT.Sqrt).then_inc(sem("moe_roots"), 1)
            nc.scalar.activation(stat[:, :, 4], stat[:, :, 4], ACT.Sqrt).then_inc(sem("moe_roots"), 1)
            for b in range(B):
                act.wait_ge(sem("moe_hid_raw"), b + 1)
                nc.scalar.activation(r_hid[:, b, :], bank[b][0:64, :], ACT.Gelu, bias=v("r1_b")[0:64, :]) \
                  .then_inc(sem("moe_hid_ready"), 1)
            act.wait_ge(sem("moe_shifted"), 1)
            nc.scalar.activation(prob[:, :, :], prob[:, :, :], ACT.Exp).then_inc(sem("moe_exp"), 1)
            for s in range(NB128 // 4):
                act.wait_ge(sem("xgT_raw"), s + 1)
                nc.scalar.activation(xgT[:, 512 * s:512 * s + 512], bank[s][:, :], ACT.Copy) \
                  .then_inc(sem("xgT_ready"), 1)
            nc.scalar.preload_act_table(ACT.Silu)
            with act.Fori(0, G // 2) as i:
                for u in range(2):
                    for q in range(3):
                        act.wait_ge(sem(f"moe_up{u}"), i * 3 + (q + 1))
                        src = up(u, q, 0) if q < 2 else bank[4 + u][:, 0:2 * CAP].rearrange("p (j c) -> p j c", j=2)
                        nc.scalar.activation(moe_silu[u][:, q, :].rearrange("p (j c) -> p j c", j=2), src, ACT.Silu) \
                          .then_inc(sem(f"moe_silued{u}"), 1)

        def moe_dve(dve):
            def L(ins):
                link(dve, "dve", ins)

            for b in range(B):
                dve.wait_ge(sem("htok_ready"), B + b + 1)
                for i in range(TB):
                    t = TB * b + i
                    last = nc.vector.bn_stats(bn[:, t, :], htok[:, t, :])
            L(last)
            for t in range(TILES):
                last = nc.vector.bn_aggr(mv[:, t, :], bn[:, t, :])
            L(last)
            nc.vector.tensor_scalar(stat[:, :, 1], mv[:, :, 1], C / (C - 1.0), None, ALU.mult) \
              .then_inc(sem("moe_moments"), 1)
            L(nc.vector.tensor_tensor(stat[:, :, 0], mv[:, :, 0], mv[:, :, 0], ALU.mult))
            L(nc.vector.tensor_tensor(stat[:, :, 4], stat[:, :, 0], mv[:, :, 1], ALU.add))
            nc.vector.tensor_scalar(stat[:, :, 4], stat[:, :, 4], float(C), None, ALU.mult) \
              .then_inc(sem("moe_moments"), 1)
            L(nc.vector.tensor_copy(stat[:, :, 0], mv[:, :, 0]))
            nc.vector.tensor_reduce(stat[:, :, 2], htok[:, :, :], AX_X, ALU.min)
            nc.vector.tensor_reduce(stat[:, :, 3], htok[:, :, :], AX_X, ALU.max)
            L(nc.vector.scalar_tensor_tensor(small[:, :, :], htok[:, :, :], -1.0, htok[:, :, :], ALU.mult, ALU.max))
            L(nc.vector.tensor_scalar(small[:, :, :], small[:, :, :], 1e-6, None, ALU.is_lt))
            L(nc.vector.tensor_reduce(stat[:, :, 5], small[:, :, :], AX_X, ALU.add))
            dve.wait_ge(sem("moe_roots"), 2)
            nc.vector.tensor_scalar(stat[:, :, 5], stat[:, :, 5], 1.0 / C, None, ALU.mult) \
              .then_inc(sem("moe_stats"), 1)
            for b in range(B):
                dve.wait_ge(sem("moe_statT_raw"), b + 1)
                nc.vector.tensor_copy(statT[:, b, :], bank[4 + b][0:6, :]).then_inc(sem("moe_statT_ready"), 1)

            dve.wait_ge(sem("moe_logits"), 1)
            logits = bank[4][:, :].rearrange("p (t e) -> p t e", e=E)
            L(nc.vector.tensor_reduce(r_max[:, :], logits, AX_X, ALU.max))
            nc.vector.tensor_tensor(prob[:, :, :], logits, r_max[:, :].unsqueeze(2).to_broadcast([128, TILES, E]),
                                    ALU.subtract).then_inc(sem("moe_shifted"), 1)
            dve.wait_ge(sem("moe_exp"), 1)
            L(nc.vector.tensor_reduce(r_sum[:, :], prob[:, :, :], AX_X, ALU.add))
            L(nc.vector.reciprocal(r_inv[:, :], r_sum[:, :]))
            L(nc.vector.tensor_tensor(prob[:, :, :], prob[:, :, :],
                                      r_inv[:, :].unsqueeze(2).to_broadcast([128, TILES, E]), ALU.mult))
            for t in range(TILES):
                last = nc.vector.max(top8[:, t, :], prob[:, t, :])
            L(last)
            for t in range(TILES):
                last = nc.vector.max_index(top8_at[:, t, :], top8[:, t, :], prob[:, t, :])
            L(last)
            L(nc.vector.tensor_copy(pick[:, :, :].rearrange("p k t -> p t k"), top8_at[:, :, 0:2]))
            experts = iota_e[:, :].unsqueeze(1).to_broadcast([128, TILES, E])
            for k in range(2):
                last = nc.vector.tensor_tensor(onehot[:, k, :, :], experts,
                                               pick[:, k, :].unsqueeze(2).to_broadcast([128, TILES, E]), ALU.is_equal)
            L(last)
            L(nc.vector.tensor_tensor(hit[:, :, :], onehot[:, 0, :, :], onehot[:, 1, :, :], ALU.add))
            L(nc.vector.tensor_tensor(prob[:, :, :], prob[:, :, :], hit[:, :, :], ALU.mult))
            L(nc.vector.tensor_scalar(hit[:, :, :], hit[:, :, :], -1.0, None, ALU.add))
            nc.vector.tensor_tensor(score[:, :, :, :].rearrange("p g j e -> p j g e"),
                                    prob[:, :, :].rearrange("p (j g) e -> p j g e", j=B),
                                    hit[:, :, :].rearrange("p (j g) e -> p j g e", j=B), ALU.add) \
              .then_inc(sem("moe_scored"), 1)
            L(nc.vector.tensor_tensor(r_sum[:, :], top8[:, :, 0], top8[:, :, 1], ALU.add))
            L(nc.vector.reciprocal(r_inv[:, :], r_sum[:, :]))
            for k in range(2):
                last = nc.vector.tensor_tensor(weight[:, k, :], top8[:, :, k], r_inv[:, :], ALU.mult)
            L(last)
            dve.wait_ge(sem("moe_scoreT_raw"), 1)
            L(nc.vector.tensor_copy(scoreT[:, :], bank[5][:, :]))
            for r in range(ROUNDS):
                src = scoreT if r == 0 else rest[(r - 1) % 2]
                L(nc.vector.max(best[:, 8 * r:8 * r + 8], src[:, :]))
                if r < ROUNDS - 1:
                    L(nc.vector.match_replace(rest[r % 2][:, :], best[:, 8 * r:8 * r + 8], src[:, :], -2.0))
            nc.vector.memset(xgT[:, SLOTS:], 0.0)
            nc.vector.memset(ones[:, :], 1.0).then_inc(sem("moe_best"), 1)
            dve.wait_ge(sem("moe_spread"), 16 * B)
            for r in range(ROUNDS):
                src = cand[r % 2][:, :, :].rearrange("e j c -> e (j c)")
                L(nc.vector.max(best_all[:, 8 * r:8 * r + 8], src))
                if r < ROUNDS - 1:
                    L(nc.vector.match_replace(cand[(r + 1) % 2][:, :, :].rearrange("e j c -> e (j c)"),
                                              best_all[:, 8 * r:8 * r + 8], src, -2.0))
            L(nc.vector.tensor_copy(cut[:, 0:1], best_all[:, CAP - 1:CAP]))
            L(nc.vector.tensor_scalar(above_last[:, :], best_all[:, :], cut[:, 0:1], None, ALU.is_gt))
            nc.vector.tensor_reduce(cut[:, 1:2], above_last[:, :], AX_X, ALU.add).then_inc(sem("moe_cut"), 1)
            dve.wait_ge(sem("moe_spread"), 32 * B)
            nc.vector.tensor_scalar(is_gt[:, :], scoreT[:, :], cut4[:, 0:1], None, ALU.is_gt)
            L(nc.vector.tensor_scalar(is_eq[:, :], scoreT[:, :], cut4[:, 0:1], None, ALU.is_equal))
            nc.vector.tensor_tensor_scan(cum_gt[:, :], ones[:, :], is_gt[:, :], 0.0, ALU.mult, ALU.add)
            L(nc.vector.tensor_tensor_scan(cum_eq[:, :], ones[:, :], is_eq[:, :], 0.0, ALU.mult, ALU.add))
            nc.vector.tensor_copy(totals[:, 0:1], cum_gt[:, T - 1:T]).then_inc(sem("moe_totals"), 1)
            nc.vector.tensor_copy(totals[:, 1:2], cum_eq[:, T - 1:T]).then_inc(sem("moe_totals"), 1)
            dve.wait_ge(sem("moe_offset_raw"), 1)
            nc.vector.tensor_copy(offset[:, 0:1], bank[6][:, 0:1])
            L(nc.vector.tensor_tensor(offset[:, 1:2], bank[6][:, 1:2], cut4[:, 1:2], ALU.add))
            L(nc.vector.scalar_tensor_tensor(cum_gt[:, :], cum_gt[:, :], offset[:, 0:1], is_gt[:, :], ALU.add, ALU.mult))
            L(nc.vector.scalar_tensor_tensor(cum_eq[:, :], cum_eq[:, :], offset[:, 1:2], is_eq[:, :], ALU.add, ALU.mult))
            nc.vector.tensor_tensor(cum_gt[:, :], cum_gt[:, :], cum_eq[:, :], ALU.add).then_inc(sem("moe_placed"), 1)
            dve.wait_ge(sem("moe_placeT"), 1)
            placeT = bank[7][:, :].rearrange("p (g j e) -> p j g e", g=4, j=B)
            for k in range(2):
                last = nc.vector.tensor_tensor(looked[:, k, :, :].rearrange("p (j g) e -> p j g e", j=B),
                                               onehot[:, k, :, :].rearrange("p (j g) e -> p j g e", j=B), placeT, ALU.mult)
            L(last)
            L(nc.vector.tensor_reduce(place[:, :, :], looked[:, :, :, :], AX_X, ALU.add))
            L(nc.vector.tensor_scalar(valid[:, :, :], place[:, :, :], 1.0, None, ALU.is_ge))
            L(nc.vector.scalar_tensor_tensor(valid[:, :, :], place[:, :, :], float(CAP), valid[:, :, :],
                                             ALU.is_le, ALU.mult))
            L(nc.vector.scalar_tensor_tensor(slot[:, :, :], pick[:, :, :], float(CAP), place[:, :, :],
                                             ALU.mult, ALU.add))
            L(nc.vector.scalar_tensor_tensor(slot[:, :, :], slot[:, :, :], -1.0 - DUMP, valid[:, :, :],
                                             ALU.add, ALU.mult))
            L(nc.vector.tensor_scalar(slot[:, :, :], slot[:, :, :], float(DUMP), None, ALU.add))
            nc.vector.tensor_copy(slot_u[:, :, :], slot[:, :, :]).then_inc(sem("moe_slots"), 1)
            L(nc.vector.tensor_tensor(weight[:, :, :], weight[:, :, :], valid[:, :, :], ALU.mult))

            with dve.Fori(0, G // 2) as i:
                for u in range(2):
                    for q in range(2):
                        dve.wait_ge(sem(f"moe_silued{u}"), i * 3 + (q + 1))
                        nc.vector.tensor_tensor(moe_act[u][:, q, :].rearrange("p (j c) -> p j c", j=2),
                                                moe_silu[u][:, q, :].rearrange("p (j c) -> p j c", j=2),
                                                up(u, q, 2), ALU.mult) \
                          .then_inc(sem(f"moe_acted{u}"), 1)
                    dve.wait_ge(sem(f"moe_silued{u}"), i * 3 + 3)
                    nc.vector.scalar_tensor_tensor(moe_act[u][:, 2, :], moe_silu[u][:, 2, :], 0.05,
                                                   bank[4 + u][:, 2 * CAP:4 * CAP], ALU.mult, ALU.mult) \
                      .then_inc(sem(f"moe_acted{u}"), 1)
                for u in range(2):
                    dve.wait_ge(sem(f"moe_y{u}"), i + 1)
                    dve.wait_ge(sem(f"moe_stored{u}"), i * 16 + 16)
                    nc.vector.tensor_copy(y_slot[u][:, :, :],
                                          bank[6 + u][0:CAP, 0:2 * C].rearrange("p (q c) -> p q c", q=2)) \
                      .then_inc(sem(f"moe_y_read{u}"), 1)

            for b in range(B):
                dve.wait_ge(sem(f"y_gathered{b}"), 16 * 2 * TB)
                for t in range(TB * b, TB * b + TB):
                    last = nc.vector.tensor_scalar(y_sum[:, t, :], y_tok[:, 0, t, :], weight[:, 0, t:t + 1], None,
                                                   ALU.mult)
                L(last)
                for t in range(TB * b, TB * b + TB):
                    last = nc.vector.scalar_tensor_tensor(y_sum[:, t, :], y_tok[:, 1, t, :], weight[:, 1, t:t + 1],
                                                          y_sum[:, t, :], ALU.mult, ALU.add)
                last.then_inc(sem("y_summed"), 1)
            for b in range(B):
                dve.wait_ge(sem("moe_out"), b + 1)
                nc.vector.scalar_tensor_tensor(x[:, b, :], bank[b][:, :], gate(3, b), x[:, b, :],
                                               ALU.mult, ALU.add).then_inc(sem("x_ready"), 1)

        def moe_sp(sp):
            for name, dst in (("r1_c", r1_c), ("r1_s", r1_s), ("r2_w", r2_w), ("iota_e", iota_e),
                              ("chunk_sum", chunk_sum)):
                sp.dma_start(dst[:, :], d[name]).then_inc(sem("moe_loaded"), 16)
            sp.wait_ge(sem("filled"), 2)
            for s in range(NB128 // 4):
                sp.dma_start(xg_dram[512 * s:512 * s + 512, :].rearrange("(p r) c -> p (r c)", p=128),
                             zeros[:, :]).then_inc(sem("moe_zeroed"), 16)
            for u in range(2):
                sp.dma_start(y_dram[SLOTS:SLOTS + 1, 64 * u:64 * u + 64], zeros[0:1, 0:64]) \
                  .then_inc(sem(f"moe_stored{u}"), 16)
            for u in range(2):
                sp.dma_start(moe_w[u][:, :], d["moe_w"][u, :, :]).then_inc(sem(f"moe_w_loaded{u}"), 16)
            sp.wait_ge(sem("moe_best"), 1)
            for j in range(B):
                sp.dma_start(cand[0][:, j, :], best[E * j:E * j + E, :]).then_inc(sem("moe_spread"), 16)
            sp.wait_ge(sem("moe_cut"), 1)
            for j in range(B):
                sp.dma_start(cut4[E * j:E * j + E, :], cut[:, :]).then_inc(sem("moe_spread"), 16)
            sp.wait_ge(sem("xg_scattered"), 16 * 2 * TILES)
            sp.dma_start(xg[:, :, :], xg_dram.rearrange("(s p) c -> p s c", p=128)).then_inc(sem("xg_loaded"), 16)

            def store(i, u):
                sp.wait_ge(sem(f"moe_y_read{u}"), i + 1)
                row = i * (4 * CAP) + 2 * u * CAP
                rows = slice(row, row + 2 * CAP) if isinstance(i, int) else bass.ds(row, 2 * CAP)
                sp.dma_start(y_dram[rows, :].rearrange("(q p) c -> p q c", q=2), y_slot[u][:, :, :]) \
                  .then_inc(sem(f"moe_stored{u}"), 16)

            with sp.Fori(0, G // 2 - 1) as i:
                for u in range(2):
                    sp.wait_ge(sem(f"moe_y{u}"), i + 1)
                    sp.dma_start(moe_w[u][:, :], d["moe_w"][bass.ds(i * 2 + (2 + u), 1), :, :]
                                 .rearrange("o p w -> (o p) w")).then_inc(sem(f"moe_w_loaded{u}"), 16)
                    store(i, u)
            for u in range(2):
                store(G // 2 - 1, u)

        def moe_pool(pool):
            pool.wait_ge(sem("moe_slots"), 1)
            pool.wait_ge(sem("moe_zeroed"), 16 * (NB128 // 4))
            for t in range(TILES):
                for k in range(2):
                    nc.gpsimd.indirect_dma_start(
                        xg_dram, bass.IndirectOffsetOnAxis(slot_u[:, k, t:t + 1], 0), htok[:, t, :], None,
                        bounds_check=SLOTS - 1, oob_is_err=False).then_inc(sem("xg_scattered"), 16)
            for u in range(2):
                pool.wait_ge(sem(f"moe_stored{u}"), 16 * (G // 2) + 16)
            for t in range(TILES):
                for k in range(2):
                    nc.gpsimd.indirect_dma_start(
                        y_tok[:, k, t, :], None, y_dram, bass.IndirectOffsetOnAxis(slot_u[:, k, t:t + 1], 0)) \
                      .then_inc(sem(f"y_gathered{t // TB}"), 16)

        next_block()
        q_diag = [tmp_sb(f"q_diag{i}", [128, NBLK, 128]) for i in range(2)]
        k_rope = [tmp_sb(f"k_rope{i}", [128, T]) for i in range(2)]
        rope_part = [tmp_sb(f"rope_part{i}", [128, T]) for i in range(4)]
        v_tok = [tmp_sb(f"v_tok{i}", [128, TB, 128]) for i in range(B)]
        soft = [tmp_sb(f"soft{i}", [128, PW]) for i in range(2)]
        softT = tmp_sb("softT", [128, NFILL * 512])
        neg_max = tmp_sb("neg_max", [128, 2, NBLK])
        exp_sum = tmp_sb("exp_sum", [128, 2, NBLK])
        exp_inv = tmp_sb("exp_inv", [128, 2, NBLK])
        head_out = [tmp_sb(f"head_out{i}", [128, T]) for i in range(2)]
        gate_bo = tmp_sb("gate_bo", [128, B])
        att_w = tmp_sb("att_w", [C, 5, 128])
        att_wo = tmp_sb("att_wo", [128, C])
        rope_tab = tmp_sb("rope_tab", [128, 4, T])
        att_mask = tmp_sb("att_mask", [128, 64])

        def keys(j):
            return 64 * (j + 1)

        def att_project(pe, r, b, w, piece):
            pe.wait_ge(sem("att_w_loaded"), w * 16 + 16)
            pe.wait_ge(sem("proj_read"), r * 5 + piece)
            if piece < 4:
                last = pe.matmul(bank[0][:, :], att_w[:, piece, :], hb(b), start=True, stop=True)
            else:
                for i in range(TB):
                    last = pe.matmul(bank[0][:, 128 * i:128 * i + 128], hh(b, 128 * i, 128), att_w[:, 4, :],
                                     start=True, stop=True)
            last.then_inc(sem("proj_raw"), 1)

        def att_scores(pe, m, par, g, first):
            if g == 0:
                pe.wait_ge(sem("roped"), m * 3 + 3)
            if g >= 2:
                pe.wait_ge(sem("s_exp"), m * 8 + GCUM[g - 2])
            elif not first:
                pe.wait_ge(sem("s_exp"), m * 8 + (GCUM[g + 3] - 8))
            at = 0
            for j in GROUPS[g]:
                last = pe.matmul(bank[1 + (5 * par + g) % 2][:, at:at + keys(j)], q_diag[par][:, j, :],
                                 k_rope[par][:, 0:keys(j)], start=True, stop=True)
                at += keys(j)
            last.then_inc(sem("s_raw"), 1)

        def att_step_pe(pe, n, b, w, scores=True, project=True):
            for g in range(5):
                if scores:
                    att_scores(pe, n + 1, (b + 1) % 2, g, False)
                if project:
                    att_project(pe, n + 2, (b + 2) % B, w + (b + 2) // B, g)
            pe.wait_ge(sem("p_normed"), n + 1)
            for f in range(NFILL):
                if f >= 2:
                    pe.wait_ge(sem("pt_ready"), n * 5 + (f - 1))
                for q in range(4 * f, 4 * f + 4):
                    jc, j = CHUNKS[q]
                    last = pe.transpose(bank[3 + (5 * b + f) % 2][:, 128 * (q % 4):128 * (q % 4) + 128],
                                        soft[b % 2][:, POFF[j] + 128 * jc:POFF[j] + 128 * jc + 128], ident[:, :])
                last.then_inc(sem("pt_raw"), 1)
            pe.wait_ge(sem("pt_ready"), n * 5 + 5)
            for half in range(2):
                js = range(4 * half, 4 * half + 4)
                for jc in range(2 * half + 2):
                    q = [i for i, (a, j) in enumerate(CHUNKS) if a == jc and j in js]
                    lo = 128 * (CHUNKS[q[0]][1] - 4 * half)
                    last = pe.matmul(bank[5 + half][:, lo:512], v_tok[b][:, jc, :],
                                     softT[:, 128 * q[0]:128 * q[-1] + 128], start=(jc == 0), stop=(jc == 2 * half + 1))
                last.then_inc(sem("pv_raw"), 1)
            pe.wait_ge(sem("att_wo_loaded"), w * 16 + 16)
            pe.wait_ge(sem("pair_added"), n + B)
            for half in range(2):
                pe.wait_ge(sem("pv_read"), n * 4 + (2 * half + 2))
                last = pe.matmul(bank[7][:, 256 * half:256 * half + 256], att_wo[:, :],
                                 head_out[b % 2][:, 256 * half:256 * half + 256], start=True, stop=True)
            last.then_inc(sem("att_out"), 1)

        def att_pe(pe):
            pe.wait_ge(sem("h_ready"), 20)
            pe.wait_ge(sem("ln_normed"), 20)
            for g in range(5):
                att_project(pe, 0, 0, 0, g)
            for g in range(5):
                att_scores(pe, 0, 0, g, True)
                att_project(pe, 1, 1, 0, g)
            with pe.Fori(0, PAIRS - 1) as i:
                for b in range(B):
                    att_step_pe(pe, i * 4 + b, b, i)
            for b in range(B):
                att_step_pe(pe, 4 * (PAIRS - 1) + b, b, PAIRS - 1, scores=(b < 3), project=(b < 2))

        def att_exps(act, m, par, g):
            act.wait_ge(sem("s_max"), m * 8 + GCUM[g])
            at = 0
            for j in GROUPS[g]:
                nc.scalar.activation(soft[par][:, POFF[j]:POFF[j] + keys(j)],
                                     bank[1 + (5 * par + g) % 2][:, at:at + keys(j)], ACT.Exp,
                                     bias=neg_max[:, par, j:j + 1], accum_out=exp_sum[:, par, j:j + 1]) \
                  .then_inc(sem("s_exp"), 1)
                at += keys(j)

        def att_v(act, r, b):
            act.wait_ge(sem("proj_raw"), r * 5 + 5)
            nc.scalar.activation(v_tok[b][:, :, :], bank[0][:, :].rearrange("p (i c) -> p i c", i=TB), ACT.Copy) \
              .then_inc(sem("proj_read"), 1)

        def att_step_act(act, n, b, scores=True, project=True):
            for g in range(5):
                if scores:
                    att_exps(act, n + 1, (b + 1) % 2, g)
            if project:
                att_v(act, n + 2, (b + 2) % B)
            act.wait_ge(sem("pv_raw"), n * 2 + B)
            for f in range(NFILL):
                act.wait_ge(sem("pt_raw"), n * 5 + (f + 1))
                nc.scalar.activation(softT[:, 512 * f:512 * f + 512], bank[3 + (5 * b + f) % 2][:, :], ACT.Copy) \
                  .then_inc(sem("pt_ready"), 1)

        def att_act(act):
            nc.scalar.preload_act_table_set("natural_log_exp_and_others")
            att_v(act, 0, 0)
            for g in range(5):
                att_exps(act, 0, 0, g)
            att_v(act, 1, 1)
            with act.Fori(0, PAIRS - 1) as i:
                for b in range(B):
                    att_step_act(act, i * 4 + b, b)
            for b in range(B):
                att_step_act(act, 4 * (PAIRS - 1) + b, b, scores=(b < 3), project=(b < 2))

        def att_rope(dve, r, piece, first):
            dve.wait_ge(sem("proj_raw"), r * 5 + (piece + 1))
            if not first:
                dve.wait_ge(sem("roped"), r * 3 + (-1 if piece < 2 else 0))
            nc.vector.tensor_tensor(rope_part[piece][:, :], bank[0][:, :], rope_tab[:, piece, :], ALU.mult) \
              .then_inc(sem("proj_read"), 1)

        def att_maxes(dve, m, par, g):
            dve.wait_ge(sem("s_raw"), m * 5 + (g + 1))
            at = 0
            for k, j in enumerate(GROUPS[g]):
                c = GCUM[g] - len(GROUPS[g]) + k
                s = bank[1 + (5 * par + g) % 2][:, at:at + keys(j)]
                nc.vector.tensor_tensor(s[:, keys(j) - 64:keys(j)], s[:, keys(j) - 64:keys(j)], att_mask[:, :],
                                        ALU.add).then_inc(sem("s_masked"), 1)
                dve.wait_ge(sem("s_masked"), m * 8 + (c + 1))
                nc.vector.tensor_reduce(neg_max[:, par, j:j + 1], s, AX_X, ALU.max, negate=True) \
                  .then_inc(sem("s_max"), 1)
                at += keys(j)

        def att_norm(dve, m, par):
            dve.wait_ge(sem("s_exp"), m * 8 + 8)
            nc.vector.reciprocal(exp_inv[:, par, :], exp_sum[:, par, :]).then_inc(sem("s_inv"), 1)
            dve.wait_ge(sem("s_inv"), m + 1)
            for j in range(NBLK):
                p = soft[par][:, POFF[j]:POFF[j] + keys(j)]
                last = nc.vector.tensor_scalar(p, p, exp_inv[:, par, j:j + 1], None, ALU.mult)
            last.then_inc(sem("p_normed"), 1)

        def att_step_dve(dve, n, b, scores=True, project=True):
            for g in range(5):
                if scores:
                    att_maxes(dve, n + 1, (b + 1) % 2, g)
                if project and g < 4:
                    att_rope(dve, n + 2, g, False)
            if scores:
                att_norm(dve, n + 1, (b + 1) % 2)
            for half in range(2):
                dve.wait_ge(sem("pv_raw"), n * 2 + (B + half + 1))
                for hd in range(2):
                    lo = 64 * hd
                    nc.vector.tensor_copy(
                        head_out[b % 2][lo:lo + 64, 256 * half:256 * half + 256].rearrange("p (j i) -> p j i", j=4),
                        bank[5 + half][lo:lo + 64, :].rearrange("p (j h i) -> p j h i", j=4, h=2)[:, :, hd, :]) \
                      .then_inc(sem("pv_read"), 1)
            dve.wait_ge(sem("att_out"), n + 1)
            dve.wait_ge(sem("pair_added"), n + 1)
            nc.vector.scalar_tensor_tensor(x[:, b, :], bank[7][:, :], gate(4, b), x[:, b, :], ALU.mult, ALU.add) \
              .then_inc(sem("pair_added"), 1)

        def att_dve(dve):
            link(dve, "dve", nc.vector.tensor_scalar(gate_bo[:, :], mod[:, 2, 2, :], v("attn2_bo"), None, ALU.mult))
            for b in range(B):
                dve.wait_ge(sem("h_ready"), 16 + b + 1)
                nc.vector.tensor_scalar(x[:, b, :], x[:, b, :], gate_bo[:, b:b + 1], None, ALU.add) \
                  .then_inc(sem("pair_added"), 1)
            dve.wait_ge(sem("att_tables"), 32)
            dve.wait_ge(sem("soft_zeroed"), 4)
            for g in range(4):
                att_rope(dve, 0, g, True)
            for g in range(5):
                att_maxes(dve, 0, 0, g)
                if g < 4:
                    att_rope(dve, 1, g, False)
            att_norm(dve, 0, 0)
            with dve.Fori(0, PAIRS - 1) as i:
                for b in range(B):
                    att_step_dve(dve, i * 4 + b, b)
            for b in range(B):
                att_step_dve(dve, 4 * (PAIRS - 1) + b, b, scores=(b < 3), project=(b < 2))

        def att_sum(pool, r, par, first):
            if not first:
                pool.wait_ge(sem("s_raw"), r * 5 - 5)
            pool.wait_ge(sem("proj_read"), r * 5 + 2)
            for hd in range(2):
                lo = 64 * hd
                pool.wait_ge(sem("roped"), r * 3 + hd)
                nc.gpsimd.tensor_tensor(q_diag[par][lo:lo + 64, :, lo:lo + 64],
                                        rope_part[0][lo:lo + 64, :].rearrange("p (j i) -> p j i", i=64),
                                        rope_part[1][lo:lo + 64, :].rearrange("p (j i) -> p j i", i=64), ALU.add) \
                  .then_inc(sem("roped"), 1)
            pool.wait_ge(sem("proj_read"), r * 5 + 4)
            pool.wait_ge(sem("roped"), r * 3 + 2)
            nc.gpsimd.tensor_tensor(k_rope[par][:, :], rope_part[2][:, :], rope_part[3][:, :], ALU.add) \
              .then_inc(sem("roped"), 1)

        def att_pool(pool):
            for i in range(2):
                nc.gpsimd.memset(soft[i][:, :], 0.0).then_inc(sem("soft_zeroed"), 1)
                nc.gpsimd.memset(q_diag[i][:, :, :], 0.0).then_inc(sem("soft_zeroed"), 1)
            pool.wait_ge(sem("soft_zeroed"), 4)
            att_sum(pool, 0, 0, True)
            att_sum(pool, 1, 1, True)
            with pool.Fori(0, PAIRS - 1) as i:
                for b in range(B):
                    att_sum(pool, i * 4 + (b + 2), b % 2, False)
            for b in range(2):
                att_sum(pool, 4 * (PAIRS - 1) + b + 2, b % 2, False)

        def att_sp(sp):
            sp.wait_ge(sem("h_ready"), 17)
            sp.dma_start(att_w[:, :, :], d["att_w"][0, :, :, :]).then_inc(sem("att_w_loaded"), 16)
            sp.dma_start(rope_tab[:, :, :], d["rope_tab"]).then_inc(sem("att_tables"), 16)
            sp.dma_start(att_mask[:, :], d["att_mask"]).then_inc(sem("att_tables"), 16)
            sp.dma_start(att_wo[:, :], d["att_wo"][0, :, :]).then_inc(sem("att_wo_loaded"), 16)
            with sp.Fori(0, PAIRS - 1) as i:
                sp.wait_ge(sem("proj_raw"), i * 20 + 20)
                sp.dma_start(att_w[:, :, :], d["att_w"][bass.ds(i + 1, 1), :, :, :]
                             .rearrange("o p j n -> (o p) j n")).then_inc(sem("att_w_loaded"), 16)
                sp.wait_ge(sem("att_out"), i * 4 + 4)
                sp.dma_start(att_wo[:, :], d["att_wo"][bass.ds(i + 1, 1), :, :]
                             .rearrange("o p n -> (o p) n")).then_inc(sem("att_wo_loaded"), 16)

        next_block()
        mix_prev = tmp_sb("mix_prev", [C, 2, T])
        mix_r = tmp_sb("mix_r", [C, 2, T])
        mix_k = tmp_sb("mix_k", [C, 2, T])
        mix_gate = tmp_sb("mix_gate", [C, 2, T])
        mix_relu = tmp_sb("mix_relu", [C, 2, T])
        mix_w = tmp_sb("mix_w", [C, 3, C])

        def mix_sp(sp):
            sp.wait_ge(sem("h_ready"), 21)
            sp.dma_start(mix_w[:, :, :], d["mix_w"]).then_inc(sem("mix_loaded"), 16)

        def mix_dve(dve):
            def inputs(b):
                dve.wait_ge(sem("h_ready"), 20 + b + 1)
                if b >= 2:
                    dve.wait_ge(sem("mix_kr"), b - 1)
                now, prev = hb(b), hh(b, -1, T)
                link(dve, "dve", nc.vector.tensor_tensor(mix_prev[:, b % 2, :], now, prev, ALU.subtract))
                for dst, mu in ((mix_r, "mu_r"), (mix_k, "mu_k")):
                    nc.vector.scalar_tensor_tensor(dst[:, b % 2, :], mix_prev[:, b % 2, :], v(mu), prev,
                                                   ALU.mult, ALU.add).then_inc(sem("mix_in"), 1)
                dve.wait_ge(sem("mix_in"), 2 * b + 2)

            inputs(0)
            for b in range(B):
                if b + 1 < B:
                    inputs(b + 1)
                dve.wait_ge(sem("mix_relued"), b + 1)
                nc.vector.tensor_tensor(mix_relu[:, b % 2, :], mix_relu[:, b % 2, :], mix_relu[:, b % 2, :],
                                        ALU.mult).then_inc(sem("mix_squared"), 1)
                dve.wait_ge(sem("mix_v"), b + 1)
                dve.wait_ge(sem("mix_gated"), b + 1)
                link(dve, "dve", nc.vector.tensor_tensor(mix_gate[:, b % 2, :], bank[6][:, :], mix_gate[:, b % 2, :],
                                                         ALU.mult))
                nc.vector.scalar_tensor_tensor(x[:, b, :], mix_gate[:, b % 2, :], gate(5, b), x[:, b, :],
                                               ALU.mult, ALU.add).then_inc(sem("x_ready"), 1)

        def mix_act(act):
            for b in range(B):
                if b >= 2:
                    act.wait_ge(sem("x_ready"), 16 + b - 1)
                act.wait_ge(sem("mix_kr"), b + 1)
                nc.scalar.activation(mix_relu[:, b % 2, :], bank[4][:, :], ACT.Relu).then_inc(sem("mix_relued"), 1)
                nc.scalar.activation(mix_gate[:, b % 2, :], bank[5][:, :], ACT.Sigmoid).then_inc(sem("mix_gated"), 1)

        def mix_pe(pe):
            pe.wait_ge(sem("mix_loaded"), 16)
            for b in range(B):
                pe.wait_ge(sem("mix_in"), 2 * b + 2)
                if b:
                    pe.wait_ge(sem("mix_relued"), b)
                    pe.wait_ge(sem("mix_gated"), b)
                pe.matmul(bank[4][:, :], mix_w[:, 1, :], mix_k[:, b % 2, :], start=True, stop=True)
                pe.matmul(bank[5][:, :], mix_w[:, 0, :], mix_r[:, b % 2, :], start=True, stop=True) \
                  .then_inc(sem("mix_kr"), 1)
                pe.wait_ge(sem("mix_squared"), b + 1)
                if b:
                    pe.wait_ge(sem("x_ready"), 16 + b)
                pe.matmul(bank[6][:, :], mix_w[:, 2, :], mix_relu[:, b % 2, :], start=True, stop=True) \
                  .then_inc(sem("mix_v"), 1)

        class Window:
            def __init__(self, units, unroll, start, per, loaded, tables=None, slopes=False):
                self.units, self.unroll, self.start, self.per = units, unroll, start, per
                self.loaded = 16 * loaded
                self.tables, self.slopes = tables, slopes
                self.ssq_reader = "win_clip" if per["win_clip"] else "win_log"

            def at(self, name, n, k=0):
                return n * self.per[name] + (self.start[name] + k)

            def after(self):
                return {m: self.start[m] + self.units * c for m, c in self.per.items()}

        ROTATED = {"win_proj": 6, "win_proj_read": 6, "win_sq": 2, "win_ssq": 2, "win_clip": 2, "win_log": 2,
                   "win_rs": 2, "win_sum": 2, "win_q": 2, "win_k": 1, "win_s": 2, "win_biased": 2, "win_max": 2,
                   "win_exp": 8, "win_inv": 1, "win_normed": 1, "win_pt": 2, "win_pt_read": 2, "pv_raw": 2,
                   "win_pv_read": 4, "win_out": 1, "pair_added": 1}
        PLAIN = dict(ROTATED, win_proj=1, win_proj_read=0, win_sq=1, win_ssq=1, win_clip=0, win_log=1, win_rs=1,
                     win_sum=0, win_k=0)

        def win_alloc(pieces, own_kv):
            a = {"q": [tmp_sb(f"win_q{i}_{pieces}", [128, NBLK, 128]) for i in range(2)],
                 "soft": [tmp_sb(f"win_soft{i}_{pieces}", [128, NBLK, 128]) for i in range(2)],
                 "softT": tmp_sb(f"win_softT_{pieces}", [128, NBLK * 128]),
                 "neg_max": tmp_sb(f"win_neg_max_{pieces}", [128, 2, NBLK]),
                 "sum": tmp_sb(f"win_sum_{pieces}", [128, 2, NBLK]),
                 "inv": tmp_sb(f"win_inv_{pieces}", [128, 2, NBLK]),
                 "out": [tmp_sb(f"win_out{i}_{pieces}", [128, T]) for i in range(2)],
                 "w": tmp_sb(f"win_w_{pieces}", [C, pieces, 128]),
                 "wo": tmp_sb(f"win_wo_{pieces}", [128, C]),
                 "bias": tmp_sb(f"win_bias_{pieces}", [128, NBLK, 128]),
                 "sq": tmp_sb(f"win_sq_{pieces}", [128, 2, T]),
                 "log": tmp_sb(f"win_log_{pieces}", [128, 2, T]),
                 "rs": tmp_sb(f"win_rs_{pieces}", [128, 2, T])}
            if own_kv:
                a["part"] = [tmp_sb(f"win_part{i}", [128, T]) for i in range(4)]
                a["k"] = [tmp_sb(f"win_k{i}", [128, TP]) for i in range(2)]
                a["v"] = [tmp_sb(f"win_v{i}", [128, NBLK, 128]) for i in range(B)]
            return a

        def win_steps(W, eng, prologue, step):
            prologue()
            rounds = W.units // W.unroll
            with eng.Fori(0, rounds - 1) as i:
                for u in range(W.unroll):
                    step(i * W.unroll + u, u, i * (W.unroll // B) + u // B, True, True)
            for u in range(W.unroll):
                step(W.unroll * (rounds - 1) + u, u, (rounds - 1) * (W.unroll // B) + u // B,
                     u < W.unroll - 1, u < W.unroll - 2)

        def win_square_sum(pe, W, a, r, j, first):
            pe.wait_ge(sem("win_sq"), W.at("win_sq", r, j + 1))
            if not first:
                pe.wait_ge(sem("pair_added"), W.at("pair_added", r, -2))
            pe.wait_ge(sem(W.ssq_reader), W.at(W.ssq_reader, r, j))
            pe.matmul(bank[1][:, :], head_sum[:, :], a["sq"][:, j, :], start=True, stop=True) \
              .then_inc(sem("win_ssq"), 1)

        def win_project(pe, W, a, r, b, w, piece, tokens, first):
            pe.wait_ge(sem("win_w_loaded"), w * 16 + (16 + W.loaded))
            if W.per["win_proj"] > 1:
                pe.wait_ge(sem("win_proj_read"), W.at("win_proj_read", r, piece))
            else:
                pe.wait_ge(sem("win_q"), W.at("win_q", r))
            if piece < 4:
                last = pe.matmul(bank[0][:, :], a["w"][:, piece, :], tokens(b, 0, T), start=True, stop=True)
            else:
                for i in range(4):
                    j = 4 * (piece - 4) + i
                    last = pe.matmul(bank[0][:, 128 * i:128 * i + 128], tokens(b, 64 * j - 64, 128), a["w"][:, 4, :],
                                     start=True, stop=True)
            last.then_inc(sem("win_proj"), 1)

        def win_scores(pe, W, a, m, u, half, keys_of, first):
            if half == 0:
                pe.wait_ge(sem("win_q"), W.at("win_q", m, 2))
                if W.per["win_k"]:
                    pe.wait_ge(sem("win_k"), W.at("win_k", m, 1))
            if not first:
                pe.wait_ge(sem("win_exp"), W.at("win_exp", m, 4 * half - 4))
            for i in range(4):
                j = 4 * half + i
                last = pe.matmul(bank[2 + half][:, 128 * i:128 * i + 128], a["q"][u % 2][:, j, :], keys_of(u, j),
                                 start=True, stop=True)
            last.then_inc(sem("win_s"), 1)

        def win_pe(pe, W, a, tokens, keys_of, values_of):
            pieces = W.per["win_proj"]

            def lookahead(n, u, w, scores, project, first_s=False, first_p=False):
                u1, u2, w2 = (u + 1) % W.unroll, (u + 2) % W.unroll, w + (u % B + 2) // B

                def p(piece):
                    if project:
                        win_project(pe, W, a, n + 2, u2 % B, w2, piece, tokens, first_p)

                def ss(j):
                    if project:
                        win_square_sum(pe, W, a, n + 2, j, first_p)

                def s(half):
                    if scores:
                        win_scores(pe, W, a, n + 1, u1, half, keys_of, first_s)

                p(0)
                s(0)
                if pieces > 1:
                    p(1)
                    ss(0)
                    s(1)
                    p(2)
                    p(3)
                    ss(1)
                    p(4)
                    p(5)
                else:
                    s(1)
                    ss(0)

            def prologue():
                lookahead(-2, W.unroll - 2, -1, False, True, first_p=True)
                lookahead(-1, W.unroll - 1, -1, True, True, first_s=True, first_p=True)

            def step(n, u, w, scores, project):
                lookahead(n, u, w, scores, project)
                pe.wait_ge(sem("win_normed"), W.at("win_normed", n, 1))
                for f in range(2):
                    for j in range(4 * f, 4 * f + 4):
                        last = pe.transpose(bank[4 + f][:, 128 * (j % 4):128 * (j % 4) + 128],
                                            a["soft"][u % 2][:, j, :], ident[:, :])
                    last.then_inc(sem("win_pt"), 1)
                for f in range(2):
                    pe.wait_ge(sem("win_pt_read"), W.at("win_pt_read", n, f + 1))
                    for j in range(4 * f, 4 * f + 4):
                        last = pe.matmul(bank[6 + f][:, 128 * (j % 4):128 * (j % 4) + 128], values_of(u, j),
                                         a["softT"][:, 128 * j:128 * j + 128], start=True, stop=True)
                    last.then_inc(sem("pv_raw"), 1)
                pe.wait_ge(sem("win_wo_loaded"), w * 16 + (16 + W.loaded))
                s = W.ssq_reader
                pe.wait_ge(sem(s), W.at(s, n + 2, W.per[s]) if project else W.after()[s])
                pe.wait_ge(sem("pair_added"), W.at("pair_added", n))
                for half in range(2):
                    pe.wait_ge(sem("win_pv_read"), W.at("win_pv_read", n, 2 * half + 2))
                    last = pe.matmul(bank[1][:, 256 * half:256 * half + 256], a["wo"][:, :],
                                     a["out"][u % 2][:, 256 * half:256 * half + 256], start=True, stop=True)
                last.then_inc(sem("win_out"), 1)

            win_steps(W, pe, prologue, step)

        def win_norm_act(act, W, a, r, j, first):
            act.wait_ge(sem("win_proj"), W.at("win_proj", r, 2 * j + 1))
            if not first:
                act.wait_ge(sem("win_ssq"), W.at("win_ssq", r, j + 1) + -W.per["win_ssq"])
            nc.scalar.activation(a["sq"][:, j, :], bank[0][:, :], ACT.Square).then_inc(sem("win_sq"), 1)

        def win_norm_act2(act, W, a, r, j, first):
            if W.per["win_clip"]:
                act.wait_ge(sem("win_clip"), W.at("win_clip", r, j + 1))
                nc.scalar.activation(a["log"][:, j, :], a["sq"][:, j, :], ACT.Ln).then_inc(sem("win_log"), 1)
            else:
                act.wait_ge(sem("win_ssq"), W.at("win_ssq", r, j + 1))
                nc.scalar.activation(a["log"][:, j, :], bank[1][:, :], ACT.Ln, bias=rms_eps[:, 0:1],
                                     scale=1.0 / 64).then_inc(sem("win_log"), 1)
            act.wait_ge(sem("win_log"), W.at("win_log", r, j + 1))
            if not first:
                act.wait_ge(sem("win_k" if j else "win_q"), W.at("win_k" if j else "win_q", r))
            bias = ln_clip[:, 0:1] if W.per["win_clip"] else 0.0
            nc.scalar.activation(a["rs"][:, j, :], a["log"][:, j, :], ACT.Exp, scale=-0.5, bias=bias) \
              .then_inc(sem("win_rs"), 1)

        def win_exps(act, W, a, m, u, half):
            act.wait_ge(sem("win_max"), W.at("win_max", m, half + 1))
            for i in range(4):
                j = 4 * half + i
                nc.scalar.activation(a["soft"][u % 2][:, j, :], bank[2 + half][:, 128 * i:128 * i + 128], ACT.Exp,
                                     bias=a["neg_max"][:, u % 2, j:j + 1], accum_out=a["sum"][:, u % 2, j:j + 1]) \
                  .then_inc(sem("win_exp"), 1)

        def win_act(act, W, a):
            pieces = W.per["win_proj"]

            def lookahead(n, u, scores, project, first=False):
                u1, u2 = (u + 1) % W.unroll, (u + 2) % W.unroll
                if project:
                    win_norm_act(act, W, a, n + 2, 0, first)
                if scores:
                    win_exps(act, W, a, n + 1, u1, 0)
                if project:
                    win_norm_act2(act, W, a, n + 2, 0, first)
                if scores:
                    win_exps(act, W, a, n + 1, u1, 1)
                if project and pieces > 1:
                    win_norm_act(act, W, a, n + 2, 1, first)
                    win_norm_act2(act, W, a, n + 2, 1, first)
                    for f in range(2):
                        act.wait_ge(sem("win_proj"), W.at("win_proj", n + 2, 5 + f))
                        nc.scalar.activation(a["v"][u2 % B][:, 4 * f:4 * f + 4, :],
                                             bank[0][:, :].rearrange("p (i c) -> p i c", i=4), ACT.Copy) \
                          .then_inc(sem("win_proj_read"), 1)

            def prologue():
                lookahead(-2, W.unroll - 2, False, True, first=True)
                lookahead(-1, W.unroll - 1, True, True)

            def step(n, u, w, scores, project):
                lookahead(n, u, scores, project)
                act.wait_ge(sem("pv_raw"), W.at("pv_raw", n))
                for f in range(2):
                    act.wait_ge(sem("win_pt"), W.at("win_pt", n, f + 1))
                    nc.scalar.activation(a["softT"][:, 512 * f:512 * f + 512], bank[4 + f][:, :], ACT.Copy) \
                      .then_inc(sem("win_pt_read"), 1)

            win_steps(W, act, prologue, step)

        def win_maxes(dve, W, a, m, u, half, pair):
            dve.wait_ge(sem("win_s"), W.at("win_s", m, half + 1))
            s = bank[2 + half][:, :].rearrange("p (j k) -> p j k", j=4)
            t = a["bias"][:, 4 * half:4 * half + 4, :]
            if W.slopes:
                ins = nc.vector.scalar_tensor_tensor(s, t, vec[:, bass.ds(pair + VEC["slope"][0], 1)], s, ALU.mult, ALU.add)
            else:
                ins = nc.vector.tensor_tensor(s, s, t, ALU.add)
            ins.then_inc(sem("win_biased"), 1)
            dve.wait_ge(sem("win_biased"), W.at("win_biased", m, half + 1))
            nc.vector.tensor_reduce(a["neg_max"][:, u % 2, 4 * half:4 * half + 4], s, AX_X, ALU.max, negate=True) \
              .then_inc(sem("win_max"), 1)

        def win_dve(dve, W, a, scales, add):
            pieces = W.per["win_proj"]

            def to_diagonal(r, u, src, weight):
                dve.wait_ge(sem("win_rs"), W.at("win_rs", r, 1))
                for hd in range(2):
                    lo = 64 * hd
                    out_ = a["q"][u % 2][lo:lo + 64, :, lo:lo + 64]
                    q = src[lo:lo + 64, :].rearrange("p (j i) -> p j i", i=64)
                    rs = a["rs"][lo:lo + 64, 0, :].rearrange("p (j i) -> p j i", i=64)
                    if weight is None:
                        ins = nc.vector.tensor_tensor(out_, q, rs, ALU.mult)
                    else:
                        ins = nc.vector.scalar_tensor_tensor(out_, q, weight[lo:lo + 64, :], rs, ALU.mult, ALU.mult)
                    ins.then_inc(sem("win_q"), 1)

            def rotate(r, piece, first):
                dve.wait_ge(sem("win_proj"), W.at("win_proj", r, piece + 1))
                if piece % 2 == 0:
                    dve.wait_ge(sem("win_sq"), W.at("win_sq", r, piece // 2 + 1))
                if not first:
                    if piece < 2:
                        dve.wait_ge(sem("win_sum"), W.at("win_sum", r, -1))
                        dve.wait_ge(sem("win_q"), W.at("win_q", r))
                    else:
                        dve.wait_ge(sem("win_k"), W.at("win_k", r))
                nc.vector.scalar_tensor_tensor(a["part"][piece][:, :], bank[0][:, :], scales[piece],
                                               W.tables[:, piece, :], ALU.mult, ALU.mult) \
                  .then_inc(sem("win_proj_read"), 1)

            def clip(r, j):
                dve.wait_ge(sem("win_ssq"), W.at("win_ssq", r, j + 1))
                nc.vector.tensor_scalar(a["sq"][:, j, :], bank[1][:, :], 1e-24, 2.0 ** 30, ALU.max, ALU.mult) \
                  .then_inc(sem("win_clip"), 1)

            def lookahead(n, u, w, scores, project, first=False):
                u1, u2 = (u + 1) % W.unroll, (u + 2) % W.unroll
                pair = w + (u % B + 1) // B
                if pieces > 1:
                    if project:
                        rotate(n + 2, 0, first)
                    if scores:
                        win_maxes(dve, W, a, n + 1, u1, 0, pair)
                    if project:
                        rotate(n + 2, 1, first)
                        clip(n + 2, 0)
                    if scores:
                        win_maxes(dve, W, a, n + 1, u1, 1, pair)
                    if project:
                        rotate(n + 2, 2, first)
                        rotate(n + 2, 3, first)
                        clip(n + 2, 1)
                        dve.wait_ge(sem("win_sum"), W.at("win_sum", n + 2, 1))
                        to_diagonal(n + 2, u2, a["part"][0], None)
                else:
                    for half in range(2):
                        if scores:
                            win_maxes(dve, W, a, n + 1, u1, half, pair)
                    if project:
                        to_diagonal(n + 2, u2, bank[0], scales[0])
                if scores:
                    dve.wait_ge(sem("win_exp"), W.at("win_exp", n + 1, 8))
                    nc.vector.reciprocal(a["inv"][:, u1 % 2, :], a["sum"][:, u1 % 2, :]).then_inc(sem("win_inv"), 1)
                    dve.wait_ge(sem("win_inv"), W.at("win_inv", n + 1, 1))
                    nc.vector.tensor_tensor(a["soft"][u1 % 2][:, :, :], a["soft"][u1 % 2][:, :, :],
                                            a["inv"][:, u1 % 2, :].unsqueeze(2).to_broadcast([128, NBLK, 128]),
                                            ALU.mult).then_inc(sem("win_normed"), 1)

            def prologue():
                lookahead(-2, W.unroll - 2, -1, False, True, first=True)
                lookahead(-1, W.unroll - 1, -1, True, True)

            def step(n, u, w, scores, project):
                lookahead(n, u, w, scores, project)
                for half in range(2):
                    dve.wait_ge(sem("pv_raw"), W.at("pv_raw", n, half + 1))
                    for hd in range(2):
                        lo = 64 * hd
                        nc.vector.tensor_copy(
                            a["out"][u % 2][lo:lo + 64, 256 * half:256 * half + 256].rearrange("p (j i) -> p j i", j=4),
                            bank[6 + half][lo:lo + 64, :].rearrange("p (j h i) -> p j h i", j=4, h=2)[:, :, hd, :]) \
                          .then_inc(sem("win_pv_read"), 1)
                dve.wait_ge(sem("win_out"), W.at("win_out", n, 1))
                dve.wait_ge(sem("pair_added"), W.at("pair_added", n))
                add(u % B).then_inc(sem("pair_added"), 1)

            win_steps(W, dve, prologue, step)

        def win_pool(pool, W, a):
            def unit(r, par, first):
                pool.wait_ge(sem("win_proj_read"), W.at("win_proj_read", r, 2))
                nc.gpsimd.tensor_tensor(a["part"][0][:, :], a["part"][0][:, :], a["part"][1][:, :], ALU.add) \
                  .then_inc(sem("win_sum"), 1)
                pool.wait_ge(sem("win_proj_read"), W.at("win_proj_read", r, 4))
                nc.gpsimd.tensor_tensor(a["part"][2][:, :], a["part"][2][:, :], a["part"][3][:, :], ALU.add) \
                  .then_inc(sem("win_sum"), 1)
                pool.wait_ge(sem("win_sum"), W.at("win_sum", r, 2))
                pool.wait_ge(sem("win_rs"), W.at("win_rs", r, 2))
                if not first:
                    pool.wait_ge(sem("win_s"), W.at("win_s", r, -2))
                nc.gpsimd.tensor_tensor(a["k"][par][:, PAD:TP], a["part"][2][:, :], a["rs"][:, 1, :], ALU.mult) \
                  .then_inc(sem("win_k"), 1)

            def prologue():
                unit(0, 0, True)
                unit(1, 1, True)

            def step(n, u, w, scores, project):
                if project:
                    unit(n + 2, u % 2, False)

            win_steps(W, pool, prologue, step)

        def win_sp(sp, W, a, w_of, wo_of):
            sp.dma_start(a["w"][:, :, :], w_of(0)).then_inc(sem("win_w_loaded"), 16)
            sp.dma_start(a["wo"][:, :], wo_of(0)).then_inc(sem("win_wo_loaded"), 16)
            with sp.Fori(0, W.units // B - 1) as i:
                sp.wait_ge(sem("win_proj"), W.at("win_proj", i * B + B))
                sp.dma_start(a["w"][:, :, :], w_of(i + 1)).then_inc(sem("win_w_loaded"), 16)
                sp.wait_ge(sem("win_out"), W.at("win_out", i * B + B))
                sp.dma_start(a["wo"][:, :], wo_of(i + 1)).then_inc(sem("win_wo_loaded"), 16)

        next_block()
        kv_k = [tmp_sb(f"kv_k{i}", [128, B, TP]) for i in range(2)]
        kv_v = [tmp_sb(f"kv_v{b}", [128, NBLK, 256]) for b in range(B)]
        kv_w = tmp_sb("kv_w", [C, 2, 256])
        kv_sq = tmp_sb("kv_sq", [128, 2, T])
        kv_log = tmp_sb("kv_log", [128, 2, T])
        kv_rs = tmp_sb("kv_rs", [128, 2, T])
        q_w8 = tmp_sb("q_w8", [128, 1])
        A6 = win_alloc(1, False)
        start = dict({m: 0 for m in PLAIN}, pv_raw=B + 2 * B * PAIRS, pair_added=B + B * PAIRS)
        W6 = Window(PAIRS * B, 2 * B, start, PLAIN, 0, slopes=True)

        def kv_pe(pe):
            pe.wait_ge(sem("h_ready"), 28)
            pe.wait_ge(sem("ln_normed"), 28)
            pe.wait_ge(sem("kv_loaded"), 48)

            def key(j):
                if j >= 2:
                    pe.wait_ge(sem("kv_key"), j - 1)
                pe.matmul(bank[j % 2][:, :], kv_w[:, 0, 128 * (j % 2):128 * (j % 2) + 128], hb(j // 2),
                          start=True, stop=True).then_inc(sem("kv_raw"), 1)

            key(0)
            for j in range(2 * B):
                if j + 1 < 2 * B:
                    key(j + 1)
                for f in (2 * j, 2 * j + 1):
                    if f >= 4:
                        pe.wait_ge(sem("kv_v_read"), f - 3)
                    for i in range(2):
                        blk = 2 * (f % 4) + i
                        last = pe.matmul(bank[4 + f % 4][:, 256 * i:256 * i + 256], hh(f // 4, 64 * blk - 64, 128),
                                         kv_w[:, 1, :], start=True, stop=True)
                    last.then_inc(sem("kv_v_raw"), 1)
                pe.wait_ge(sem("kv_squared"), j + 1)
                if j >= 2:
                    pe.wait_ge(sem("kv_logged"), j - 1)
                pe.matmul(bank[2 + j % 2][:, :], head_sum[:, :], kv_sq[:, j % 2, :], start=True, stop=True) \
                  .then_inc(sem("kv_ssq"), 1)

        def kv_act(act):
            for j in range(2 * B):
                act.wait_ge(sem("kv_raw"), j + 1)
                if j >= 2:
                    act.wait_ge(sem("kv_ssq"), j - 1)
                nc.scalar.activation(kv_sq[:, j % 2, :], bank[j % 2][:, :], ACT.Square).then_inc(sem("kv_squared"), 1)
                for f in (2 * j, 2 * j + 1):
                    act.wait_ge(sem("kv_v_raw"), f + 1)
                    nc.scalar.activation(kv_v[f // 4][:, 2 * (f % 4):2 * (f % 4) + 2, :],
                                         bank[4 + f % 4][:, :].rearrange("p (i c) -> p i c", i=2), ACT.Copy) \
                      .then_inc(sem("kv_v_read"), 1)
                act.wait_ge(sem("kv_ssq"), j + 1)
                nc.scalar.activation(kv_log[:, j % 2, :], bank[2 + j % 2][:, :], ACT.Ln, bias=rms_eps[:, 0:1],
                                     scale=1.0 / 64).then_inc(sem("kv_logged"), 1)
                act.wait_ge(sem("kv_logged"), j + 1)
                if j >= 2:
                    act.wait_ge(sem("kv_key"), j - 1)
                nc.scalar.activation(kv_rs[:, j % 2, :], kv_log[:, j % 2, :], ACT.Exp, scale=-0.5) \
                  .then_inc(sem("kv_rs_ready"), 1)

        def kv_dve(dve):
            link(dve, "dve", nc.vector.tensor_scalar(q_w8[:, :], v("qn_w"), 0.125, None, ALU.mult))
            for i in range(2):
                link(dve, "dve", nc.vector.memset(A6["q"][i][:, :, :], 0.0))
                link(dve, "dve", nc.vector.memset(kv_k[i][:, :, 0:PAD], 0.0))
            for j in range(2 * B):
                dve.wait_ge(sem("kv_rs_ready"), j + 1)
                nc.vector.scalar_tensor_tensor(kv_k[j % 2][:, j // 2, PAD:TP], bank[j % 2][:, :], v("kn_w"),
                                               kv_rs[:, j % 2, :], ALU.mult, ALU.mult).then_inc(sem("kv_key"), 1)
            dve.wait_ge(sem("win_bias_loaded"), 16)

        def alibi_pe(pe):
            pe.wait_ge(sem("kv_key"), 2 * B)
            pe.wait_ge(sem("kv_v_read"), 4 * B)
            win_pe(pe, W6, A6, tokens=lambda b, lo, n: hh(b, lo, n),
                   keys_of=lambda u, j: kv_k[u // B][:, u % B, 64 * j:64 * j + 128],
                   values_of=lambda u, j: kv_v[u % B][:, j, 128 * (u // B):128 * (u // B) + 128])

        def alibi_dve(dve):
            win_dve(dve, W6, A6, [q_w8[:, 0:1]],
                    lambda b: nc.vector.scalar_tensor_tensor(x[:, b, :], bank[1][:, :], gate(6, b), x[:, b, :],
                                                             ALU.mult, ALU.add))

        def alibi_sp(sp):
            sp.wait_ge(sem("h_ready"), 25)
            sp.dma_start(kv_w[:, 0, :], d["kv_w"][:, 0, :]).then_inc(sem("kv_loaded"), 16)
            sp.dma_start(kv_w[:, 1, :], d["kv_w"][:, 1, :]).then_inc(sem("kv_loaded"), 16)
            sp.dma_start(A6["bias"][:, :, :], d["alibi_rel"]).then_inc(sem("win_bias_loaded"), 16)

            def one(name, i):
                return d[name][i, :, :] if isinstance(i, int) else \
                    d[name][bass.ds(i, 1), :, :].rearrange("o p n -> (o p) n")

            win_sp(sp, W6, A6, lambda i: one("alibi_wq", i).rearrange("p (j n) -> p j n", j=1),
                   lambda i: one("alibi_wo", i))

        next_block()
        shifted = tmp_sb("shifted", [C, B, TP])
        A7 = win_alloc(5, True)
        qk_tab = tmp_sb("qk_tab", [128, 4, T])
        w1 = tmp_sb("w1", [C, 2, 2 * HID])
        w2 = tmp_sb("w2", [128, 2, 3, C])
        mlp_gelu = [tmp_sb(f"mlp_gelu{i}", [128, T]) for i in range(2)]
        mlp_hid = A7["part"][0:3]
        mlp_in = [A7["v"][b][:, :, :].rearrange("p j c -> p (j c)")[:, 0:T] for b in range(B)]
        layers = []
        for l in range(2):
            layers.append(Window(4 * B, B, (layers[-1] if l else W6).after(), ROTATED, PAIRS + 4 * l, tables=qk_tab))

        def shift_dve(dve, l, sub):
            if sub:
                dve.wait_ge(sem("pair_added"), layers[l].after()["pair_added"])
            for b in range(B):
                if l == 0 and sub == 0:
                    dve.wait_ge(sem("h_ready"), 28 + b + 1)
                lo, hi = shifted[0:64, b, PAD:TP], shifted[64:128, b, PAD:TP]
                nc.vector.tensor_copy(lo, h[0:64, b, PAD:TP])
                nc.vector.tensor_copy(hi, h[64:128, b, PAD - 1:TP - 1]).then_inc(sem("shifted"), 1)

        def local_pe(pe, l):
            pe.wait_ge(sem("shifted"), 8 * l + B)
            if l == 0:
                pe.wait_ge(sem("ln_normed"), 32)
                pe.wait_ge(sem("local_cleared"), 5)
            win_pe(pe, layers[l], A7, tokens=lambda b, lo, n: shifted[:, b, PAD + lo:PAD + lo + n],
                   keys_of=lambda u, j: A7["k"][u % 2][:, 64 * j:64 * j + 128],
                   values_of=lambda u, j: A7["v"][u][:, j, :])

        def local_dve(dve, l):
            win_dve(dve, layers[l], A7, [v("q_scale", l), v("q_scale_rot", l), v("k_scale", l), v("k_scale_rot", l)],
                    lambda b: nc.vector.tensor_tensor(hb(b), hb(b), bank[1][:, :], ALU.add))

        def clear_dve(dve):
            nc.vector.memset(shifted[:, :, 0:PAD], 0.0).then_inc(sem("local_cleared"), 1)
            for i in range(2):
                nc.vector.memset(A7["q"][i][:, :, :], 0.0).then_inc(sem("local_cleared"), 1)
                nc.vector.memset(A7["k"][i][:, 0:PAD], 0.0).then_inc(sem("local_cleared"), 1)
            dve.wait_ge(sem("local_cleared"), 5)
            dve.wait_ge(sem("win_bias_loaded"), 32)
            dve.wait_ge(sem("local_loaded"), 48)

        def local_sp(sp):
            sp.wait_ge(sem("h_ready"), 29)
            sp.dma_start(A7["bias"][:, :, :], d["local_mask"]).then_inc(sem("win_bias_loaded"), 16)
            sp.dma_start(qk_tab[:, :, :], d["qk_tab"]).then_inc(sem("local_loaded"), 16)
            sp.dma_start(w1[:, :, :], d["local_w1"]).then_inc(sem("local_loaded"), 16)
            sp.dma_start(w2[:, :, :, :], d["local_w2"]).then_inc(sem("local_loaded"), 16)

            def one(name, l, i):
                return d[name][l, i, :, :] if isinstance(i, int) else \
                    d[name][l, bass.ds(i, 1), :, :].rearrange("o p n -> (o p) n")

            for l in range(2):
                if l:
                    sp.wait_ge(sem("win_out"), layers[0].after()["win_out"])
                win_sp(sp, layers[l], A7, lambda i: one("local_w", l, i).rearrange("p (j n) -> p j n", j=5),
                       lambda i: one("local_wo", l, i))

        def mlp_pe(pe, l):
            pe.wait_ge(sem("local_loaded"), 48)
            pe.wait_ge(sem("ln_normed"), 4 * (9 + l))

            def up(b):
                pe.wait_ge(sem("h_ready"), 4 * (8 + l) + b + 1)
                for c in range(3):
                    f = 12 * l + 3 * b + c
                    n = min(128, HID - 128 * c)
                    if f - 12 * l >= 2:
                        pe.wait_ge(sem("mlp_hidden"), f - 1)
                    for half in range(2):
                        lo = HID * half + 128 * c
                        last = pe.matmul(bank[4 + 2 * (f % 2) + half][0:n, :], w1[:, l, lo:lo + n], mlp_in[b],
                                         start=True, stop=True)
                    last.then_inc(sem("up_raw"), 1)

            def down(b):
                for c in range(3):
                    n = min(128, HID - 128 * c)
                    pe.wait_ge(sem("mlp_hidden"), 12 * l + 3 * b + c + 1)
                    last = pe.matmul(bank[b][:, :], w2[0:n, l, c, :], mlp_hid[c][0:n, :],
                                     start=(c == 0), stop=(c == 2))
                    last.then_inc(sem("mlp_hid_read"), 1)

            for b in range(B):
                up(b)
                down(b)

        def mlp_act(act, l):
            for f in range(12 * l, 12 * l + 12):
                c = f % 3
                n = min(128, HID - 128 * c)
                act.wait_ge(sem("up_raw"), FB * B + f + 1)
                if f >= 2:
                    act.wait_ge(sem("mlp_hidden"), f - 1)
                nc.scalar.activation(mlp_gelu[f % 2][0:n, :], bank[5 + 2 * (f % 2)][0:n, :], ACT.Gelu,
                                     bias=v("b1g", 3 * l + c)[0:n, :]).then_inc(sem("up_acted"), 1)

        def mlp_dve(dve, l):
            for b in range(B):
                for c in range(3):
                    f = 12 * l + 3 * b + c
                    n = min(128, HID - 128 * c)
                    dve.wait_ge(sem("up_acted"), FB * B + f + 1)
                    if b:
                        dve.wait_ge(sem("mlp_hid_read"), f - 2)
                    nc.vector.scalar_tensor_tensor(mlp_hid[c][0:n, :], bank[4 + 2 * (f % 2)][0:n, :],
                                                   v("b1a", 3 * l + c)[0:n, :], mlp_gelu[f % 2][0:n, :],
                                                   ALU.add, ALU.mult).then_inc(sem("mlp_hidden"), 1)
                dve.wait_ge(sem("mlp_hid_read"), 12 * l + 3 * b + 3)
                link(dve, "dve", nc.vector.scalar_tensor_tensor(hb(b), bank[b][:, :], v("b2", l), hb(b),
                                                                ALU.add, ALU.add))

        def final_dve(dve):
            for b in range(B):
                nc.vector.scalar_tensor_tensor(x[:, b, :], hb(b), gate(7, b), x[:, b, :], ALU.mult, ALU.add) \
                  .then_inc(sem("x_ready"), 1)

        @block.sync
        def _(sp):
            sp.dma_start(cond[:, :], d["cond"]).then_inc(sem("cond_loaded"), 16)
            for b in range(B):
                sp.dma_start(x[:, b, :], d["x"][:, b, :]).then_inc(sem(f"x_loaded{b}"), 16)
                if b == 0:
                    sp.dma_start(centre[:, :], d["centre"]).then_inc(sem("consts"), 16)
                    sp.dma_start(mean[:, :], d["mean"]).then_inc(sem("consts"), 16)
                    sp.dma_start(ident[:, :], d["ident"]).then_inc(sem("consts"), 16)
                    sp.dma_start(vec[:, :], d["vec"]).then_inc(sem("consts"), 16)
                    sp.dma_start(conv_w[:, :], d["conv_w"]).then_inc(sem("consts"), 16)
            sp.dma_start(wmod[:, :, :], d["wmod"]).then_inc(sem("wmod_loaded"), 16)
            for p in range(2):
                sp.dma_start(conv_bias[64 * p:64 * p + 64, :, :],
                             d["conv_bias"][p:p + 1, :, :].to_broadcast([64, 16, K])).then_inc(sem("conv_tables"), 16)
            sp.dma_start(conv_mask[:, :, :], d["conv_mask"]).then_inc(sem("conv_tables"), 16)
            sp.dma_start(conv_edge[:, :], d["conv_edge"]).then_inc(sem("conv_tables"), 16)
            sp.dma_start(head_sum[:, :], d["head_sum"]).then_inc(sem("kv_loaded"), 16)
            sp.dma_start(lr_u1[:, :], d["lr_u1"]).then_inc(sem("early_loaded"), 16)
            sp.dma_start(lr_v1[:, :], d["lr_v1"]).then_inc(sem("early_loaded"), 16)
            sp.dma_start(lr_u2[:, :, :], d["lr_u2"]).then_inc(sem("early_loaded"), 16)
            sp.dma_start(lr_v2[:, :], d["lr_v2"]).then_inc(sem("early_loaded"), 16)
            sp.dma_start(scan_w[:, :, :], d["scan_w"]).then_inc(sem("early_loaded"), 16)
            moe_sp(sp)
            att_sp(sp)
            mix_sp(sp)
            alibi_sp(sp)
            local_sp(sp)
            for b in range(B):
                sp.wait_ge(sem("x_ready"), LAST + b + 1)
                sp.dma_start(out[:, b, :], x[:, b, :]).then_inc(sem("stored"), 16)
            sp.wait_ge(sem("stored"), 16 * B)

        @block.gpsimd
        def _(pool):
            nc.gpsimd.memset(rms_eps[:, :], 0.01)
            nc.gpsimd.memset(ln_clip[:, :], 15.0 * LN2)
            nc.gpsimd.memset(eps_col[:, :], EPS).then_inc(sem("filled"), 1)
            nc.gpsimd.memset(zeros[:, :], 0.0).then_inc(sem("filled"), 1)
            nc.gpsimd.memset(h[:, :, 0:PAD], 0.0)
            ln_pool(pool, 0)
            ln_pool(pool, 1)
            ln_pool(pool, 2)
            scan_pool(pool)
            ln_pool(pool, 3)
            moe_pool(pool)
            ln_pool(pool, 4)
            att_pool(pool)
            ln_pool(pool, 5)
            ln_pool(pool, 6)
            ln_pool(pool, 7)
            for l in range(2):
                win_pool(pool, layers[l], A7)
                ln_pool(pool, 8 + l)

        @block.scalar
        def _(act):
            mod_act(act)
            ln_act(act, 0)
            conv_act(act)
            act.wait_ge(sem("consts"), 80)
            ln_act(act, 1)
            lr_act(act)
            ln_act(act, 2)
            scan_act(act)
            ln_act(act, 3)
            moe_act_engine(act)
            ln_act(act, 4)
            att_act(act)
            ln_act(act, 5)
            mix_act(act)
            ln_act(act, 6)
            kv_act(act)
            win_act(act, W6, A6)
            ln_act(act, 7)
            for l in range(2):
                win_act(act, layers[l], A7)
                ln_act(act, 8 + l)
                mlp_act(act, l)

        @block.vector
        def _(dve):
            mod_dve(dve)
            ln_dve(dve, 0)
            conv_dve(dve)
            dve.wait_ge(sem("consts"), 80)
            ln_dve(dve, 1)
            lr_dve(dve)
            ln_dve(dve, 2)
            scan_dve(dve)
            ln_dve(dve, 3)
            moe_dve(dve)
            ln_dve(dve, 4)
            att_dve(dve)
            ln_dve(dve, 5)
            mix_dve(dve)
            ln_dve(dve, 6)
            kv_dve(dve)
            alibi_dve(dve)
            ln_dve(dve, 7)
            clear_dve(dve)
            for l in range(2):
                shift_dve(dve, l, 0)
                local_dve(dve, l)
                shift_dve(dve, l, 1)
                ln_dve(dve, 8 + l)
                mlp_dve(dve, l)
            final_dve(dve)

        @block.tensor
        def _(pe):
            pe.wait_ge(sem("consts"), 80)
            mod_pe(pe)
            ln_pe(pe, 0)
            conv_pe(pe)
            ln_pe(pe, 1, after_all=True)
            lr_pe(pe)
            ln_pe(pe, 2)
            scan_pe(pe)
            ln_pe(pe, 3, after_all=True)
            moe_pe(pe)
            ln_pe(pe, 4, after_all=True)
            att_pe(pe)
            ln_pe(pe, 5)
            mix_pe(pe)
            ln_pe(pe, 6)
            kv_pe(pe)
            alibi_pe(pe)
            ln_pe(pe, 7, after_all=True)
            for l in range(2):
                local_pe(pe, l)
                ln_pe(pe, 8 + l, after_all=True)
                mlp_pe(pe, l)


def _layouts(a):
    f = np.float32
    d = {"x": a["L0_attn_x"].transpose(2, 0, 1)}
    d["cond"] = np.concatenate([a[f"L{i}_c"] for i in range(4)], 0).T
    d["wmod"] = np.stack([a[f"L{i}_wmod"] for i in range(4)], 1)
    d["ident"] = np.eye(128, dtype=f)
    d["centre"] = (np.eye(C) - 1.0 / C).astype(f)
    d["mean"] = np.full((C, C), 1.0 / C, f)
    vec = np.zeros((128, NVEC), f)

    def put(name, *cols):
        for i, col in enumerate(cols):
            vec[:len(col), VEC[name][0] + i] = col

    put("ffn0_b1", *a["L0_ffn_b1"].reshape(4, 128))
    put("ffn0_b2", a["L0_ffn_b2"])
    for n in ("ba", "bb", "bc"):
        put("scan_" + n, a["L1_attn_" + n])
    put("r1_b", a["L1_ffn_r1_b"])
    put("attn2_bo", a["L2_attn_bo"])
    put("mu_r", a["L2_ffn_mu_r"])
    put("mu_k", a["L2_ffn_mu_k"])
    put("qn_w", np.tile(a["L3_attn_q_norm_w"], 2))
    put("kn_w", np.tile(a["L3_attn_k_norm_w"], 2))
    half = np.concatenate([np.arange(32, 64), np.arange(32)])
    for l in range(2):
        for n in ("q_scale", "k_scale"):
            s = a["L3_ffn_" + n][l]
            vec[:, VEC[n][0] + l] = np.tile(s, 2)
            vec[:, VEC[n + "_rot"][0] + l] = np.tile(s[half], 2)
    put("ln_g", *a["L3_ffn_ln_g"])
    put("ln_b", *a["L3_ffn_ln_b"])
    put("b2", *a["L3_ffn_b2"])
    for l in range(2):
        for j in range(3):
            n = min(128, HID - 128 * j)
            vec[:n, VEC["b1a"][0] + 3 * l + j] = a["L3_ffn_b1"][l, 128 * j:128 * j + n]
            vec[:n, VEC["b1g"][0] + 3 * l + j] = a["L3_ffn_b1"][l, HID + 128 * j:HID + 128 * j + n]
    for p in range(8):
        vec[:, VEC["slope"][0] + p] = np.repeat(2.0 ** (-0.5 * (2 * p + 1 + np.arange(2))), 64)
    d["vec"] = vec
    j = np.arange(32)
    d["conv_w"] = a["L0_attn_W"].T[:, np.tile(j, 2)]
    res = np.arange(32).reshape(16, 2).T
    d["conv_bias"] = a["L0_attn_b"][(j[None, None, :] - res[:, :, None]) % 32]
    s = np.arange(128)[:, None, None] - 32 * np.arange(4)[None, :, None] - j[None, None, :]
    d["conv_mask"] = ((s >= 0) & (s < 32)).astype(f)
    d["conv_edge"] = (j[:, None] < j[None, :]).astype(f)
    d["lr_u1"], d["lr_v1"], d["lr_v2"] = a["L0_ffn_U1"], a["L0_ffn_V1"], a["L0_ffn_V2"]
    d["lr_u2"] = a["L0_ffn_U2"].reshape(4, 128, 32).transpose(1, 0, 2)
    d["scan_w"] = np.stack([a["L1_attn_W" + n].T for n in "abc"], 1)
    r1 = a["L1_ffn_r1_w"].T
    d["r1_c"], d["r1_s"], d["r2_w"] = r1[:C], r1[C:], a["L1_ffn_r2_w"].T
    d["iota_e"] = np.tile(np.arange(32, dtype=f), (128, 1))
    p = np.arange(128)
    d["chunk_sum"] = ((p[:, None] % 32 == p[None, :] % 32) & (p[:, None] // 32 < p[None, :] // 32)).astype(f)
    up = a["L1_ffn_w_up"].transpose(0, 2, 1).reshape(16, 2, C, 512).transpose(0, 2, 1, 3).reshape(16, C, 1024)
    down = a["L1_ffn_w_down"].transpose(0, 2, 1).reshape(16, 2, 2, 128, C).transpose(0, 3, 1, 2, 4).reshape(16, 128, 512)
    d["moe_w"] = np.concatenate([up, down, a["L1_ffn_a_up"].transpose(0, 2, 1), a["L1_ffn_a_down"].transpose(0, 2, 1)], 2)
    def pairs(w):
        return w.reshape(C, 8, 128).transpose(1, 0, 2)

    swap = np.arange(128) ^ 1
    q, k = pairs(a["L2_attn_Wq"]), pairs(a["L2_attn_Wk"])
    d["att_w"] = np.stack([q, q[:, :, swap], k, k[:, :, swap], pairs(a["L2_attn_Wv"])], 2)
    d["att_wo"] = a["L2_attn_Wo"].reshape(8, 128, C)
    inv = (1.0 / (np.float32(10000.0) ** (np.arange(0, 64, 2, dtype=f) / f(64)))).astype(f)
    ang = (np.arange(T, dtype=f)[None, :] * inv[:, None]).astype(f).astype(np.float64)
    cos, sin = (np.tile(np.repeat(t(ang), 2, 0), (2, 1)) for t in (np.cos, np.sin))
    sin = sin * np.where(np.arange(128) % 2 == 0, -1.0, 1.0)[:, None]
    d["rope_tab"] = np.stack([cos / 8, sin / 8, cos, sin], 1).astype(f)
    i64 = np.arange(128) % 64
    d["att_mask"] = np.where(np.arange(64)[None, :] <= i64[:, None], 0.0, -1e30).astype(f)
    d["mix_w"] = np.stack([a["L2_ffn_W_" + n].T for n in "rkv"], 1)
    d["head_sum"] = (p[:, None] // 64 == p[None, :] // 64).astype(f)
    d["kv_w"] = np.stack([a["L3_attn_wk"].T, a["L3_attn_wv"].T], 1)
    d["alibi_wq"] = pairs(a["L3_attn_wq"].T)
    d["alibi_wo"] = a["L3_attn_wo"].T.reshape(8, 128, C)
    qi, kj = i64[:, None, None], np.arange(128)[None, None, :]
    rel = kj - 64 - qi + 0 * np.arange(8)[None, :, None]
    there = (kj >= 64) | (np.arange(8)[None, :, None] > 0)
    d["alibi_rel"] = np.where((rel <= 0) & (rel >= -16) & there, rel, -1e30).astype(f)
    d["local_mask"] = np.where((rel <= 0) & (rel >= -64) & there, 0.0, -1e30).astype(f)
    w = a["L3_ffn_wqkv"].reshape(2, C, 3, 4, 128).transpose(2, 0, 3, 1, 4)
    rot = np.concatenate([half, 64 + half])
    d["local_w"] = np.stack([w[0], w[0][..., rot], w[1], w[1][..., rot], w[2]], 3).reshape(2, 4, C, 640)
    d["local_wo"] = a["L3_ffn_wo"].reshape(2, 4, 128, C)
    d["local_w1"] = a["L3_ffn_w1"].transpose(1, 0, 2)
    w2 = np.zeros((128, 2, 3, C), f)
    for j in range(3):
        n = min(128, HID - 128 * j)
        w2[:n, :, j, :] = a["L3_ffn_w2"][:, 128 * j:128 * j + n, :].transpose(1, 0, 2)
    d["local_w2"] = w2
    idx = np.arange(0, 64, 2, dtype=f)
    t = np.arange(T, dtype=f)
    ang = (t[None, :] * inv[:, None]).astype(f).astype(np.float64)
    base = ((idx + f(0.4 * 64)) / f(1.4 * 64)).astype(np.float64)
    sc = base[:, None] ** ((t[None, :].astype(np.float64) - T // 2) / 32.0)
    cos, sin = np.tile(np.cos(ang), (4, 1)), np.tile(np.sin(ang), (4, 1))
    sc = np.tile(sc, (4, 1))
    sin = sin * np.where(p % 64 < 32, -1.0, 1.0)[:, None]
    d["qk_tab"] = np.stack([8 * cos * sc, 8 * sin * sc, cos / sc, sin / sc], 1).astype(f)
    return d


def kernel(**inputs):
    import concourse.bacc as _bacc
    from concourse.bass_utils import run_bass_kernel_spmd as _run

    nc = _bacc.Bacc("TRN2", target_bir_lowering=False, num_devices=1)
    arrays, aps = {}, {}
    for name, a in _layouts({k: np.asarray(val) for k, val in inputs.items()}).items():
        a = np.ascontiguousarray(a)
        arrays["in_" + name] = a
        aps[name] = nc.dram_tensor("in_" + name, a.shape, mybir.dt.from_np(a.dtype), kind="ExternalInput").ap()
    out = nc.dram_tensor("out_x", (C, B, T), F32, kind="ExternalOutput").ap()
    adaln_blocks(nc, aps, out)
    r = _run(nc, [arrays], core_ids=[0])
    return np.ascontiguousarray(r.results[0]["out_x"].transpose(1, 2, 0))
```

```python
from contextlib import ExitStack

import numpy as np

import concourse.bass as bass
from concourse import mybir

F32 = mybir.dt.float32
U32 = mybir.dt.uint32
ALU = mybir.AluOpType
ACT = mybir.ActivationFunctionType
AX_X = mybir.AxisListType.X

C = 128
B = 4
T = 512
N = B * T
PAD = 64
TP = PAD + T
TILES = N // 128
TB = T // 128
EPS = 1e-5
LN2 = 0.6931471805599453

K = 32
R = 32
FB = 4
E = 32
CAP = int(1.25 * N / E)
G = 16
SLOTS = E * CAP
DUMP = SLOTS
ROUNDS = CAP // 8
WG = 2 * 512 + 2 * 256 + 256 + 128
NB128 = SLOTS // 128

NBLK = T // 64
PAIRS = 8
UNROLL = 8
SWAP = [i ^ 1 for i in range(32)]
GROUPS = [[7], [6, 0], [5, 1], [4, 2], [3]]
GCUM = [1, 3, 5, 7, 8]
PCH = [j // 2 + 1 for j in range(NBLK)]
POFF = [128 * sum(PCH[:j]) for j in range(NBLK)]
PW = 128 * sum(PCH)
CHUNKS = [(jc, j) for jc in range(TB) for j in range(NBLK) if j // 2 >= jc]
NFILL = len(CHUNKS) // 4

HID = int(C * 4 * 2 / 3)

VEC = {}
for _name, _n in (("ffn0_b1", 4), ("ffn0_b2", 1), ("scan_ba", 1), ("scan_bb", 1), ("scan_bc", 1),
                  ("r1_b", 1), ("attn2_bo", 1), ("mu_r", 1), ("mu_k", 1), ("qn_w", 1), ("kn_w", 1),
                  ("q_scale", 2), ("k_scale", 2), ("q_scale_rot", 2), ("k_scale_rot", 2),
                  ("ln_g", 2), ("ln_b", 2), ("b2", 2), ("b1a", 6), ("b1g", 6), ("slope", 8)):
    VEC[_name] = (sum(n for _, n in VEC.values()), _n)
NVEC = sum(n for _, n in VEC.values())


def adaln_blocks(nc, d, out):
    ctx = ExitStack()
    with ctx:
        def sb(name, shape, dt=F32):
            return ctx.enter_context(nc.sbuf_tensor(name, shape, dt))

        scope = [ExitStack()]

        def tmp_sb(name, shape, dt=F32):
            return scope[0].enter_context(nc.sbuf_tensor(name, shape, dt))

        def next_block():
            scope[0].close()
            scope[0] = ExitStack()

        sems = {}

        def sem(name):
            if name not in sems:
                sems[name] = ctx.enter_context(nc.semaphore(name))
            return sems[name]

        bank = [ctx.enter_context(nc.psum_tensor(f"bank{i}", [128, 512], F32)) for i in range(8)]

        x = sb("x", [C, B, T])
        h = sb("h", [C, B, TP])
        ident = sb("ident", [128, 128])
        centre = sb("centre", [128, 128])
        mean = sb("mean", [128, 128])
        vec = sb("vec", [128, NVEC])
        cond = sb("cond", [C, 16])
        cond_silu = sb("cond_silu", [C, 16])
        mod = sb("mod", [C, 4, 6, B])
        
        gate_sign = sb("gate_sign", [C, 4, 2, B])
        gate_abs = sb("gate_abs", [C, 4, 2, B])
        eps_col = sb("eps_col", [128, 1])
        rms_eps = sb("rms_eps", [128, 1])
        ln_clip = sb("ln_clip", [128, 1])
        head_sum = sb("head_sum", [128, 128])
        ln_square = sb("ln_square", [C, 2, T])
        ln_log = sb("ln_log", [C, 2, T])
        ln_rstd = sb("ln_rstd", [C, 2, T])
        ln_norm = sb("ln_norm", [C, 2, T])

        lr_u1 = sb("lr_u1", [C, R])
        lr_v1 = sb("lr_v1", [R, FB * 128])
        lr_u2 = sb("lr_u2", [128, FB, R])
        lr_v2 = sb("lr_v2", [R, C])
        scan_w = sb("scan_w", [C, 3, C])
        moe_w = [sb(f"moe_w{u}", [128, WG]) for u in range(2)]
        r1_c = sb("r1_c", [C, 64])
        r1_s = sb("r1_s", [6, 64])
        r2_w = sb("r2_w", [64, E])
        iota_e = sb("iota_e", [128, E])
        chunk_sum = sb("chunk_sum", [128, 128])
        zeros = sb("zeros", [128, 4 * C])
        htok = sb("htok", [128, TILES, C])

        ctx.callback(lambda: scope[0].close())

        def v(name, i=0):
            at, n = VEC[name]
            assert i < n
            return vec[:, at + i:at + i + 1]

        def gate(k, b):
            return mod[:, k // 2, 3 * (k % 2) + 2, b:b + 1]

        def scale1(k, b):
            return mod[:, k // 2, 3 * (k % 2) + 1, b:b + 1]

        def shift(k, b):
            return mod[:, k // 2, 3 * (k % 2), b:b + 1]

        def hb(b):
            return h[:, b, PAD:TP]

        def hh(b, lo, n):
            return h[:, b, PAD + lo:PAD + lo + n]

        steps = {"dve": 0, "act": 0, "pool": 0}

        def link(eng, name, ins):
            steps[name] += 1
            ins.then_inc(sem(name + "_step"), 1)
            eng.wait_ge(sem(name + "_step"), steps[name])

        LAST = 4 * 5
        block = ctx.enter_context(nc.Block())

        def x_written(k):
            if k == 4:
                return "pair_added", B * PAIRS
            if k == 6:
                return "pair_added", 2 * B * PAIRS
            return "x_ready", 4 * (k if k < 4 else k - 1)

        def ln_pe(pe, k, after_all=False):
            def centred(b):
                n = 4 * k + b
                src = x[:, b, :]
                if k == 0:
                    pe.wait_ge(sem(f"x_loaded{b}"), 16)
                else:
                    name, base = ("shifted", 8 * (k - 8) + 4) if k >= 8 else x_written(k - 1)
                    pe.wait_ge(sem(name), base + (B if after_all else b + 1))
                if k >= 8:
                    src = shifted[:, b, PAD:TP]
                if n >= 2:
                    pe.wait_ge(sem("ln_normed"), n - 1)
                pe.matmul(bank[n % 2][:, :], centre[:, :], src, start=True, stop=True) \
                  .then_inc(sem("ln_centred"), 1)

            def variance(b):
                n = 4 * k + b
                pe.wait_ge(sem("ln_squared"), n + 1)
                pe.matmul(bank[2 + n % 2][:, :], mean[:, :], ln_square[:, n % 2, :], start=True, stop=True) \
                  .then_inc(sem("ln_variance"), 1)

            centred(0)
            for b in range(B):
                if b + 1 < B:
                    centred(b + 1)
                variance(b)

        def ln_act(act, k):
            nc.scalar.preload_act_table_set("natural_log_exp_and_others")
            for b in range(B):
                n = 4 * k + b
                act.wait_ge(sem("ln_centred"), n + 1)
                if n >= 2:
                    act.wait_ge(sem("ln_variance"), n - 1)
                nc.scalar.activation(ln_square[:, n % 2, :], bank[n % 2][:, :], ACT.Square) \
                  .then_inc(sem("ln_squared"), 1)
                act.wait_ge(sem("ln_variance"), n + 1)
                if n == 0:
                    act.wait_ge(sem("filled"), 1)
                nc.scalar.activation(ln_log[:, n % 2, :], bank[2 + n % 2][:, :], ACT.Ln,
                                     bias=eps_col[:, 0:1]).then_inc(sem("ln_log"), 1)
                act.wait_ge(sem("ln_log"), n + 1)
                if n >= 2:
                    act.wait_ge(sem("ln_normed"), n - 1)
                nc.scalar.activation(ln_rstd[:, n % 2, :], ln_log[:, n % 2, :], ACT.Exp, scale=-0.5) \
                  .then_inc(sem("ln_rstd"), 1)

        def ln_dve(dve, k):
            for b in range(B):
                n = 4 * k + b
                dve.wait_ge(sem("ln_rstd"), n + 1)
                if n >= 2:
                    dve.wait_ge(sem("h_ready"), n - 1)
                nc.vector.tensor_tensor(ln_norm[:, n % 2, :], bank[n % 2][:, :], ln_rstd[:, n % 2, :],
                                        ALU.mult).then_inc(sem("ln_normed"), 1)

        def ln_pool(pool, k):
            for b in range(B):
                n = 4 * k + b
                if k == 0 and b == 0:
                    pool.wait_ge(sem("mod_ready"), 4)
                pool.wait_ge(sem("ln_normed"), n + 1)
                dst = conv_h[:, T * b:T * b + T] if k == 0 else hb(b)
                scale, bias = (scale1(k, b), shift(k, b)) if k < 8 else (v("ln_g", k - 8), v("ln_b", k - 8))
                if k >= 8:
                    dst = mlp_in[b]
                nc.gpsimd.tensor_scalar(dst, ln_norm[:, n % 2, :], scale, bias,
                                        ALU.mult, ALU.add).then_inc(sem("h_ready"), 1)

        def mod_act(act):
            act.wait_ge(sem("cond_loaded"), 16)
            nc.scalar.activation(cond_silu[:, :], cond[:, :], ACT.Silu).then_inc(sem("cond_ready"), 1)

        def mod_pe(pe):
            pe.wait_ge(sem("cond_ready"), 1)
            pe.wait_ge(sem("wmod_loaded"), 16)
            for l in range(4):
                for j in range(6):
                    at = (6 * l + j) * B
                    last = pe.matmul(bank[7][:, at:at + B], wmod[:, l, j * C:(j + 1) * C],
                                     cond_silu[:, B * l:B * l + B], start=True, stop=True)
            last.then_inc(sem("mod_raw"), 1)

        def mod_dve(dve):
            dve.wait_ge(sem("mod_raw"), 1)
            raw = bank[7][:, 0:96].rearrange("p (l j b) -> p l j b", l=4, j=6)
            for i in range(2):
                s, c, g = (mod[:, :, 3 * i + j, :] for j in range(3))
                nc.vector.tensor_copy(s, raw[:, :, 3 * i, :]).then_inc(sem("mod_ready"), 1)
                nc.vector.tensor_scalar(c, raw[:, :, 3 * i + 1, :], 1.0, None, ALU.add) \
                  .then_inc(sem("mod_ready"), 1)
                r = raw[:, :, 3 * i + 2, :]
                link(dve, "dve", nc.vector.tensor_scalar(gate_sign[:, :, i, :], r, 0.0, 2.0, ALU.is_ge, ALU.mult))
                link(dve, "dve", nc.vector.tensor_scalar(gate_abs[:, :, i, :], r, -1.0, None, ALU.mult))
                link(dve, "dve", nc.vector.tensor_tensor(gate_abs[:, :, i, :], gate_abs[:, :, i, :], r, ALU.max))
                link(dve, "dve", nc.vector.tensor_scalar(gate_abs[:, :, i, :], gate_abs[:, :, i, :], 0.25, None,
                                                         ALU.max))
                link(dve, "dve", nc.vector.scalar_tensor_tensor(g, gate_sign[:, :, i, :], -1.0,
                                                                gate_abs[:, :, i, :], ALU.add, ALU.mult))

        wmod = tmp_sb("wmod", [C, 4, 6 * C])
        conv_h = tmp_sb("conv_h", [C, N])
        conv_w = tmp_sb("conv_w", [C, 2 * K])
        conv_bias = tmp_sb("conv_bias", [128, 16, K])
        conv_mask = tmp_sb("conv_mask", [128, TB, K])
        conv_edge = tmp_sb("conv_edge", [K, K])
        logit = tmp_sb("logit", [128, 16, K])
        row_max = tmp_sb("row_max", [128, 16])
        row_sum = tmp_sb("row_sum", [128, 16])
        row_inv = tmp_sb("row_inv", [128, 16])
        prob4 = tmp_sb("prob4", [128, 16, 4, K])
        band = tmp_sb("band", [128, TILES, 128])
        edge = tmp_sb("edge", [K, TILES, K])

        def htok_pe(pe, banks, tokens):
            for b in range(B):
                for i in range(TB):
                    last = pe.transpose(banks[b][:, 128 * i:128 * i + 128], tokens(b, i), ident[:, :])
                last.then_inc(sem("htok_raw"), 1)

        def conv_pe(pe):
            pe.wait_ge(sem("h_ready"), 4)
            for r in range(K):
                half = 64 * (r % 2)
                last = pe.matmul(bank[4][half:half + 64, K * (r // 2):K * (r // 2) + K],
                                 conv_h[:, r:N:K], conv_w[:, K - r:2 * K - r], start=True, stop=True)
            last.then_inc(sem("conv_logits"), 1)
            pe.wait_ge(sem("ln_normed"), 4)
            htok_pe(pe, bank[0:4], lambda b, i: conv_h[:, T * b + 128 * i:T * b + 128 * i + 128])
            pe.wait_ge(sem("conv_prob"), 1)
            for g in range(4):
                for i in range(4):
                    last = pe.transpose(bank[4 + g][:, 128 * i:128 * i + 128],
                                        prob4[:, 4 * g + i, :, :].rearrange("p a b -> p (a b)"), ident[:, :])
                last.then_inc(sem("conv_probT"), 1)
            pe.wait_ge(sem("conv_band"), 8)
            for b in range(B):
                pe.wait_ge(sem("htok_ready"), b + 1)
                if b + 1 < B:
                    pe.wait_ge(sem("htok_ready"), b + 2)
                for i in range(TB):
                    t = TB * b + i
                    last = pe.matmul(bank[b][:, 128 * i:128 * i + 128], htok[:, t, :], band[:, t, :],
                                     start=True, stop=(i == TB - 1))
                    if i < TB - 1:
                        last = pe.matmul(bank[b][:, 128 * i + 96:128 * i + 128], htok[0:K, t + 1, :],
                                         edge[:, t, :], start=False, stop=True)
                last.then_inc(sem("pv_raw"), 1)

        def htok_act(act, base):
            for b in range(B):
                act.wait_ge(sem("htok_raw"), base + b + 1)
                nc.scalar.activation(htok[:, TB * b:TB * b + TB, :],
                                     bank[b][:, :].rearrange("p (i c) -> p i c", i=TB), ACT.Copy) \
                  .then_inc(sem("htok_ready"), 1)

        def conv_act(act):
            act.wait_ge(sem("conv_shifted"), 1)
            nc.scalar.activation(logit[:, :, :], logit[:, :, :], ACT.Exp).then_inc(sem("conv_exp"), 1)
            htok_act(act, 0)

        def conv_dve(dve):
            dve.wait_ge(sem("conv_logits"), 1)
            dve.wait_ge(sem("conv_tables"), 64)
            link(dve, "dve", nc.vector.tensor_tensor(
                logit[:, :, :], bank[4][:, :].rearrange("p (r j) -> p r j", j=K), conv_bias[:, :, :], ALU.add))
            link(dve, "dve", nc.vector.tensor_reduce(row_max[:, :], logit[:, :, :], AX_X, ALU.max))
            nc.vector.tensor_tensor(logit[:, :, :], logit[:, :, :],
                                    row_max[:, :].unsqueeze(2).to_broadcast([128, 16, K]), ALU.subtract) \
              .then_inc(sem("conv_shifted"), 1)
            dve.wait_ge(sem("conv_exp"), 1)
            link(dve, "dve", nc.vector.tensor_reduce(row_sum[:, :], logit[:, :, :], AX_X, ALU.add))
            link(dve, "dve", nc.vector.reciprocal(row_inv[:, :], row_sum[:, :]))
            for a in range(4):
                last = nc.vector.tensor_tensor(prob4[:, :, a, :], logit[:, :, :],
                                               row_inv[:, :].unsqueeze(2).to_broadcast([128, 16, K]), ALU.mult)
            last.then_inc(sem("conv_prob"), 1)
            bandv = band[:, :, :].rearrange("s t (q r) -> s t q r", r=K)
            for g in range(4):
                dve.wait_ge(sem("conv_probT"), g + 1)
                p = bank[4 + g][:, :].rearrange("s (r t q) -> s t q r", r=8, q=TB)
                m = conv_mask[:, :, 8 * g:8 * g + 8].unsqueeze(1).to_broadcast([128, TILES, TB, 8])
                nc.vector.tensor_tensor(bandv[:, :, :, 8 * g:8 * g + 8], p, m, ALU.mult) \
                  .then_inc(sem("conv_band"), 1)
                m = conv_edge[:, 8 * g:8 * g + 8].unsqueeze(1).to_broadcast([K, TILES, 8])
                nc.vector.tensor_tensor(edge[:, :, 8 * g:8 * g + 8], p[0:K, :, TB - 1, :], m, ALU.mult) \
                  .then_inc(sem("conv_band"), 1)
            for b in range(B):
                dve.wait_ge(sem("pv_raw"), b + 1)
                nc.vector.scalar_tensor_tensor(x[:, b, :], bank[b][:, :], gate(0, b), x[:, b, :],
                                               ALU.mult, ALU.add).then_inc(sem("x_ready"), 1)

        next_block()
        lr_p = tmp_sb("lr_p", [R, 2, T])
        lr_h = tmp_sb("lr_h", [128, 2, FB, T])
        lr_q = tmp_sb("lr_q", [R, 2, T])
        tmp = tmp_sb("tmp", [C, 2, T])

        def lr_pe(pe):
            def up(b):
                pe.wait_ge(sem("h_ready"), 4 + b + 1)
                if b:
                    pe.wait_ge(sem("lr_out_read"), b - 1) if b > 1 else None
                    pe.wait_ge(sem("lr_p_ready"), b)
                else:
                    pe.wait_ge(sem("early_loaded"), 80)
                pe.matmul(bank[4][0:R, :], lr_u1[:, :], hb(b), start=True, stop=True) \
                  .then_inc(sem("lr_p_raw"), 1)
                pe.wait_ge(sem("lr_p_ready"), b + 1)
                for f in range(FB):
                    n = FB * b + f
                    if n >= 2:
                        pe.wait_ge(sem("up_acted"), n - 1)
                    pe.matmul(bank[5 + n % 2][:, :], lr_v1[:, 128 * f:128 * f + 128], lr_p[:, b % 2, :],
                              start=True, stop=True).then_inc(sem("up_raw"), 1)

            def down(b):
                pe.wait_ge(sem("up_acted"), FB * b + FB)
                if b:
                    pe.wait_ge(sem("lr_out_read"), b)
                for f in range(FB):
                    last = pe.matmul(bank[7][0:R, :], lr_u2[:, f, :], lr_h[:, b % 2, f, :],
                                     start=(f == 0), stop=(f == FB - 1))
                last.then_inc(sem("lr_q_raw"), 1)
                pe.wait_ge(sem("lr_q_ready"), b + 1)
                pe.matmul(bank[7][:, :], lr_v2[:, :], lr_q[:, b % 2, :], start=True, stop=True) \
                  .then_inc(sem("lr_out"), 1)

            up(0)
            for b in range(B):
                if b + 1 < B:
                    up(b + 1)
                down(b)

        def lr_act(act):
            for b in range(B):
                for f in range(FB):
                    n = FB * b + f
                    act.wait_ge(sem("up_raw"), n + 1)
                    if b >= 2 and f == 0:
                        act.wait_ge(sem("lr_q_raw"), b - 1)
                    nc.scalar.activation(lr_h[:, b % 2, f, :], bank[5 + n % 2][:, :], ACT.Gelu_apprx_tanh,
                                         bias=v("ffn0_b1", f)).then_inc(sem("up_acted"), 1)

        def lr_dve(dve):
            def p(b):
                dve.wait_ge(sem("lr_p_raw"), b + 1)
                if b >= 2:
                    dve.wait_ge(sem("up_raw"), FB * (b - 1))
                nc.vector.tensor_copy(lr_p[:, b % 2, :], bank[4][0:R, :]).then_inc(sem("lr_p_ready"), 1)

            p(0)
            for b in range(B):
                if b + 1 < B:
                    p(b + 1)
                dve.wait_ge(sem("lr_q_raw"), b + 1)
                if b >= 2:
                    dve.wait_ge(sem("lr_out"), b - 1)
                nc.vector.tensor_copy(lr_q[:, b % 2, :], bank[7][0:R, :]).then_inc(sem("lr_q_ready"), 1)
                dve.wait_ge(sem("lr_out"), b + 1)
                if b >= 2:
                    dve.wait_ge(sem("x_ready"), 4 + b - 1)
                nc.vector.tensor_scalar(tmp[:, b % 2, :], bank[7][:, :], v("ffn0_b2"), gate(1, b),
                                        ALU.add, ALU.mult).then_inc(sem("lr_out_read"), 1)
                dve.wait_ge(sem("lr_out_read"), b + 1)
                nc.vector.tensor_tensor(x[:, b, :], x[:, b, :], tmp[:, b % 2, :], ALU.add) \
                  .then_inc(sem("x_ready"), 1)

        next_block()
        scan_a = tmp_sb("scan_a", [C, 2, T])
        scan_b = tmp_sb("scan_b", [C, 2, T])
        scan_c = tmp_sb("scan_c", [C, 2, T])
        scan_1a = tmp_sb("scan_1a", [C, 2, T])

        def scan_banks(b):
            return (bank[4], bank[5], bank[6]) if b % 2 == 0 else (bank[7], bank[0], bank[1])

        def scan_pe(pe):
            pe.wait_ge(sem("ln_normed"), 12)
            for b in range(B):
                pe.wait_ge(sem("h_ready"), 8 + b + 1)
                if b >= 2:
                    pe.wait_ge(sem("scan_gates"), 3 * (b - 1))
                for i in range(3):
                    pe.matmul(scan_banks(b)[i][:, :], scan_w[:, i, :], hb(b), start=True, stop=True) \
                      .then_inc(sem("scan_raw"), 1)

        def scan_act(act):
            for b in range(B):
                if b >= 2:
                    act.wait_ge(sem("x_ready"), 8 + b - 1)
                for i, (dst, f, bias) in enumerate(((scan_a, ACT.Sigmoid, "scan_ba"), (scan_b, ACT.Tanh, "scan_bb"),
                                                    (scan_c, ACT.Sigmoid, "scan_bc"))):
                    act.wait_ge(sem("scan_raw"), 3 * b + i + 1)
                    nc.scalar.activation(dst[:, b % 2, :], scan_banks(b)[i][:, :], f, bias=v(bias)) \
                      .then_inc(sem("scan_gates"), 1)

        def scan_pool(pool):
            for b in range(B):
                pool.wait_ge(sem("scan_gates"), 3 * b + 1)
                if b >= 2:
                    pool.wait_ge(sem("scan_in"), b - 1)
                nc.gpsimd.tensor_scalar(scan_1a[:, b % 2, :], scan_a[:, b % 2, :], -1.0, 1.0,
                                        ALU.mult, ALU.add).then_inc(sem("scan_1a_ready"), 1)

        def scan_dve(dve):
            for b in range(B):
                i = b % 2
                dve.wait_ge(sem("scan_gates"), 3 * b + 3)
                dve.wait_ge(sem("scan_1a_ready"), b + 1)
                nc.vector.tensor_tensor(scan_b[:, i, :], scan_1a[:, i, :], scan_b[:, i, :], ALU.mult) \
                  .then_inc(sem("scan_in"), 1)
                dve.wait_ge(sem("scan_in"), b + 1)
                link(dve, "dve", nc.vector.tensor_tensor_scan(scan_1a[:, i, :], scan_a[:, i, :], scan_b[:, i, :],
                                                              0.0, ALU.mult, ALU.add))
                link(dve, "dve", nc.vector.tensor_tensor(scan_c[:, i, :], scan_c[:, i, :], scan_1a[:, i, :], ALU.mult))
                nc.vector.scalar_tensor_tensor(x[:, b, :], scan_c[:, i, :], gate(2, b), x[:, b, :],
                                               ALU.mult, ALU.add).then_inc(sem("x_ready"), 1)

        next_block()
        bn = tmp_sb("bn", [128, TILES, 6])
        mv = tmp_sb("mv", [128, TILES, 2])
        stat = tmp_sb("stat", [128, TILES, 6])
        small = tmp_sb("small", [128, TILES, C])
        statT = tmp_sb("statT", [6, B, T])
        r_hid = tmp_sb("r_hid", [64, B, T])
        prob = tmp_sb("prob", [128, TILES, E])
        r_max = tmp_sb("r_max", [128, TILES])
        r_sum = tmp_sb("r_sum", [128, TILES])
        r_inv = tmp_sb("r_inv", [128, TILES])
        top8 = tmp_sb("top8", [128, TILES, 8])
        top8_at = tmp_sb("top8_at", [128, TILES, 8], U32)
        pick = tmp_sb("pick", [128, 2, TILES])
        onehot = tmp_sb("onehot", [128, 2, TILES, E])
        hit = tmp_sb("hit", [128, TILES, E])
        score = tmp_sb("score", [128, 4, B, E])
        scoreT = tmp_sb("scoreT", [128, T])
        rest = [tmp_sb(f"rest{i}", [128, T]) for i in range(2)]
        best = tmp_sb("best", [128, CAP])
        cand = [tmp_sb(f"cand{i}", [E, B, CAP]) for i in range(2)]
        best_all = tmp_sb("best_all", [E, CAP])
        above_last = tmp_sb("above_last", [E, CAP])
        cut = tmp_sb("cut", [E, 2])
        cut4 = tmp_sb("cut4", [128, 2])
        ones = tmp_sb("ones", [128, T])
        is_gt = tmp_sb("is_gt", [128, T])
        is_eq = tmp_sb("is_eq", [128, T])
        cum_gt = tmp_sb("cum_gt", [128, T])
        cum_eq = tmp_sb("cum_eq", [128, T])
        totals = tmp_sb("totals", [128, 2])
        offset = tmp_sb("offset", [128, 2])
        looked = tmp_sb("looked", [128, 2, TILES, E])
        place = tmp_sb("place", [128, 2, TILES])
        valid = tmp_sb("valid", [128, 2, TILES])
        slot = tmp_sb("slot", [128, 2, TILES])
        slot_u = tmp_sb("slot_u", [128, 2, TILES], U32)
        weight = tmp_sb("weight", [128, 2, TILES])
        xg = tmp_sb("xg", [128, SLOTS // 128, C])
        xgT = tmp_sb("xgT", [C, SLOTS + 128 - CAP])
        moe_silu = [tmp_sb(f"moe_silu{u}", [128, 3, 2 * CAP]) for u in range(2)]
        moe_act = [tmp_sb(f"moe_act{u}", [128, 3, 2 * CAP]) for u in range(2)]
        y_slot = [tmp_sb(f"y_slot{u}", [CAP, 2, C]) for u in range(2)]

        def up(u, q, j):
            return bank[2 * u + q][:, :].rearrange("p (j c) -> p j c", c=128)[:, j:j + 2, 0:CAP]

        y_tok = tmp_sb("y_tok", [128, 2, TILES, C])
        y_sum = tmp_sb("y_sum", [128, TILES, C])
        xg_dram = nc.dram_tensor("xg_dram", (SLOTS, C), F32, kind="Internal").ap()
        y_dram = nc.dram_tensor("y_dram", (SLOTS + 1, C), F32, kind="Internal").ap()

        def moe_pe(pe):
            pe.wait_ge(sem("h_ready"), 16)
            pe.wait_ge(sem("ln_normed"), 16)
            pe.wait_ge(sem("x_ready"), 12)
            htok_pe(pe, bank[0:4], lambda b, i: hh(b, 128 * i, 128))
            pe.wait_ge(sem("moe_stats"), 1)
            for b in range(B):
                for i in range(TB):
                    last = pe.transpose(bank[4 + b][0:6, 128 * i:128 * i + 128], stat[:, TB * b + i, :], ident[:, :])
                last.then_inc(sem("moe_statT_raw"), 1)
            pe.wait_ge(sem("moe_loaded"), 80)
            for b in range(B):
                pe.wait_ge(sem("htok_ready"), B + b + 1)
                pe.matmul(bank[b][0:64, :], r1_c[:, :], hb(b), start=True, stop=False)
                pe.wait_ge(sem("moe_statT_ready"), b + 1)
                pe.matmul(bank[b][0:64, :], r1_s[:, :], statT[:, b, :], start=False, stop=True) \
                  .then_inc(sem("moe_hid_raw"), 1)
            for b in range(B):
                pe.wait_ge(sem("moe_hid_ready"), b + 1)
                for i in range(TB):
                    t = TB * b + i
                    last = pe.matmul(bank[4][:, E * t:E * t + E], r_hid[:, b, 128 * i:128 * i + 128], r2_w[:, :],
                                     start=True, stop=True)
            last.then_inc(sem("moe_logits"), 1)
            pe.wait_ge(sem("moe_scored"), 1)
            for g in range(4):
                last = pe.transpose(bank[5][:, 128 * g:128 * g + 128],
                                    score[:, g, :, :].rearrange("p j e -> p (j e)"), ident[:, :])
            last.then_inc(sem("moe_scoreT_raw"), 1)
            pe.wait_ge(sem("moe_totals"), 2)
            pe.matmul(bank[6][:, 0:2], chunk_sum[:, :], totals[:, :], start=True, stop=True) \
              .then_inc(sem("moe_offset_raw"), 1)
            pe.wait_ge(sem("moe_placed"), 1)
            for g in range(4):
                last = pe.transpose(bank[7][:, 128 * g:128 * g + 128], cum_gt[:, 128 * g:128 * g + 128], ident[:, :])
            last.then_inc(sem("moe_placeT"), 1)
            pe.wait_ge(sem("xg_loaded"), 16)
            for s in range(NB128 // 4):
                for i in range(4):
                    last = pe.transpose(bank[s][:, 128 * i:128 * i + 128], xg[:, 4 * s + i, :], ident[:, :])
                last.then_inc(sem("xgT_raw"), 1)
            pe.wait_ge(sem("xgT_ready"), NB128 // 4)

            with pe.Fori(0, G // 2) as i:
                for u in range(2):
                    w = moe_w[u]
                    pe.wait_ge(sem(f"moe_w_loaded{u}"), i * 16 + 16)
                    for q in range(2):
                        for j in range(4):
                            last = pe.matmul(bank[2 * u + q][:, 128 * j:128 * j + 128],
                                             w[:, 512 * q + 128 * j:512 * q + 128 * j + 128],
                                             xgT[:, bass.ds(i * (4 * CAP) + (2 * u + q) * CAP, 128)],
                                             start=True, stop=True)
                        last.then_inc(sem(f"moe_up{u}"), 1)
                    for j in range(2):
                        last = pe.matmul(bank[4 + u][:, 2 * CAP * j:2 * CAP * j + 2 * CAP],
                                         w[:, 1536 + 128 * j:1536 + 128 * j + 128],
                                         xgT[:, bass.ds(i * (4 * CAP) + 2 * u * CAP, 2 * CAP)],
                                         start=True, stop=True)
                    last.then_inc(sem(f"moe_up{u}"), 1)
                for u in range(2):
                    w = moe_w[u]
                    pe.wait_ge(sem(f"moe_acted{u}"), i * 3 + 3)
                    for q in range(2):
                        y = bank[6 + u][0:CAP, C * q:C * q + C]
                        for j in range(2):
                            pe.matmul(y, moe_act[u][:, q, CAP * j:CAP * j + CAP],
                                      w[:, 1024 + 256 * q + 128 * j:1024 + 256 * q + 128 * j + 128],
                                      start=(j == 0), stop=False)
                        last = pe.matmul(y, moe_act[u][:, 2, CAP * q:CAP * q + CAP], w[:, 1792:1920],
                                         start=False, stop=True)
                    last.then_inc(sem(f"moe_y{u}"), 1)

            for b in range(B):
                pe.wait_ge(sem("y_summed"), b + 1)
                for i in range(TB):
                    last = pe.transpose(bank[b][:, 128 * i:128 * i + 128], y_sum[:, TB * b + i, :], ident[:, :])
                last.then_inc(sem("moe_out"), 1)

        def moe_act_engine(act):
            htok_act(act, B)
            act.wait_ge(sem("moe_moments"), 2)
            nc.scalar.activation(stat[:, :, 1], stat[:, :, 1], ACT.Sqrt).then_inc(sem("moe_roots"), 1)
            nc.scalar.activation(stat[:, :, 4], stat[:, :, 4], ACT.Sqrt).then_inc(sem("moe_roots"), 1)
            for b in range(B):
                act.wait_ge(sem("moe_hid_raw"), b + 1)
                nc.scalar.activation(r_hid[:, b, :], bank[b][0:64, :], ACT.Gelu, bias=v("r1_b")[0:64, :]) \
                  .then_inc(sem("moe_hid_ready"), 1)
            act.wait_ge(sem("moe_shifted"), 1)
            nc.scalar.activation(prob[:, :, :], prob[:, :, :], ACT.Exp).then_inc(sem("moe_exp"), 1)
            for s in range(NB128 // 4):
                act.wait_ge(sem("xgT_raw"), s + 1)
                nc.scalar.activation(xgT[:, 512 * s:512 * s + 512], bank[s][:, :], ACT.Copy) \
                  .then_inc(sem("xgT_ready"), 1)
            nc.scalar.preload_act_table(ACT.Silu)
            with act.Fori(0, G // 2) as i:
                for u in range(2):
                    for q in range(3):
                        act.wait_ge(sem(f"moe_up{u}"), i * 3 + (q + 1))
                        src = up(u, q, 0) if q < 2 else bank[4 + u][:, 0:2 * CAP].rearrange("p (j c) -> p j c", j=2)
                        nc.scalar.activation(moe_silu[u][:, q, :].rearrange("p (j c) -> p j c", j=2), src, ACT.Silu) \
                          .then_inc(sem(f"moe_silued{u}"), 1)

        def moe_dve(dve):
            def L(ins):
                link(dve, "dve", ins)

            for b in range(B):
                dve.wait_ge(sem("htok_ready"), B + b + 1)
                for i in range(TB):
                    t = TB * b + i
                    last = nc.vector.bn_stats(bn[:, t, :], htok[:, t, :])
            L(last)
            for t in range(TILES):
                last = nc.vector.bn_aggr(mv[:, t, :], bn[:, t, :])
            L(last)
            nc.vector.tensor_scalar(stat[:, :, 1], mv[:, :, 1], C / (C - 1.0), None, ALU.mult) \
              .then_inc(sem("moe_moments"), 1)
            L(nc.vector.tensor_tensor(stat[:, :, 0], mv[:, :, 0], mv[:, :, 0], ALU.mult))
            L(nc.vector.tensor_tensor(stat[:, :, 4], stat[:, :, 0], mv[:, :, 1], ALU.add))
            nc.vector.tensor_scalar(stat[:, :, 4], stat[:, :, 4], float(C), None, ALU.mult) \
              .then_inc(sem("moe_moments"), 1)
            L(nc.vector.tensor_copy(stat[:, :, 0], mv[:, :, 0]))
            nc.vector.tensor_reduce(stat[:, :, 2], htok[:, :, :], AX_X, ALU.min)
            nc.vector.tensor_reduce(stat[:, :, 3], htok[:, :, :], AX_X, ALU.max)
            L(nc.vector.scalar_tensor_tensor(small[:, :, :], htok[:, :, :], -1.0, htok[:, :, :], ALU.mult, ALU.max))
            L(nc.vector.tensor_scalar(small[:, :, :], small[:, :, :], 1e-6, None, ALU.is_lt))
            L(nc.vector.tensor_reduce(stat[:, :, 5], small[:, :, :], AX_X, ALU.add))
            dve.wait_ge(sem("moe_roots"), 2)
            nc.vector.tensor_scalar(stat[:, :, 5], stat[:, :, 5], 1.0 / C, None, ALU.mult) \
              .then_inc(sem("moe_stats"), 1)
            for b in range(B):
                dve.wait_ge(sem("moe_statT_raw"), b + 1)
                nc.vector.tensor_copy(statT[:, b, :], bank[4 + b][0:6, :]).then_inc(sem("moe_statT_ready"), 1)

            dve.wait_ge(sem("moe_logits"), 1)
            logits = bank[4][:, :].rearrange("p (t e) -> p t e", e=E)
            L(nc.vector.tensor_reduce(r_max[:, :], logits, AX_X, ALU.max))
            nc.vector.tensor_tensor(prob[:, :, :], logits, r_max[:, :].unsqueeze(2).to_broadcast([128, TILES, E]),
                                    ALU.subtract).then_inc(sem("moe_shifted"), 1)
            dve.wait_ge(sem("moe_exp"), 1)
            L(nc.vector.tensor_reduce(r_sum[:, :], prob[:, :, :], AX_X, ALU.add))
            L(nc.vector.reciprocal(r_inv[:, :], r_sum[:, :]))
            L(nc.vector.tensor_tensor(prob[:, :, :], prob[:, :, :],
                                      r_inv[:, :].unsqueeze(2).to_broadcast([128, TILES, E]), ALU.mult))
            for t in range(TILES):
                last = nc.vector.max(top8[:, t, :], prob[:, t, :])
            L(last)
            for t in range(TILES):
                last = nc.vector.max_index(top8_at[:, t, :], top8[:, t, :], prob[:, t, :])
            L(last)
            L(nc.vector.tensor_copy(pick[:, :, :].rearrange("p k t -> p t k"), top8_at[:, :, 0:2]))
            experts = iota_e[:, :].unsqueeze(1).to_broadcast([128, TILES, E])
            for k in range(2):
                last = nc.vector.tensor_tensor(onehot[:, k, :, :], experts,
                                               pick[:, k, :].unsqueeze(2).to_broadcast([128, TILES, E]), ALU.is_equal)
            L(last)
            L(nc.vector.tensor_tensor(hit[:, :, :], onehot[:, 0, :, :], onehot[:, 1, :, :], ALU.add))
            L(nc.vector.tensor_tensor(prob[:, :, :], prob[:, :, :], hit[:, :, :], ALU.mult))
            L(nc.vector.tensor_scalar(hit[:, :, :], hit[:, :, :], -1.0, None, ALU.add))
            nc.vector.tensor_tensor(score[:, :, :, :].rearrange("p g j e -> p j g e"),
                                    prob[:, :, :].rearrange("p (j g) e -> p j g e", j=B),
                                    hit[:, :, :].rearrange("p (j g) e -> p j g e", j=B), ALU.add) \
              .then_inc(sem("moe_scored"), 1)
            L(nc.vector.tensor_tensor(r_sum[:, :], top8[:, :, 0], top8[:, :, 1], ALU.add))
            L(nc.vector.reciprocal(r_inv[:, :], r_sum[:, :]))
            for k in range(2):
                last = nc.vector.tensor_tensor(weight[:, k, :], top8[:, :, k], r_inv[:, :], ALU.mult)
            L(last)
            dve.wait_ge(sem("moe_scoreT_raw"), 1)
            L(nc.vector.tensor_copy(scoreT[:, :], bank[5][:, :]))
            for r in range(ROUNDS):
                src = scoreT if r == 0 else rest[(r - 1) % 2]
                L(nc.vector.max(best[:, 8 * r:8 * r + 8], src[:, :]))
                if r < ROUNDS - 1:
                    L(nc.vector.match_replace(rest[r % 2][:, :], best[:, 8 * r:8 * r + 8], src[:, :], -2.0))
            nc.vector.memset(xgT[:, SLOTS:], 0.0)
            nc.vector.memset(ones[:, :], 1.0).then_inc(sem("moe_best"), 1)
            dve.wait_ge(sem("moe_spread"), 16 * B)
            for r in range(ROUNDS):
                src = cand[r % 2][:, :, :].rearrange("e j c -> e (j c)")
                L(nc.vector.max(best_all[:, 8 * r:8 * r + 8], src))
                if r < ROUNDS - 1:
                    L(nc.vector.match_replace(cand[(r + 1) % 2][:, :, :].rearrange("e j c -> e (j c)"),
                                              best_all[:, 8 * r:8 * r + 8], src, -2.0))
            L(nc.vector.tensor_copy(cut[:, 0:1], best_all[:, CAP - 1:CAP]))
            L(nc.vector.tensor_scalar(above_last[:, :], best_all[:, :], cut[:, 0:1], None, ALU.is_gt))
            nc.vector.tensor_reduce(cut[:, 1:2], above_last[:, :], AX_X, ALU.add).then_inc(sem("moe_cut"), 1)
            dve.wait_ge(sem("moe_spread"), 32 * B)
            nc.vector.tensor_scalar(is_gt[:, :], scoreT[:, :], cut4[:, 0:1], None, ALU.is_gt)
            L(nc.vector.tensor_scalar(is_eq[:, :], scoreT[:, :], cut4[:, 0:1], None, ALU.is_equal))
            nc.vector.tensor_tensor_scan(cum_gt[:, :], ones[:, :], is_gt[:, :], 0.0, ALU.mult, ALU.add)
            L(nc.vector.tensor_tensor_scan(cum_eq[:, :], ones[:, :], is_eq[:, :], 0.0, ALU.mult, ALU.add))
            nc.vector.tensor_copy(totals[:, 0:1], cum_gt[:, T - 1:T]).then_inc(sem("moe_totals"), 1)
            nc.vector.tensor_copy(totals[:, 1:2], cum_eq[:, T - 1:T]).then_inc(sem("moe_totals"), 1)
            dve.wait_ge(sem("moe_offset_raw"), 1)
            nc.vector.tensor_copy(offset[:, 0:1], bank[6][:, 0:1])
            L(nc.vector.tensor_tensor(offset[:, 1:2], bank[6][:, 1:2], cut4[:, 1:2], ALU.add))
            L(nc.vector.scalar_tensor_tensor(cum_gt[:, :], cum_gt[:, :], offset[:, 0:1], is_gt[:, :], ALU.add, ALU.mult))
            L(nc.vector.scalar_tensor_tensor(cum_eq[:, :], cum_eq[:, :], offset[:, 1:2], is_eq[:, :], ALU.add, ALU.mult))
            nc.vector.tensor_tensor(cum_gt[:, :], cum_gt[:, :], cum_eq[:, :], ALU.add).then_inc(sem("moe_placed"), 1)
            dve.wait_ge(sem("moe_placeT"), 1)
            placeT = bank[7][:, :].rearrange("p (g j e) -> p j g e", g=4, j=B)
            for k in range(2):
                last = nc.vector.tensor_tensor(looked[:, k, :, :].rearrange("p (j g) e -> p j g e", j=B),
                                               onehot[:, k, :, :].rearrange("p (j g) e -> p j g e", j=B), placeT, ALU.mult)
            L(last)
            L(nc.vector.tensor_reduce(place[:, :, :], looked[:, :, :, :], AX_X, ALU.add))
            L(nc.vector.tensor_scalar(valid[:, :, :], place[:, :, :], 1.0, None, ALU.is_ge))
            L(nc.vector.scalar_tensor_tensor(valid[:, :, :], place[:, :, :], float(CAP), valid[:, :, :],
                                             ALU.is_le, ALU.mult))
            L(nc.vector.scalar_tensor_tensor(slot[:, :, :], pick[:, :, :], float(CAP), place[:, :, :],
                                             ALU.mult, ALU.add))
            L(nc.vector.scalar_tensor_tensor(slot[:, :, :], slot[:, :, :], -1.0 - DUMP, valid[:, :, :],
                                             ALU.add, ALU.mult))
            L(nc.vector.tensor_scalar(slot[:, :, :], slot[:, :, :], float(DUMP), None, ALU.add))
            nc.vector.tensor_copy(slot_u[:, :, :], slot[:, :, :]).then_inc(sem("moe_slots"), 1)
            L(nc.vector.tensor_tensor(weight[:, :, :], weight[:, :, :], valid[:, :, :], ALU.mult))

            with dve.Fori(0, G // 2) as i:
                for u in range(2):
                    for q in range(2):
                        dve.wait_ge(sem(f"moe_silued{u}"), i * 3 + (q + 1))
                        nc.vector.tensor_tensor(moe_act[u][:, q, :].rearrange("p (j c) -> p j c", j=2),
                                                moe_silu[u][:, q, :].rearrange("p (j c) -> p j c", j=2),
                                                up(u, q, 2), ALU.mult) \
                          .then_inc(sem(f"moe_acted{u}"), 1)
                    dve.wait_ge(sem(f"moe_silued{u}"), i * 3 + 3)
                    nc.vector.scalar_tensor_tensor(moe_act[u][:, 2, :], moe_silu[u][:, 2, :], 0.05,
                                                   bank[4 + u][:, 2 * CAP:4 * CAP], ALU.mult, ALU.mult) \
                      .then_inc(sem(f"moe_acted{u}"), 1)
                for u in range(2):
                    dve.wait_ge(sem(f"moe_y{u}"), i + 1)
                    dve.wait_ge(sem(f"moe_stored{u}"), i * 16 + 16)
                    nc.vector.tensor_copy(y_slot[u][:, :, :],
                                          bank[6 + u][0:CAP, 0:2 * C].rearrange("p (q c) -> p q c", q=2)) \
                      .then_inc(sem(f"moe_y_read{u}"), 1)

            for b in range(B):
                dve.wait_ge(sem(f"y_gathered{b}"), 16 * 2 * TB)
                for t in range(TB * b, TB * b + TB):
                    last = nc.vector.tensor_scalar(y_sum[:, t, :], y_tok[:, 0, t, :], weight[:, 0, t:t + 1], None,
                                                   ALU.mult)
                L(last)
                for t in range(TB * b, TB * b + TB):
                    last = nc.vector.scalar_tensor_tensor(y_sum[:, t, :], y_tok[:, 1, t, :], weight[:, 1, t:t + 1],
                                                          y_sum[:, t, :], ALU.mult, ALU.add)
                last.then_inc(sem("y_summed"), 1)
            for b in range(B):
                dve.wait_ge(sem("moe_out"), b + 1)
                nc.vector.scalar_tensor_tensor(x[:, b, :], bank[b][:, :], gate(3, b), x[:, b, :],
                                               ALU.mult, ALU.add).then_inc(sem("x_ready"), 1)

        def moe_sp(sp):
            for name, dst in (("r1_c", r1_c), ("r1_s", r1_s), ("r2_w", r2_w), ("iota_e", iota_e),
                              ("chunk_sum", chunk_sum)):
                sp.dma_start(dst[:, :], d[name]).then_inc(sem("moe_loaded"), 16)
            sp.wait_ge(sem("filled"), 2)
            for s in range(NB128 // 4):
                sp.dma_start(xg_dram[512 * s:512 * s + 512, :].rearrange("(p r) c -> p (r c)", p=128),
                             zeros[:, :]).then_inc(sem("moe_zeroed"), 16)
            for u in range(2):
                sp.dma_start(y_dram[SLOTS:SLOTS + 1, 64 * u:64 * u + 64], zeros[0:1, 0:64]) \
                  .then_inc(sem(f"moe_stored{u}"), 16)
            for u in range(2):
                sp.dma_start(moe_w[u][:, :], d["moe_w"][u, :, :]).then_inc(sem(f"moe_w_loaded{u}"), 16)
            sp.wait_ge(sem("moe_best"), 1)
            for j in range(B):
                sp.dma_start(cand[0][:, j, :], best[E * j:E * j + E, :]).then_inc(sem("moe_spread"), 16)
            sp.wait_ge(sem("moe_cut"), 1)
            for j in range(B):
                sp.dma_start(cut4[E * j:E * j + E, :], cut[:, :]).then_inc(sem("moe_spread"), 16)
            sp.wait_ge(sem("xg_scattered"), 16 * 2 * TILES)
            sp.dma_start(xg[:, :, :], xg_dram.rearrange("(s p) c -> p s c", p=128)).then_inc(sem("xg_loaded"), 16)

            def store(i, u):
                sp.wait_ge(sem(f"moe_y_read{u}"), i + 1)
                row = i * (4 * CAP) + 2 * u * CAP
                rows = slice(row, row + 2 * CAP) if isinstance(i, int) else bass.ds(row, 2 * CAP)
                sp.dma_start(y_dram[rows, :].rearrange("(q p) c -> p q c", q=2), y_slot[u][:, :, :]) \
                  .then_inc(sem(f"moe_stored{u}"), 16)

            with sp.Fori(0, G // 2 - 1) as i:
                for u in range(2):
                    sp.wait_ge(sem(f"moe_y{u}"), i + 1)
                    sp.dma_start(moe_w[u][:, :], d["moe_w"][bass.ds(i * 2 + (2 + u), 1), :, :]
                                 .rearrange("o p w -> (o p) w")).then_inc(sem(f"moe_w_loaded{u}"), 16)
                    store(i, u)
            for u in range(2):
                store(G // 2 - 1, u)

        def moe_pool(pool):
            pool.wait_ge(sem("moe_slots"), 1)
            pool.wait_ge(sem("moe_zeroed"), 16 * (NB128 // 4))
            for t in range(TILES):
                for k in range(2):
                    nc.gpsimd.indirect_dma_start(
                        xg_dram, bass.IndirectOffsetOnAxis(slot_u[:, k, t:t + 1], 0), htok[:, t, :], None,
                        bounds_check=SLOTS - 1, oob_is_err=False).then_inc(sem("xg_scattered"), 16)
            for u in range(2):
                pool.wait_ge(sem(f"moe_stored{u}"), 16 * (G // 2) + 16)
            for t in range(TILES):
                for k in range(2):
                    nc.gpsimd.indirect_dma_start(
                        y_tok[:, k, t, :], None, y_dram, bass.IndirectOffsetOnAxis(slot_u[:, k, t:t + 1], 0)) \
                      .then_inc(sem(f"y_gathered{t // TB}"), 16)

        next_block()
        q_diag = [tmp_sb(f"q_diag{i}", [128, NBLK, 128]) for i in range(2)]
        k_rope = [tmp_sb(f"k_rope{i}", [128, T]) for i in range(2)]
        rope_part = [tmp_sb(f"rope_part{i}", [128, T]) for i in range(4)]
        v_tok = [tmp_sb(f"v_tok{i}", [128, TB, 128]) for i in range(B)]
        soft = [tmp_sb(f"soft{i}", [128, PW]) for i in range(2)]
        softT = tmp_sb("softT", [128, NFILL * 512])
        neg_max = tmp_sb("neg_max", [128, 2, NBLK])
        exp_sum = tmp_sb("exp_sum", [128, 2, NBLK])
        exp_inv = tmp_sb("exp_inv", [128, 2, NBLK])
        head_out = [tmp_sb(f"head_out{i}", [128, T]) for i in range(2)]
        gate_bo = tmp_sb("gate_bo", [128, B])
        att_w = [tmp_sb(f"att_w{i}", [C, 3, 128]) for i in range(2)]
        att_wo = tmp_sb("att_wo", [128, C])
        rope_tab = tmp_sb("rope_tab", [128, 4, T])
        att_mask = tmp_sb("att_mask", [128, 64])

        def keys(j):
            return 64 * (j + 1)

        def att_loop(eng, part):
            part(0, 0, True, True, True, True, False)
            with eng.Fori(0, PAIRS * B // UNROLL - 1) as i:
                for u in range(UNROLL):
                    part(i, u, False, True, True, True, False)
                    part(i, u + 1, True, True, True, True, True)
            i = PAIRS * B // UNROLL - 1
            for u in range(UNROLL):
                left = UNROLL - 1 - u
                part(i, u, False, left >= 1, left >= 2, True, False)
                part(i, u + 1, True, left >= 2, left >= 3, left >= 1, True)

        def att_project(pe, i, u, piece):
            b, p = u % B, u // B % 2
            pe.wait_ge(sem(f"w_loaded{p}"), i * 16 + (16 * (u // UNROLL) + 16))
            if not isinstance(i, int) or u or piece:
                pe.wait_ge(sem("proj_read"), i * (3 * UNROLL) + (3 * u + piece))
            if piece < 2:
                last = pe.matmul(bank[0][:, :], att_w[p][:, piece, :], hb(b), start=True, stop=True)
            else:
                for t in range(TB):
                    last = pe.matmul(bank[0][:, 128 * t:128 * t + 128], hh(b, 128 * t, 128), att_w[p][:, 2, :],
                                     start=True, stop=True)
            last.then_inc(sem("proj_raw"), 1)

        def att_scores(pe, i, u, g, first=False):
            par = u % 2
            if g == 0:
                pe.wait_ge(sem("roped"), i * (5 * UNROLL) + (5 * u + 5))
            if g >= 2:
                pe.wait_ge(sem("s_exp"), i * (8 * UNROLL) + (8 * u + GCUM[g - 2]))
            elif not first:
                pe.wait_ge(sem("s_exp"), i * (8 * UNROLL) + (8 * u + GCUM[g + 3] - 8))
            at = 0
            for j in GROUPS[g]:
                last = pe.matmul(bank[1 + (5 * par + g) % 2][:, at:at + keys(j)], q_diag[par][:, j, :],
                                 k_rope[par][:, 0:keys(j)], start=True, stop=True)
                at += keys(j)
            last.then_inc(sem("s_raw"), 1)

        def att_transpose(pe, i, u, f):
            if f == 0:
                pe.wait_ge(sem("p_normed"), i * UNROLL + (u + 1))
            if f >= 2:
                pe.wait_ge(sem("pt_ready"), i * (5 * UNROLL) + (5 * u + f - 1))
            for q in range(4 * f, 4 * f + 4):
                jc, j = CHUNKS[q]
                last = pe.transpose(bank[3 + (u + f) % 2][:, 128 * (q % 4):128 * (q % 4) + 128],
                                    soft[u % 2][:, POFF[j] + 128 * jc:POFF[j] + 128 * jc + 128], ident[:, :])
            last.then_inc(sem("pt_raw"), 1)

        def att_values(pe, i, u):
            for half in range(2):
                pe.wait_ge(sem("pt_ready"), i * (5 * UNROLL) + (5 * u + (5 if half else 3)))
                js = range(4 * half, 4 * half + 4)
                for jc in range(2 * half + 2):
                    q = [a for a, (c, j) in enumerate(CHUNKS) if c == jc and j in js]
                    lo = 128 * (CHUNKS[q[0]][1] - 4 * half)
                    last = pe.matmul(bank[5 + half][:, lo:512], v_tok[u % B][:, jc, :],
                                     softT[:, 128 * q[0]:128 * q[-1] + 128], start=(jc == 0), stop=(jc == 2 * half + 1))
                last.then_inc(sem("pv_raw"), 1)

        def att_output(pe, i, u):
            pe.wait_ge(sem("wo_loaded"), i * (16 * UNROLL // B) + (16 * (u // B) + 16))
            pe.wait_ge(sem("pair_added"), i * UNROLL + (u + B))
            pe.wait_ge(sem("pv_read"), i * (4 * UNROLL) + (4 * u + 4))
            pe.matmul(bank[7][:, :], att_wo[:, :], head_out[u % 2][:, :], start=True, stop=True) \
              .then_inc(sem("att_out"), 1)

        def att_pe(pe):
            pe.wait_ge(sem("h_ready"), 20)
            pe.wait_ge(sem("ln_normed"), 20)

            def part(i, u, early, scores, project, work, out):
                for g in range(2) if early else range(2, 5):
                    if scores:
                        att_scores(pe, i, u + 1, g)
                    if project and g % 2 == 0:
                        att_project(pe, i, u + 2, g // 2)
                    if out and g == 0:
                        att_output(pe, i, u - 1)
                    if work and g:
                        att_transpose(pe, i, u, g - 1)
                if not early:
                    att_transpose(pe, i, u, 4)
                    att_values(pe, i, u)

            for g in range(3):
                att_project(pe, 0, 0, g)
            for g in range(5):
                att_scores(pe, 0, 0, g, first=True)
                if g < 3:
                    att_project(pe, 0, 1, g)
            att_loop(pe, part)

        def att_exps(act, i, u, g):
            par = u % 2
            act.wait_ge(sem("s_max"), i * (8 * UNROLL) + (8 * u + GCUM[g]))
            at = 0
            for j in GROUPS[g]:
                nc.scalar.activation(soft[par][:, POFF[j]:POFF[j] + keys(j)],
                                     bank[1 + (5 * par + g) % 2][:, at:at + keys(j)], ACT.Exp,
                                     bias=neg_max[:, par, j:j + 1], accum_out=exp_sum[:, par, j:j + 1]) \
                  .then_inc(sem("s_exp"), 1)
                at += keys(j)

        def att_v(act, i, u):
            act.wait_ge(sem("proj_raw"), i * (3 * UNROLL) + (3 * u + 3))
            nc.scalar.activation(v_tok[u % B][:, :, :], bank[0][:, :].rearrange("p (i c) -> p i c", i=TB), ACT.Copy) \
              .then_inc(sem("proj_read"), 1)

        def att_act(act):
            nc.scalar.preload_act_table_set("natural_log_exp_and_others")

            def transposed(i, u, f):
                if f == 0:
                    act.wait_ge(sem("pv_raw"), i * (2 * UNROLL) + (2 * u + B))
                act.wait_ge(sem("pt_raw"), i * (5 * UNROLL) + (5 * u + f + 1))
                nc.scalar.activation(softT[:, 512 * f:512 * f + 512], bank[3 + (u + f) % 2][:, :], ACT.Copy) \
                  .then_inc(sem("pt_ready"), 1)

            def part(i, u, early, scores, project, work, out):
                for g in range(2) if early else range(2, 5):
                    if scores:
                        att_exps(act, i, u + 1, g)
                    if work and g:
                        transposed(i, u, g - 1)
                if not early:
                    transposed(i, u, 4)
                    if project:
                        att_v(act, i, u + 2)

            att_v(act, 0, 0)
            for g in range(5):
                att_exps(act, 0, 0, g)
            att_v(act, 0, 1)
            att_loop(act, part)

        def att_rope(dve, i, u, piece, first=False):
            dve.wait_ge(sem("proj_raw"), i * (3 * UNROLL) + (3 * u + piece + 1))
            if not first:
                dve.wait_ge(sem("roped"), i * (5 * UNROLL) + (5 * u + (0 if piece else -2)))
            nc.vector.tensor_tensor(rope_part[2 * piece][:, :], bank[0][:, :], rope_tab[:, 2 * piece, :], ALU.mult)
            nc.vector.stream_shuffle(rope_part[2 * piece + 1][:, :], bank[0][:, :], SWAP) \
              .then_inc(sem("proj_read"), 1)

        def att_maxes(dve, i, u, g):
            par = u % 2
            dve.wait_ge(sem("s_raw"), i * (5 * UNROLL) + (5 * u + g + 1))
            at = 0
            for j in GROUPS[g]:
                s = bank[1 + (5 * par + g) % 2][:, at:at + keys(j)]
                nc.vector.tensor_tensor(s[:, keys(j) - 64:keys(j)], s[:, keys(j) - 64:keys(j)], att_mask[:, :],
                                        ALU.add).then_inc(sem("s_masked"), 1)
                at += keys(j)
            at = 0
            for k, j in enumerate(GROUPS[g]):
                s = bank[1 + (5 * par + g) % 2][:, at:at + keys(j)]
                dve.wait_ge(sem("s_masked"), i * (8 * UNROLL) + (8 * u + GCUM[g] - len(GROUPS[g]) + k + 1))
                nc.vector.tensor_reduce(neg_max[:, par, j:j + 1], s, AX_X, ALU.max, negate=True) \
                  .then_inc(sem("s_max"), 1)
                at += keys(j)

        def att_norm(dve, i, u):
            par = u % 2
            dve.wait_ge(sem("s_exp"), i * (8 * UNROLL) + (8 * u + 8))
            nc.vector.reciprocal(exp_inv[:, par, :], exp_sum[:, par, :]).then_inc(sem("s_inv"), 1)
            dve.wait_ge(sem("s_inv"), i * UNROLL + (u + 1))
            for j in range(NBLK):
                p = soft[par][:, POFF[j]:POFF[j] + keys(j)]
                last = nc.vector.tensor_scalar(p, p, exp_inv[:, par, j:j + 1], None, ALU.mult)
            last.then_inc(sem("p_normed"), 1)

        def att_heads(dve, i, u):
            for half in range(2):
                dve.wait_ge(sem("pv_raw"), i * (2 * UNROLL) + (2 * u + B + half + 1))
                for hd in range(2):
                    lo = 64 * hd
                    nc.vector.tensor_copy(
                        head_out[u % 2][lo:lo + 64, 256 * half:256 * half + 256].rearrange("p (j i) -> p j i", j=4),
                        bank[5 + half][lo:lo + 64, :].rearrange("p (j h i) -> p j h i", j=4, h=2)[:, :, hd, :]) \
                      .then_inc(sem("pv_read"), 1)

        def att_add(dve, i, u):
            b = u % B
            dve.wait_ge(sem("att_out"), i * UNROLL + (u + 1))
            dve.wait_ge(sem("pair_added"), i * UNROLL + (u + 1))
            nc.vector.scalar_tensor_tensor(x[:, b, :], bank[7][:, :], gate(4, b), x[:, b, :], ALU.mult, ALU.add) \
              .then_inc(sem("pair_added"), 1)

        def att_dve(dve):
            def part(i, u, early, scores, project, work, out):
                for g in range(2) if early else range(2, 5):
                    if scores:
                        att_maxes(dve, i, u + 1, g)
                    if project and g in (0, 2):
                        att_rope(dve, i, u + 2, g // 2)
                if out:
                    att_add(dve, i, u - 1)
                if not early:
                    if scores:
                        att_norm(dve, i, u + 1)
                    att_heads(dve, i, u)

            link(dve, "dve", nc.vector.tensor_scalar(gate_bo[:, :], mod[:, 2, 2, :], v("attn2_bo"), None, ALU.mult))
            for b in range(B):
                dve.wait_ge(sem("h_ready"), 16 + b + 1)
                nc.vector.tensor_scalar(x[:, b, :], x[:, b, :], gate_bo[:, b:b + 1], None, ALU.add) \
                  .then_inc(sem("pair_added"), 1)
            dve.wait_ge(sem("att_tables"), 32)
            dve.wait_ge(sem("soft_zeroed"), 4)
            for g in range(2):
                att_rope(dve, 0, 0, g, first=True)
            for g in range(5):
                att_maxes(dve, 0, 0, g)
                if g < 2:
                    att_rope(dve, 0, 1, g)
            att_norm(dve, 0, 0)
            att_loop(dve, part)

        def att_sum(pool, i, u, first=False):
            par = u % 2

            def rotated(k):
                pool.wait_ge(sem("roped"), i * (5 * UNROLL) + (5 * u + k))

            if not first:
                pool.wait_ge(sem("s_raw"), i * (5 * UNROLL) + (5 * u - 5))
            pool.wait_ge(sem("proj_read"), i * (3 * UNROLL) + (3 * u + 1))
            nc.gpsimd.tensor_tensor(rope_part[1][:, :], rope_part[1][:, :], rope_tab[:, 1, :], ALU.mult) \
              .then_inc(sem("roped"), 1)
            for hd in range(2):
                lo = 64 * hd
                rotated(1 + hd)
                nc.gpsimd.tensor_tensor(q_diag[par][lo:lo + 64, :, lo:lo + 64],
                                        rope_part[0][lo:lo + 64, :].rearrange("p (j i) -> p j i", i=64),
                                        rope_part[1][lo:lo + 64, :].rearrange("p (j i) -> p j i", i=64), ALU.add) \
                  .then_inc(sem("roped"), 1)
            pool.wait_ge(sem("proj_read"), i * (3 * UNROLL) + (3 * u + 2))
            rotated(3)
            nc.gpsimd.tensor_tensor(rope_part[3][:, :], rope_part[3][:, :], rope_tab[:, 3, :], ALU.mult) \
              .then_inc(sem("roped"), 1)
            rotated(4)
            nc.gpsimd.tensor_tensor(k_rope[par][:, :], rope_part[2][:, :], rope_part[3][:, :], ALU.add) \
              .then_inc(sem("roped"), 1)

        def att_pool(pool):
            def part(i, u, early, scores, project, work, out):
                if project and not early:
                    att_sum(pool, i, u + 2)

            for i in range(2):
                nc.gpsimd.memset(soft[i][:, :], 0.0).then_inc(sem("soft_zeroed"), 1)
                nc.gpsimd.memset(q_diag[i][:, :, :], 0.0).then_inc(sem("soft_zeroed"), 1)
            pool.wait_ge(sem("soft_zeroed"), 4)
            pool.wait_ge(sem("att_tables"), 32)
            att_sum(pool, 0, 0, first=True)
            att_sum(pool, 0, 1, first=True)
            att_loop(pool, part)

        def att_sp(sp):
            sp.wait_ge(sem("h_ready"), 17)
            for p in range(2):
                sp.dma_start(att_w[p][:, :, :], d["att_w"][p, :, :, :]).then_inc(sem(f"w_loaded{p}"), 16)
            sp.dma_start(rope_tab[:, :, :], d["rope_tab"]).then_inc(sem("att_tables"), 16)
            sp.dma_start(att_mask[:, :], d["att_mask"]).then_inc(sem("att_tables"), 16)
            sp.dma_start(att_wo[:, :], d["att_wo"][0, :, :]).then_inc(sem("wo_loaded"), 16)

            def next_wo(i, p):
                sp.wait_ge(sem("att_out"), i * UNROLL + (B * p + B))
                wo = d["att_wo"][i * 2 + p + 1, :, :] if isinstance(i, int) else \
                    d["att_wo"][bass.ds(i * 2 + (p + 1), 1), :, :].rearrange("o p n -> (o p) n")
                sp.dma_start(att_wo[:, :], wo).then_inc(sem("wo_loaded"), 16)

            with sp.Fori(0, PAIRS // 2 - 1) as i:
                for p in range(2):
                    sp.wait_ge(sem("proj_raw"), i * (3 * UNROLL) + (12 * p + 12))
                    sp.dma_start(att_w[p][:, :, :], d["att_w"][bass.ds(i * 2 + (p + 2), 1), :, :, :]
                                 .rearrange("o p j n -> (o p) j n")).then_inc(sem(f"w_loaded{p}"), 16)
                    next_wo(i, p)
            next_wo(PAIRS // 2 - 1, 0)

        next_block()
        mix_prev = tmp_sb("mix_prev", [C, 2, T])
        mix_r = tmp_sb("mix_r", [C, 2, T])
        mix_k = tmp_sb("mix_k", [C, 2, T])
        mix_gate = tmp_sb("mix_gate", [C, 2, T])
        mix_relu = tmp_sb("mix_relu", [C, 2, T])
        mix_w = tmp_sb("mix_w", [C, 3, C])

        def mix_sp(sp):
            sp.wait_ge(sem("h_ready"), 21)
            sp.dma_start(mix_w[:, :, :], d["mix_w"]).then_inc(sem("mix_loaded"), 16)

        def mix_dve(dve):
            def inputs(b):
                dve.wait_ge(sem("h_ready"), 20 + b + 1)
                if b >= 2:
                    dve.wait_ge(sem("mix_kr"), b - 1)
                now, prev = hb(b), hh(b, -1, T)
                link(dve, "dve", nc.vector.tensor_tensor(mix_prev[:, b % 2, :], now, prev, ALU.subtract))
                for dst, mu in ((mix_r, "mu_r"), (mix_k, "mu_k")):
                    nc.vector.scalar_tensor_tensor(dst[:, b % 2, :], mix_prev[:, b % 2, :], v(mu), prev,
                                                   ALU.mult, ALU.add).then_inc(sem("mix_in"), 1)
                dve.wait_ge(sem("mix_in"), 2 * b + 2)

            inputs(0)
            for b in range(B):
                if b + 1 < B:
                    inputs(b + 1)
                dve.wait_ge(sem("mix_relued"), b + 1)
                nc.vector.tensor_tensor(mix_relu[:, b % 2, :], mix_relu[:, b % 2, :], mix_relu[:, b % 2, :],
                                        ALU.mult).then_inc(sem("mix_squared"), 1)
                dve.wait_ge(sem("mix_v"), b + 1)
                dve.wait_ge(sem("mix_gated"), b + 1)
                link(dve, "dve", nc.vector.tensor_tensor(mix_gate[:, b % 2, :], bank[6][:, :], mix_gate[:, b % 2, :],
                                                         ALU.mult))
                nc.vector.scalar_tensor_tensor(x[:, b, :], mix_gate[:, b % 2, :], gate(5, b), x[:, b, :],
                                               ALU.mult, ALU.add).then_inc(sem("x_ready"), 1)

        def mix_act(act):
            for b in range(B):
                if b >= 2:
                    act.wait_ge(sem("x_ready"), 16 + b - 1)
                act.wait_ge(sem("mix_kr"), b + 1)
                nc.scalar.activation(mix_relu[:, b % 2, :], bank[4][:, :], ACT.Relu).then_inc(sem("mix_relued"), 1)
                nc.scalar.activation(mix_gate[:, b % 2, :], bank[5][:, :], ACT.Sigmoid).then_inc(sem("mix_gated"), 1)

        def mix_pe(pe):
            pe.wait_ge(sem("mix_loaded"), 16)
            for b in range(B):
                pe.wait_ge(sem("mix_in"), 2 * b + 2)
                if b:
                    pe.wait_ge(sem("mix_relued"), b)
                    pe.wait_ge(sem("mix_gated"), b)
                pe.matmul(bank[4][:, :], mix_w[:, 1, :], mix_k[:, b % 2, :], start=True, stop=True)
                pe.matmul(bank[5][:, :], mix_w[:, 0, :], mix_r[:, b % 2, :], start=True, stop=True) \
                  .then_inc(sem("mix_kr"), 1)
                pe.wait_ge(sem("mix_squared"), b + 1)
                if b:
                    pe.wait_ge(sem("x_ready"), 16 + b)
                pe.matmul(bank[6][:, :], mix_w[:, 2, :], mix_relu[:, b % 2, :], start=True, stop=True) \
                  .then_inc(sem("mix_v"), 1)

        class Window:
            def __init__(self, units, start, per, loaded, tables=None, slopes=False):
                self.units, self.start, self.per = units, start, per
                self.loaded = loaded
                self.tables, self.slopes = tables, slopes
                self.ssq_reader = "win_clip" if per["win_clip"] else "win_log"

            def at(self, name, i, u, k=0):
                return i * (UNROLL * self.per[name]) + (u * self.per[name] + self.start[name] + k)

            def after(self):
                return {m: self.start[m] + self.units * c for m, c in self.per.items()}

        ROTATED = {"win_proj": 4, "win_proj_read": 2, "win_v_read": 2, "win_sq": 2, "win_ssq": 2, "win_clip": 2, "win_log": 2,
                   "win_rs": 2, "win_sum": 4, "win_q": 2, "win_k": 1, "win_s": 2, "win_biased": 2, "win_max": 2,
                   "win_exp": 8, "win_inv": 1, "win_normed": 1, "win_pt": 2, "win_pt_read": 2, "pv_raw": 2,
                   "win_pv_read": 4, "win_out": 1, "pair_added": 1}
        PLAIN = dict(ROTATED, win_proj=1, win_proj_read=0, win_v_read=0, win_sq=1, win_ssq=1, win_clip=0, win_log=1, win_rs=1,
                     win_sum=0, win_k=0)

        def win_alloc(pieces, own_kv):
            a = {"q": [tmp_sb(f"win_q{i}_{pieces}", [128, NBLK, 128]) for i in range(2)],
                 "soft": [tmp_sb(f"win_soft{i}_{pieces}", [128, NBLK, 128]) for i in range(2)],
                 "softT": tmp_sb(f"win_softT_{pieces}", [128, NBLK * 128]),
                 "neg_max": tmp_sb(f"win_neg_max_{pieces}", [128, 2, NBLK]),
                 "sum": tmp_sb(f"win_sum_{pieces}", [128, 2, NBLK]),
                 "inv": tmp_sb(f"win_inv_{pieces}", [128, 2, NBLK]),
                 "out": [tmp_sb(f"win_out{i}_{pieces}", [128, T]) for i in range(2)],
                 "w": [tmp_sb(f"win_w{i}_{pieces}", [C, pieces, 128]) for i in range(2)],
                 "wo": tmp_sb(f"win_wo_{pieces}", [128, C]),
                 "bias": tmp_sb(f"win_bias_{pieces}", [128, NBLK, 128]),
                 "sq": tmp_sb(f"win_sq_{pieces}", [128, 2, T]),
                 "log": tmp_sb(f"win_log_{pieces}", [128, 2, T]),
                 "rs": tmp_sb(f"win_rs_{pieces}", [128, 2, T])}
            if own_kv:
                a["part"] = [tmp_sb(f"win_part{i}", [128, T]) for i in range(4)]
                a["k"] = [tmp_sb(f"win_k{i}", [128, TP]) for i in range(2)]
                a["v"] = [tmp_sb(f"win_v{i}", [128, NBLK, 128]) for i in range(B)]
            return a

        def proj_bank(W, u, piece):
            return bank[5 * ((u if W.per["win_proj"] == 1 else piece) % 2)]

        def win_loop(W, eng, part):
            for early in (True, False):
                part(0, -2, early, False, True, False, False, True)
            for early in (True, False):
                part(0, -1, early, True, True, False, False, True)
            part(0, 0, True, True, True, True, False, False)
            rounds = W.units // UNROLL
            with eng.Fori(0, rounds - 1) as i:
                for u in range(UNROLL):
                    part(i, u, False, True, True, True, False, False)
                    part(i, u + 1, True, True, True, True, True, False)
            for u in range(UNROLL):
                left = UNROLL - 1 - u
                part(rounds - 1, u, False, left >= 1, left >= 2, True, False, False)
                part(rounds - 1, u + 1, True, left >= 2, left >= 3, left >= 1, True, False)

        def win_pe(pe, W, a, tokens, keys_of, values_of):
            pieces = W.per["win_proj"]

            def project(i, u, piece, first):
                b, p = u % B, u // B % 2
                pe.wait_ge(sem(f"w_loaded{p}"), i * 16 + (16 * (u // UNROLL) + 16 + 8 * W.loaded))
                dst = proj_bank(W, u, piece)
                if pieces == 1:
                    if not first:
                        pe.wait_ge(sem("win_q"), W.at("win_q", i, u, -2))
                elif piece >= 2:
                    pe.wait_ge(sem("win_proj_read"), W.at("win_proj_read", i, u, piece - 1))
                elif u or not first:
                    pe.wait_ge(sem("win_v_read"), W.at("win_v_read", i, u, piece - 1))
                if piece < 2:
                    last = pe.matmul(dst[:, :], a["w"][p][:, piece, :], tokens(b, 0, T), start=True, stop=True)
                else:
                    for k in range(4):
                        j = 4 * (piece - 2) + k
                        last = pe.matmul(dst[:, 128 * k:128 * k + 128], tokens(b, 64 * j - 64, 128),
                                         a["w"][p][:, 2, :], start=True, stop=True)
                last.then_inc(sem("win_proj"), 1)

            def square_sum(i, u, j, first):
                pe.wait_ge(sem("win_sq"), W.at("win_sq", i, u, j + 1))
                if j or u or not first:
                    pe.wait_ge(sem(W.ssq_reader), W.at(W.ssq_reader, i, u, j))
                pe.matmul(bank[1][:, :], head_sum[:, :], a["sq"][:, j, :], start=True, stop=True) \
                  .then_inc(sem("win_ssq"), 1)

            def scores(i, u, half, first):
                if half == 0:
                    pe.wait_ge(sem("win_q"), W.at("win_q", i, u, 2))
                    if W.per["win_k"]:
                        pe.wait_ge(sem("win_k"), W.at("win_k", i, u, 1))
                if not first:
                    pe.wait_ge(sem("win_exp"), W.at("win_exp", i, u, 4 * half - 4))
                for j in range(4 * half, 4 * half + 4):
                    last = pe.matmul(bank[2 + half][:, 128 * (j % 4):128 * (j % 4) + 128], a["q"][u % 2][:, j, :],
                                     keys_of(u % UNROLL, j), start=True, stop=True)
                last.then_inc(sem("win_s"), 1)

            def transpose(i, u, half):
                if half == 0:
                    pe.wait_ge(sem("win_normed"), W.at("win_normed", i, u, 1))
                else:
                    pe.wait_ge(sem("win_pt_read"), W.at("win_pt_read", i, u, 1))
                for j in range(4 * half, 4 * half + 4):
                    last = pe.transpose(bank[4][:, 128 * (j % 4):128 * (j % 4) + 128],
                                        a["soft"][u % 2][:, j, :], ident[:, :])
                last.then_inc(sem("win_pt"), 1)

            def values(i, u, half):
                if half == 0:
                    pe.wait_ge(sem("pair_added"), W.at("pair_added", i, u))
                pe.wait_ge(sem("win_pt_read"), W.at("win_pt_read", i, u, half + 1))
                for j in range(4 * half, 4 * half + 4):
                    last = pe.matmul(bank[6 + half][:, 128 * (j % 4):128 * (j % 4) + 128],
                                     values_of(u % UNROLL, j), a["softT"][:, 128 * j:128 * j + 128],
                                     start=True, stop=True)
                last.then_inc(sem("pv_raw"), 1)

            def output(i, u):
                pe.wait_ge(sem("wo_loaded"), i * (16 * UNROLL // B) + (16 * (u // B) + 16 + 16 * W.loaded))
                pe.wait_ge(sem("win_pv_read"), W.at("win_pv_read", i, u, 4))
                pe.matmul(bank[6][:, :], a["wo"][:, :], a["out"][u % 2][:, :], start=True, stop=True) \
                  .then_inc(sem("win_out"), 1)

            def part(i, u, early, s, p, work, out, first):
                if early:
                    if p:
                        project(i, u + 2, 0, first)
                    if s:
                        scores(i, u + 1, 0, first)
                    if p and pieces > 1:
                        project(i, u + 2, 1, first)
                    if out:
                        output(i, u - 1)
                    if work:
                        transpose(i, u, 0)
                    return
                if s:
                    scores(i, u + 1, 1, first)
                if p and pieces > 1:
                    square_sum(i, u + 2, 0, first)
                if work:
                    transpose(i, u, 1)
                if p and pieces > 1:
                    project(i, u + 2, 2, first)
                    square_sum(i, u + 2, 1, first)
                elif p:
                    square_sum(i, u + 2, 0, first)
                if work:
                    values(i, u, 0)
                if p and pieces > 1:
                    project(i, u + 2, 3, first)
                if work:
                    values(i, u, 1)

            win_loop(W, pe, part)

        def win_act(act, W, a):
            pieces = W.per["win_proj"]
            nc.scalar.preload_act_table_set("natural_log_exp_and_others")

            def square(i, u, j, first):
                act.wait_ge(sem("win_proj"), W.at("win_proj", i, u, j + 1))
                if not first:
                    act.wait_ge(sem("win_ssq"), W.at("win_ssq", i, u, j + 1 - W.per["win_ssq"]))
                nc.scalar.activation(a["sq"][:, j, :], proj_bank(W, u, j)[:, :], ACT.Square).then_inc(sem("win_sq"), 1)

            def norm(i, u, j, first):
                if W.per["win_clip"]:
                    act.wait_ge(sem("win_clip"), W.at("win_clip", i, u, j + 1))
                    nc.scalar.activation(a["log"][:, j, :], a["sq"][:, j, :], ACT.Ln).then_inc(sem("win_log"), 1)
                else:
                    act.wait_ge(sem("win_ssq"), W.at("win_ssq", i, u, j + 1))
                    nc.scalar.activation(a["log"][:, j, :], bank[1][:, :], ACT.Ln, bias=rms_eps[:, 0:1],
                                         scale=1.0 / 64).then_inc(sem("win_log"), 1)
                act.wait_ge(sem("win_log"), W.at("win_log", i, u, j + 1))
                if not first:
                    name = "win_k" if j else "win_q"
                    act.wait_ge(sem(name), W.at(name, i, u))
                bias = ln_clip[:, 0:1] if W.per["win_clip"] else 0.0
                nc.scalar.activation(a["rs"][:, j, :], a["log"][:, j, :], ACT.Exp, scale=-0.5, bias=bias) \
                  .then_inc(sem("win_rs"), 1)

            def exps(i, u, half):
                act.wait_ge(sem("win_max"), W.at("win_max", i, u, half + 1))
                for k in range(4):
                    j = 4 * half + k
                    nc.scalar.activation(a["soft"][u % 2][:, j, :], bank[2 + half][:, 128 * k:128 * k + 128], ACT.Exp,
                                         bias=a["neg_max"][:, u % 2, j:j + 1], accum_out=a["sum"][:, u % 2, j:j + 1]) \
                      .then_inc(sem("win_exp"), 1)

            def transposed(i, u, half):
                if half == 0:
                    act.wait_ge(sem("pv_raw"), W.at("pv_raw", i, u))
                act.wait_ge(sem("win_pt"), W.at("win_pt", i, u, half + 1))
                nc.scalar.activation(a["softT"][:, 512 * half:512 * half + 512], bank[4][:, :], ACT.Copy) \
                  .then_inc(sem("win_pt_read"), 1)

            def take_values(i, u, half):
                act.wait_ge(sem("win_proj"), W.at("win_proj", i, u, 3 + half))
                nc.scalar.activation(a["v"][u % B][:, 4 * half:4 * half + 4, :],
                                     proj_bank(W, u, half)[:, :].rearrange("p (i c) -> p i c", i=4), ACT.Copy) \
                  .then_inc(sem("win_v_read"), 1)

            def heads(i, u):
                act.wait_ge(sem("pv_raw"), W.at("pv_raw", i, u, 2))
                for hd in range(2):
                    dst, src = win_head(a, u, 1, hd)
                    nc.scalar.activation(dst, src, ACT.Copy).then_inc(sem("win_pv_read"), 1)

            def part(i, u, early, s, p, work, out, first):
                if early:
                    if p:
                        square(i, u + 2, 0, first)
                        if pieces > 1:
                            square(i, u + 2, 1, first)
                    if s:
                        exps(i, u + 1, 0)
                    if work:
                        transposed(i, u, 0)
                elif pieces > 1:
                    if p:
                        norm(i, u + 2, 0, first)
                    if work:
                        transposed(i, u, 1)
                    if p:
                        take_values(i, u + 2, 0)
                        norm(i, u + 2, 1, first)
                    if s:
                        exps(i, u + 1, 1)
                    if p:
                        take_values(i, u + 2, 1)
                    if work:
                        heads(i, u)
                else:
                    if work:
                        transposed(i, u, 1)
                    if s:
                        exps(i, u + 1, 1)
                    if p:
                        norm(i, u + 2, 0, first)
                    if work:
                        heads(i, u)

            win_loop(W, act, part)

        def win_head(a, u, half, hd):
            lo = 64 * hd
            return (a["out"][u % 2][lo:lo + 64, 256 * half:256 * half + 256].rearrange("p (j i) -> p j i", j=4),
                    bank[6 + half][lo:lo + 64, :].rearrange("p (j h i) -> p j h i", j=4, h=2)[:, :, hd, :])

        def win_dve(dve, W, a, scales, add):
            pieces = W.per["win_proj"]

            def maxes(i, u, half):
                dve.wait_ge(sem("win_s"), W.at("win_s", i, u, half + 1))
                s = bank[2 + half][:, :].rearrange("p (j k) -> p j k", j=4)
                t = a["bias"][:, 4 * half:4 * half + 4, :]
                if W.slopes:
                    slope = vec[:, bass.ds(i * (UNROLL // B) + (u // B + VEC["slope"][0]), 1)]
                    ins = nc.vector.scalar_tensor_tensor(s, t, slope, s, ALU.mult, ALU.add)
                else:
                    ins = nc.vector.tensor_tensor(s, s, t, ALU.add)
                ins.then_inc(sem("win_biased"), 1)
                dve.wait_ge(sem("win_biased"), W.at("win_biased", i, u, half + 1))
                nc.vector.tensor_reduce(a["neg_max"][:, u % 2, 4 * half:4 * half + 4], s, AX_X, ALU.max, negate=True) \
                  .then_inc(sem("win_max"), 1)

            def to_diagonal(i, u, src, weight):
                dve.wait_ge(sem("win_rs"), W.at("win_rs", i, u, 1))
                for hd in range(2):
                    lo = 64 * hd
                    out_ = a["q"][u % 2][lo:lo + 64, :, lo:lo + 64]
                    q = src[lo:lo + 64, :].rearrange("p (j i) -> p j i", i=64)
                    rs = a["rs"][lo:lo + 64, 0, :].rearrange("p (j i) -> p j i", i=64)
                    if weight is None:
                        ins = nc.vector.tensor_tensor(out_, q, rs, ALU.mult)
                    else:
                        ins = nc.vector.scalar_tensor_tensor(out_, q, weight[lo:lo + 64, :], rs, ALU.mult, ALU.mult)
                    ins.then_inc(sem("win_q"), 1)

            def rotate(i, u, piece, first):
                dve.wait_ge(sem("win_sq"), W.at("win_sq", i, u, piece + 1))
                if u or not first:
                    if piece:
                        dve.wait_ge(sem("win_k"), W.at("win_k", i, u))
                    else:
                        dve.wait_ge(sem("win_sum"), W.at("win_sum", i, u, -2))
                        dve.wait_ge(sem("win_q"), W.at("win_q", i, u))
                src = proj_bank(W, u, piece)[:, :]
                nc.vector.tensor_tensor(a["part"][2 * piece][:, :], src, W.tables[:, 2 * piece, :], ALU.mult)
                nc.vector.stream_shuffle(a["part"][2 * piece + 1][:, :], src, SWAP).then_inc(sem("win_proj_read"), 1)

            def clip(i, u, j):
                dve.wait_ge(sem("win_ssq"), W.at("win_ssq", i, u, j + 1))
                nc.vector.tensor_scalar(a["sq"][:, j, :], bank[1][:, :], 1e-24, 2.0 ** 30, ALU.max, ALU.mult) \
                  .then_inc(sem("win_clip"), 1)

            def inverse(i, u):
                dve.wait_ge(sem("win_exp"), W.at("win_exp", i, u, 8))
                nc.vector.reciprocal(a["inv"][:, u % 2, :], a["sum"][:, u % 2, :]).then_inc(sem("win_inv"), 1)

            def heads(i, u):
                dve.wait_ge(sem("pv_raw"), W.at("pv_raw", i, u, 1))
                for hd in range(2):
                    dst, src = win_head(a, u, 0, hd)
                    nc.vector.tensor_copy(dst, src).then_inc(sem("win_pv_read"), 1)

            def output(i, u):
                dve.wait_ge(sem("win_out"), W.at("win_out", i, u, 1))
                dve.wait_ge(sem("pair_added"), W.at("pair_added", i, u))
                add(u % B).then_inc(sem("pair_added"), 1)

            def part(i, u, early, s, p, work, out, first):
                if early:
                    if p and pieces > 1:
                        rotate(i, u + 2, 0, first)
                    if s:
                        maxes(i, u + 1, 0)
                    if p and pieces > 1:
                        rotate(i, u + 2, 1, first)
                    if out:
                        output(i, u - 1)
                elif pieces > 1:
                    if p:
                        clip(i, u + 2, 0)
                    if s:
                        maxes(i, u + 1, 1)
                    if p:
                        clip(i, u + 2, 1)
                        dve.wait_ge(sem("win_sum"), W.at("win_sum", i, u + 2, 2))
                        to_diagonal(i, u + 2, a["part"][0], None)
                    if s:
                        inverse(i, u + 1)
                    if work:
                        heads(i, u)
                else:
                    if s:
                        maxes(i, u + 1, 1)
                        inverse(i, u + 1)
                    if p:
                        to_diagonal(i, u + 2, proj_bank(W, u + 2, 0), scales[0])
                    if work:
                        heads(i, u)

            win_loop(W, dve, part)

        def win_pool(pool, W, a):
            pieces = W.per["win_proj"]

            def sum_of(i, u, j):
                swapped = a["part"][2 * j + 1][:, :]
                pool.wait_ge(sem("win_proj_read"), W.at("win_proj_read", i, u, j + 1))
                nc.gpsimd.tensor_tensor(swapped, swapped, W.tables[:, 2 * j + 1, :], ALU.mult) \
                  .then_inc(sem("win_sum"), 1)
                pool.wait_ge(sem("win_sum"), W.at("win_sum", i, u, 2 * j + 1))
                nc.gpsimd.tensor_tensor(a["part"][2 * j][:, :], a["part"][2 * j][:, :], swapped,
                                        ALU.add).then_inc(sem("win_sum"), 1)

            def key(i, u, first):
                pool.wait_ge(sem("win_sum"), W.at("win_sum", i, u, 4))
                pool.wait_ge(sem("win_rs"), W.at("win_rs", i, u, 2))
                if not first:
                    pool.wait_ge(sem("win_s"), W.at("win_s", i, u, -2))
                nc.gpsimd.tensor_tensor(a["k"][u % 2][:, PAD:TP], a["part"][2][:, :], a["rs"][:, 1, :], ALU.mult) \
                  .then_inc(sem("win_k"), 1)

            def divide(i, u):
                pool.wait_ge(sem("win_inv"), W.at("win_inv", i, u, 1))
                nc.gpsimd.tensor_tensor(a["soft"][u % 2][:, :, :], a["soft"][u % 2][:, :, :],
                                        a["inv"][:, u % 2, :].unsqueeze(2).to_broadcast([128, NBLK, 128]),
                                        ALU.mult).then_inc(sem("win_normed"), 1)

            def part(i, u, early, s, p, work, out, first):
                if not early:
                    if p and pieces > 1:
                        sum_of(i, u + 2, 0)
                        sum_of(i, u + 2, 1)
                        key(i, u + 2, first)
                    if s:
                        divide(i, u + 1)

            win_loop(W, pool, part)

        def win_sp(sp, W, a, w_of, wo_of):
            for p in range(2):
                sp.dma_start(a["w"][p][:, :, :], w_of(p)).then_inc(sem(f"w_loaded{p}"), 16)
            sp.dma_start(a["wo"][:, :], wo_of(0)).then_inc(sem("wo_loaded"), 16)

            def next_wo(i, p):
                sp.wait_ge(sem("win_out"), W.at("win_out", i, B * p + B))
                sp.dma_start(a["wo"][:, :], wo_of(i * 2 + (p + 1))).then_inc(sem("wo_loaded"), 16)

            rounds = W.units // UNROLL
            with sp.Fori(0, rounds - 1) as i:
                for p in range(2):
                    sp.wait_ge(sem("win_proj"), W.at("win_proj", i, B * p + B))
                    sp.dma_start(a["w"][p][:, :, :], w_of(i * 2 + (p + 2))).then_inc(sem(f"w_loaded{p}"), 16)
                    next_wo(i, p)
            next_wo(rounds - 1, 0)

        next_block()
        kv_k = [tmp_sb(f"kv_k{i}", [128, B, TP]) for i in range(2)]
        kv_v = [tmp_sb(f"kv_v{b}", [128, NBLK, 256]) for b in range(B)]
        kv_w = tmp_sb("kv_w", [C, 2, 256])
        kv_sq = tmp_sb("kv_sq", [128, 2, T])
        kv_log = tmp_sb("kv_log", [128, 2, T])
        kv_rs = tmp_sb("kv_rs", [128, 2, T])
        q_w8 = tmp_sb("q_w8", [128, 1])
        A6 = win_alloc(1, False)
        start = dict({m: 0 for m in PLAIN}, pv_raw=B + 2 * B * PAIRS, pair_added=B + B * PAIRS)
        W6 = Window(PAIRS * B, start, PLAIN, PAIRS, slopes=True)

        def kv_pe(pe):
            pe.wait_ge(sem("h_ready"), 28)
            pe.wait_ge(sem("ln_normed"), 28)
            pe.wait_ge(sem("kv_loaded"), 48)

            def key(j):
                if j >= 2:
                    pe.wait_ge(sem("kv_key"), j - 1)
                pe.matmul(bank[j % 2][:, :], kv_w[:, 0, 128 * (j % 2):128 * (j % 2) + 128], hb(j // 2),
                          start=True, stop=True).then_inc(sem("kv_raw"), 1)

            key(0)
            for j in range(2 * B):
                if j + 1 < 2 * B:
                    key(j + 1)
                for f in (2 * j, 2 * j + 1):
                    if f >= 4:
                        pe.wait_ge(sem("kv_v_read"), f - 3)
                    for i in range(2):
                        blk = 2 * (f % 4) + i
                        last = pe.matmul(bank[4 + f % 4][:, 256 * i:256 * i + 256], hh(f // 4, 64 * blk - 64, 128),
                                         kv_w[:, 1, :], start=True, stop=True)
                    last.then_inc(sem("kv_v_raw"), 1)
                pe.wait_ge(sem("kv_squared"), j + 1)
                if j >= 2:
                    pe.wait_ge(sem("kv_logged"), j - 1)
                pe.matmul(bank[2 + j % 2][:, :], head_sum[:, :], kv_sq[:, j % 2, :], start=True, stop=True) \
                  .then_inc(sem("kv_ssq"), 1)

        def kv_act(act):
            for j in range(2 * B):
                act.wait_ge(sem("kv_raw"), j + 1)
                if j >= 2:
                    act.wait_ge(sem("kv_ssq"), j - 1)
                nc.scalar.activation(kv_sq[:, j % 2, :], bank[j % 2][:, :], ACT.Square).then_inc(sem("kv_squared"), 1)
                for f in (2 * j, 2 * j + 1):
                    act.wait_ge(sem("kv_v_raw"), f + 1)
                    nc.scalar.activation(kv_v[f // 4][:, 2 * (f % 4):2 * (f % 4) + 2, :],
                                         bank[4 + f % 4][:, :].rearrange("p (i c) -> p i c", i=2), ACT.Copy) \
                      .then_inc(sem("kv_v_read"), 1)
                act.wait_ge(sem("kv_ssq"), j + 1)
                nc.scalar.activation(kv_log[:, j % 2, :], bank[2 + j % 2][:, :], ACT.Ln, bias=rms_eps[:, 0:1],
                                     scale=1.0 / 64).then_inc(sem("kv_logged"), 1)
                act.wait_ge(sem("kv_logged"), j + 1)
                if j >= 2:
                    act.wait_ge(sem("kv_key"), j - 1)
                nc.scalar.activation(kv_rs[:, j % 2, :], kv_log[:, j % 2, :], ACT.Exp, scale=-0.5) \
                  .then_inc(sem("kv_rs_ready"), 1)

        def kv_dve(dve):
            link(dve, "dve", nc.vector.tensor_scalar(q_w8[:, :], v("qn_w"), 0.125, None, ALU.mult))
            for i in range(2):
                link(dve, "dve", nc.vector.memset(A6["q"][i][:, :, :], 0.0))
                link(dve, "dve", nc.vector.memset(kv_k[i][:, :, 0:PAD], 0.0))
            for j in range(2 * B):
                dve.wait_ge(sem("kv_rs_ready"), j + 1)
                nc.vector.scalar_tensor_tensor(kv_k[j % 2][:, j // 2, PAD:TP], bank[j % 2][:, :], v("kn_w"),
                                               kv_rs[:, j % 2, :], ALU.mult, ALU.mult).then_inc(sem("kv_key"), 1)
            dve.wait_ge(sem("win_bias_loaded"), 16)

        def alibi_pe(pe):
            pe.wait_ge(sem("kv_key"), 2 * B)
            pe.wait_ge(sem("kv_v_read"), 4 * B)
            win_pe(pe, W6, A6, tokens=lambda b, lo, n: hh(b, lo, n),
                   keys_of=lambda u, j: kv_k[u // B][:, u % B, 64 * j:64 * j + 128],
                   values_of=lambda u, j: kv_v[u % B][:, j, 128 * (u // B):128 * (u // B) + 128])

        def alibi_dve(dve):
            win_dve(dve, W6, A6, [q_w8[:, 0:1]],
                    lambda b: nc.vector.scalar_tensor_tensor(x[:, b, :], bank[6][:, :], gate(6, b), x[:, b, :],
                                                             ALU.mult, ALU.add))

        def alibi_sp(sp):
            sp.wait_ge(sem("h_ready"), 25)
            sp.dma_start(kv_w[:, 0, :], d["kv_w"][:, 0, :]).then_inc(sem("kv_loaded"), 16)
            sp.dma_start(kv_w[:, 1, :], d["kv_w"][:, 1, :]).then_inc(sem("kv_loaded"), 16)
            sp.dma_start(A6["bias"][:, :, :], d["alibi_rel"]).then_inc(sem("win_bias_loaded"), 16)

            def one(name, i):
                return d[name][i, :, :] if isinstance(i, int) else \
                    d[name][bass.ds(i, 1), :, :].rearrange("o p n -> (o p) n")

            win_sp(sp, W6, A6, lambda i: one("alibi_wq", i).rearrange("p (j n) -> p j n", j=1),
                   lambda i: one("alibi_wo", i))

        next_block()
        shifted = tmp_sb("shifted", [C, B, TP])
        A7 = win_alloc(3, True)
        qk_tab = tmp_sb("qk_tab", [128, 4, T])
        scaled_tab = tmp_sb("scaled_tab", [128, 4, T])
        w1 = tmp_sb("w1", [C, 2, 2 * HID])
        w2 = tmp_sb("w2", [128, 2, 3, C])
        mlp_gelu = [tmp_sb(f"mlp_gelu{i}", [128, T]) for i in range(2)]
        mlp_hid = A7["part"][0:3]
        mlp_in = [A7["v"][b][:, :, :].rearrange("p j c -> p (j c)")[:, 0:T] for b in range(B)]
        layers = []
        for l in range(2):
            layers.append(Window(4 * B, (layers[-1] if l else W6).after(), ROTATED, 2 * PAIRS + 4 * l, tables=scaled_tab))

        def shift_dve(dve, l, sub):
            if sub:
                dve.wait_ge(sem("pair_added"), layers[l].after()["pair_added"])
            for b in range(B):
                if l == 0 and sub == 0:
                    dve.wait_ge(sem("h_ready"), 28 + b + 1)
                lo, hi = shifted[0:64, b, PAD:TP], shifted[64:128, b, PAD:TP]
                nc.vector.tensor_copy(lo, h[0:64, b, PAD:TP])
                nc.vector.tensor_copy(hi, h[64:128, b, PAD - 1:TP - 1]).then_inc(sem("shifted"), 1)

        def scale_tables(dve, l):
            for j, name in enumerate(("q_scale", "q_scale_rot", "k_scale", "k_scale_rot")):
                link(dve, "dve", nc.vector.tensor_scalar(scaled_tab[:, j, :], qk_tab[:, j, :], v(name, l), None, ALU.mult))

        def local_pe(pe, l):
            pe.wait_ge(sem("shifted"), 8 * l + B)
            if l == 0:
                pe.wait_ge(sem("ln_normed"), 32)
                pe.wait_ge(sem("local_cleared"), 5)
            win_pe(pe, layers[l], A7, tokens=lambda b, lo, n: shifted[:, b, PAD + lo:PAD + lo + n],
                   keys_of=lambda u, j: A7["k"][u % 2][:, 64 * j:64 * j + 128],
                   values_of=lambda u, j: A7["v"][u % B][:, j, :])

        def local_dve(dve, l):
            win_dve(dve, layers[l], A7, None,
                    lambda b: nc.vector.tensor_tensor(hb(b), hb(b), bank[6][:, :], ALU.add))

        def clear_dve(dve):
            nc.vector.memset(shifted[:, :, 0:PAD], 0.0).then_inc(sem("local_cleared"), 1)
            for i in range(2):
                nc.vector.memset(A7["q"][i][:, :, :], 0.0).then_inc(sem("local_cleared"), 1)
                nc.vector.memset(A7["k"][i][:, 0:PAD], 0.0).then_inc(sem("local_cleared"), 1)
            dve.wait_ge(sem("local_cleared"), 5)
            dve.wait_ge(sem("win_bias_loaded"), 32)
            dve.wait_ge(sem("local_loaded"), 48)

        def local_sp(sp):
            sp.wait_ge(sem("h_ready"), 29)
            sp.dma_start(A7["bias"][:, :, :], d["local_mask"]).then_inc(sem("win_bias_loaded"), 16)
            sp.dma_start(qk_tab[:, :, :], d["qk_tab"]).then_inc(sem("local_loaded"), 16)
            sp.dma_start(w1[:, :, :], d["local_w1"]).then_inc(sem("local_loaded"), 16)
            sp.dma_start(w2[:, :, :, :], d["local_w2"]).then_inc(sem("local_loaded"), 16)

            def one(name, l, i):
                return d[name][l, i, :, :] if isinstance(i, int) else \
                    d[name][l, bass.ds(i, 1), :, :].rearrange("o p n -> (o p) n")

            for l in range(2):
                if l:
                    sp.wait_ge(sem("win_out"), layers[0].after()["win_out"])
                win_sp(sp, layers[l], A7, lambda i: one("local_w", l, i).rearrange("p (j n) -> p j n", j=3),
                       lambda i: one("local_wo", l, i))

        def mlp_pe(pe, l):
            pe.wait_ge(sem("local_loaded"), 48)
            pe.wait_ge(sem("ln_normed"), 4 * (9 + l))

            def up(b):
                pe.wait_ge(sem("h_ready"), 4 * (8 + l) + b + 1)
                for c in range(3):
                    f = 12 * l + 3 * b + c
                    n = min(128, HID - 128 * c)
                    if f - 12 * l >= 2:
                        pe.wait_ge(sem("mlp_hidden"), f - 1)
                    for half in range(2):
                        lo = HID * half + 128 * c
                        last = pe.matmul(bank[4 + 2 * (f % 2) + half][0:n, :], w1[:, l, lo:lo + n], mlp_in[b],
                                         start=True, stop=True)
                    last.then_inc(sem("up_raw"), 1)

            def down(b):
                for c in range(3):
                    n = min(128, HID - 128 * c)
                    pe.wait_ge(sem("mlp_hidden"), 12 * l + 3 * b + c + 1)
                    last = pe.matmul(bank[b][:, :], w2[0:n, l, c, :], mlp_hid[c][0:n, :],
                                     start=(c == 0), stop=(c == 2))
                    last.then_inc(sem("mlp_hid_read"), 1)

            for b in range(B):
                up(b)
                down(b)

        def mlp_act(act, l):
            for f in range(12 * l, 12 * l + 12):
                c = f % 3
                n = min(128, HID - 128 * c)
                act.wait_ge(sem("up_raw"), FB * B + f + 1)
                if f >= 2:
                    act.wait_ge(sem("mlp_hidden"), f - 1)
                nc.scalar.activation(mlp_gelu[f % 2][0:n, :], bank[5 + 2 * (f % 2)][0:n, :], ACT.Gelu,
                                     bias=v("b1g", 3 * l + c)[0:n, :]).then_inc(sem("up_acted"), 1)

        def mlp_dve(dve, l):
            for b in range(B):
                for c in range(3):
                    f = 12 * l + 3 * b + c
                    n = min(128, HID - 128 * c)
                    dve.wait_ge(sem("up_acted"), FB * B + f + 1)
                    if b:
                        dve.wait_ge(sem("mlp_hid_read"), f - 2)
                    nc.vector.scalar_tensor_tensor(mlp_hid[c][0:n, :], bank[4 + 2 * (f % 2)][0:n, :],
                                                   v("b1a", 3 * l + c)[0:n, :], mlp_gelu[f % 2][0:n, :],
                                                   ALU.add, ALU.mult).then_inc(sem("mlp_hidden"), 1)
                dve.wait_ge(sem("mlp_hid_read"), 12 * l + 3 * b + 3)
                link(dve, "dve", nc.vector.scalar_tensor_tensor(hb(b), bank[b][:, :], v("b2", l), hb(b),
                                                                ALU.add, ALU.add))

        def final_dve(dve):
            for b in range(B):
                nc.vector.scalar_tensor_tensor(x[:, b, :], hb(b), gate(7, b), x[:, b, :], ALU.mult, ALU.add) \
                  .then_inc(sem("x_ready"), 1)

        @block.sync
        def _(sp):
            sp.dma_start(cond[:, :], d["cond"]).then_inc(sem("cond_loaded"), 16)
            for b in range(B):
                sp.dma_start(x[:, b, :], d["x"][:, b, :]).then_inc(sem(f"x_loaded{b}"), 16)
                if b == 0:
                    sp.dma_start(centre[:, :], d["centre"]).then_inc(sem("consts"), 16)
                    sp.dma_start(mean[:, :], d["mean"]).then_inc(sem("consts"), 16)
                    sp.dma_start(ident[:, :], d["ident"]).then_inc(sem("consts"), 16)
                    sp.dma_start(vec[:, :], d["vec"]).then_inc(sem("consts"), 16)
                    sp.dma_start(conv_w[:, :], d["conv_w"]).then_inc(sem("consts"), 16)
            sp.dma_start(wmod[:, :, :], d["wmod"]).then_inc(sem("wmod_loaded"), 16)
            for p in range(2):
                sp.dma_start(conv_bias[64 * p:64 * p + 64, :, :],
                             d["conv_bias"][p:p + 1, :, :].to_broadcast([64, 16, K])).then_inc(sem("conv_tables"), 16)
            sp.dma_start(conv_mask[:, :, :], d["conv_mask"]).then_inc(sem("conv_tables"), 16)
            sp.dma_start(conv_edge[:, :], d["conv_edge"]).then_inc(sem("conv_tables"), 16)
            sp.dma_start(head_sum[:, :], d["head_sum"]).then_inc(sem("kv_loaded"), 16)
            sp.dma_start(lr_u1[:, :], d["lr_u1"]).then_inc(sem("early_loaded"), 16)
            sp.dma_start(lr_v1[:, :], d["lr_v1"]).then_inc(sem("early_loaded"), 16)
            sp.dma_start(lr_u2[:, :, :], d["lr_u2"]).then_inc(sem("early_loaded"), 16)
            sp.dma_start(lr_v2[:, :], d["lr_v2"]).then_inc(sem("early_loaded"), 16)
            sp.dma_start(scan_w[:, :, :], d["scan_w"]).then_inc(sem("early_loaded"), 16)
            moe_sp(sp)
            att_sp(sp)
            mix_sp(sp)
            alibi_sp(sp)
            local_sp(sp)
            for b in range(B):
                sp.wait_ge(sem("x_ready"), LAST + b + 1)
                sp.dma_start(out[:, b, :], x[:, b, :]).then_inc(sem("stored"), 16)
            sp.wait_ge(sem("stored"), 16 * B)

        @block.gpsimd
        def _(pool):
            nc.gpsimd.memset(rms_eps[:, :], 0.01)
            nc.gpsimd.memset(ln_clip[:, :], 15.0 * LN2)
            nc.gpsimd.memset(eps_col[:, :], EPS).then_inc(sem("filled"), 1)
            nc.gpsimd.memset(zeros[:, :], 0.0).then_inc(sem("filled"), 1)
            nc.gpsimd.memset(h[:, :, 0:PAD], 0.0)
            ln_pool(pool, 0)
            ln_pool(pool, 1)
            ln_pool(pool, 2)
            scan_pool(pool)
            ln_pool(pool, 3)
            moe_pool(pool)
            ln_pool(pool, 4)
            att_pool(pool)
            ln_pool(pool, 5)
            ln_pool(pool, 6)
            win_pool(pool, W6, A6)
            ln_pool(pool, 7)
            for l in range(2):
                win_pool(pool, layers[l], A7)
                ln_pool(pool, 8 + l)

        @block.scalar
        def _(act):
            mod_act(act)
            ln_act(act, 0)
            conv_act(act)
            act.wait_ge(sem("consts"), 80)
            ln_act(act, 1)
            lr_act(act)
            ln_act(act, 2)
            scan_act(act)
            ln_act(act, 3)
            moe_act_engine(act)
            ln_act(act, 4)
            att_act(act)
            ln_act(act, 5)
            mix_act(act)
            ln_act(act, 6)
            kv_act(act)
            win_act(act, W6, A6)
            ln_act(act, 7)
            for l in range(2):
                win_act(act, layers[l], A7)
                ln_act(act, 8 + l)
                mlp_act(act, l)

        @block.vector
        def _(dve):
            mod_dve(dve)
            ln_dve(dve, 0)
            conv_dve(dve)
            dve.wait_ge(sem("consts"), 80)
            ln_dve(dve, 1)
            lr_dve(dve)
            ln_dve(dve, 2)
            scan_dve(dve)
            ln_dve(dve, 3)
            moe_dve(dve)
            ln_dve(dve, 4)
            att_dve(dve)
            ln_dve(dve, 5)
            mix_dve(dve)
            ln_dve(dve, 6)
            kv_dve(dve)
            alibi_dve(dve)
            ln_dve(dve, 7)
            clear_dve(dve)
            for l in range(2):
                scale_tables(dve, l)
                shift_dve(dve, l, 0)
                local_dve(dve, l)
                shift_dve(dve, l, 1)
                ln_dve(dve, 8 + l)
                mlp_dve(dve, l)
            final_dve(dve)

        @block.tensor
        def _(pe):
            pe.wait_ge(sem("consts"), 80)
            mod_pe(pe)
            ln_pe(pe, 0)
            conv_pe(pe)
            ln_pe(pe, 1, after_all=True)
            lr_pe(pe)
            ln_pe(pe, 2)
            scan_pe(pe)
            ln_pe(pe, 3, after_all=True)
            moe_pe(pe)
            ln_pe(pe, 4, after_all=True)
            att_pe(pe)
            ln_pe(pe, 5)
            mix_pe(pe)
            ln_pe(pe, 6)
            kv_pe(pe)
            alibi_pe(pe)
            ln_pe(pe, 7, after_all=True)
            for l in range(2):
                local_pe(pe, l)
                ln_pe(pe, 8 + l, after_all=True)
                mlp_pe(pe, l)


def _layouts(a):
    f = np.float32
    d = {"x": a["L0_attn_x"].transpose(2, 0, 1)}
    d["cond"] = np.concatenate([a[f"L{i}_c"] for i in range(4)], 0).T
    d["wmod"] = np.stack([a[f"L{i}_wmod"] for i in range(4)], 1)
    d["ident"] = np.eye(128, dtype=f)
    d["centre"] = (np.eye(C) - 1.0 / C).astype(f)
    d["mean"] = np.full((C, C), 1.0 / C, f)
    vec = np.zeros((128, NVEC), f)

    def put(name, *cols):
        for i, col in enumerate(cols):
            vec[:len(col), VEC[name][0] + i] = col

    put("ffn0_b1", *a["L0_ffn_b1"].reshape(4, 128))
    put("ffn0_b2", a["L0_ffn_b2"])
    for n in ("ba", "bb", "bc"):
        put("scan_" + n, a["L1_attn_" + n])
    put("r1_b", a["L1_ffn_r1_b"])
    put("attn2_bo", a["L2_attn_bo"])
    put("mu_r", a["L2_ffn_mu_r"])
    put("mu_k", a["L2_ffn_mu_k"])
    put("qn_w", np.tile(a["L3_attn_q_norm_w"], 2))
    put("kn_w", np.tile(a["L3_attn_k_norm_w"], 2))
    couples = np.arange(64).reshape(2, 32).T.reshape(-1)
    for l in range(2):
        for n in ("q_scale", "k_scale"):
            s = a["L3_ffn_" + n][l]
            vec[:, VEC[n][0] + l] = np.tile(s[couples], 2)
            vec[:, VEC[n + "_rot"][0] + l] = np.tile(s[couples[np.arange(64) ^ 1]], 2)
    put("ln_g", *a["L3_ffn_ln_g"])
    put("ln_b", *a["L3_ffn_ln_b"])
    put("b2", *a["L3_ffn_b2"])
    for l in range(2):
        for j in range(3):
            n = min(128, HID - 128 * j)
            vec[:n, VEC["b1a"][0] + 3 * l + j] = a["L3_ffn_b1"][l, 128 * j:128 * j + n]
            vec[:n, VEC["b1g"][0] + 3 * l + j] = a["L3_ffn_b1"][l, HID + 128 * j:HID + 128 * j + n]
    for p in range(8):
        vec[:, VEC["slope"][0] + p] = np.repeat(2.0 ** (-0.5 * (2 * p + 1 + np.arange(2))), 64)
    d["vec"] = vec
    j = np.arange(32)
    d["conv_w"] = a["L0_attn_W"].T[:, np.tile(j, 2)]
    res = np.arange(32).reshape(16, 2).T
    d["conv_bias"] = a["L0_attn_b"][(j[None, None, :] - res[:, :, None]) % 32]
    s = np.arange(128)[:, None, None] - 32 * np.arange(4)[None, :, None] - j[None, None, :]
    d["conv_mask"] = ((s >= 0) & (s < 32)).astype(f)
    d["conv_edge"] = (j[:, None] < j[None, :]).astype(f)
    d["lr_u1"], d["lr_v1"], d["lr_v2"] = a["L0_ffn_U1"], a["L0_ffn_V1"], a["L0_ffn_V2"]
    d["lr_u2"] = a["L0_ffn_U2"].reshape(4, 128, 32).transpose(1, 0, 2)
    d["scan_w"] = np.stack([a["L1_attn_W" + n].T for n in "abc"], 1)
    r1 = a["L1_ffn_r1_w"].T
    d["r1_c"], d["r1_s"], d["r2_w"] = r1[:C], r1[C:], a["L1_ffn_r2_w"].T
    d["iota_e"] = np.tile(np.arange(32, dtype=f), (128, 1))
    p = np.arange(128)
    d["chunk_sum"] = ((p[:, None] % 32 == p[None, :] % 32) & (p[:, None] // 32 < p[None, :] // 32)).astype(f)
    up = a["L1_ffn_w_up"].transpose(0, 2, 1).reshape(16, 2, C, 512).transpose(0, 2, 1, 3).reshape(16, C, 1024)
    down = a["L1_ffn_w_down"].transpose(0, 2, 1).reshape(16, 2, 2, 128, C).transpose(0, 3, 1, 2, 4).reshape(16, 128, 512)
    d["moe_w"] = np.concatenate([up, down, a["L1_ffn_a_up"].transpose(0, 2, 1), a["L1_ffn_a_down"].transpose(0, 2, 1)], 2)
    def pairs(w):
        return w.reshape(C, 8, 128).transpose(1, 0, 2)

    d["att_w"] = np.stack([pairs(a["L2_attn_W" + n]) for n in "qkv"], 2)
    d["att_wo"] = a["L2_attn_Wo"].reshape(8, 128, C)
    inv = (1.0 / (np.float32(10000.0) ** (np.arange(0, 64, 2, dtype=f) / f(64)))).astype(f)
    ang = (np.arange(T, dtype=f)[None, :] * inv[:, None]).astype(f).astype(np.float64)
    cos, sin = (np.tile(np.repeat(t(ang), 2, 0), (2, 1)) for t in (np.cos, np.sin))
    sin = sin * np.where(np.arange(128) % 2 == 0, -1.0, 1.0)[:, None]
    d["rope_tab"] = np.stack([cos / 8, sin / 8, cos, sin], 1).astype(f)
    i64 = np.arange(128) % 64
    d["att_mask"] = np.where(np.arange(64)[None, :] <= i64[:, None], 0.0, -1e30).astype(f)
    d["mix_w"] = np.stack([a["L2_ffn_W_" + n].T for n in "rkv"], 1)
    d["head_sum"] = (p[:, None] // 64 == p[None, :] // 64).astype(f)
    d["kv_w"] = np.stack([a["L3_attn_wk"].T, a["L3_attn_wv"].T], 1)
    d["alibi_wq"] = pairs(a["L3_attn_wq"].T)
    d["alibi_wo"] = a["L3_attn_wo"].T.reshape(8, 128, C)
    qi, kj = i64[:, None, None], np.arange(128)[None, None, :]
    rel = kj - 64 - qi + 0 * np.arange(8)[None, :, None]
    there = (kj >= 64) | (np.arange(8)[None, :, None] > 0)
    d["alibi_rel"] = np.where((rel <= 0) & (rel >= -16) & there, rel, -1e30).astype(f)
    d["local_mask"] = np.where((rel <= 0) & (rel >= -64) & there, 0.0, -1e30).astype(f)
    w = a["L3_ffn_wqkv"].reshape(2, C, 3, 4, 128).transpose(2, 0, 3, 1, 4)
    c2 = np.concatenate([couples, 64 + couples])
    d["local_w"] = np.stack([w[0][..., c2], w[1][..., c2], w[2]], 3).reshape(2, 4, C, 384)
    d["local_wo"] = a["L3_ffn_wo"].reshape(2, 4, 128, C)
    d["local_w1"] = a["L3_ffn_w1"].transpose(1, 0, 2)
    w2 = np.zeros((128, 2, 3, C), f)
    for j in range(3):
        n = min(128, HID - 128 * j)
        w2[:n, :, j, :] = a["L3_ffn_w2"][:, 128 * j:128 * j + n, :].transpose(1, 0, 2)
    d["local_w2"] = w2
    idx = np.arange(0, 64, 2, dtype=f)
    t = np.arange(T, dtype=f)
    ang = (t[None, :] * inv[:, None]).astype(f).astype(np.float64)
    base = ((idx + f(0.4 * 64)) / f(1.4 * 64)).astype(np.float64)
    sc = base[:, None] ** ((t[None, :].astype(np.float64) - T // 2) / 32.0)
    cos, sin, sc = (np.tile(np.repeat(t, 2, 0), (2, 1)) for t in (np.cos(ang), np.sin(ang), sc))
    sin = sin * np.where(p % 2 == 0, -1.0, 1.0)[:, None]
    d["qk_tab"] = np.stack([8 * cos * sc, 8 * sin * sc, cos / sc, sin / sc], 1).astype(f)
    return d


def kernel(**inputs):
    import concourse.bacc as _bacc
    from concourse.bass_utils import run_bass_kernel_spmd as _run

    nc = _bacc.Bacc("TRN2", target_bir_lowering=False, num_devices=1)
    arrays, aps = {}, {}
    for name, a in _layouts({k: np.asarray(val) for k, val in inputs.items()}).items():
        a = np.ascontiguousarray(a)
        arrays["in_" + name] = a
        aps[name] = nc.dram_tensor("in_" + name, a.shape, mybir.dt.from_np(a.dtype), kind="ExternalInput").ap()
    out = nc.dram_tensor("out_x", (C, B, T), F32, kind="ExternalOutput").ap()
    adaln_blocks(nc, aps, out)
    r = _run(nc, [arrays], core_ids=[0])
    return np.ascontiguousarray(r.results[0]["out_x"].transpose(1, 2, 0))
```

```python
from contextlib import ExitStack

import numpy as np

import concourse.bass as bass
from concourse import mybir

F32 = mybir.dt.float32
U32 = mybir.dt.uint32
ALU = mybir.AluOpType
ACT = mybir.ActivationFunctionType
AX_X = mybir.AxisListType.X

C = 128
B = 4
T = 512
N = B * T
PAD = 64
TP = PAD + T
TILES = N // 128
TB = T // 128
EPS = 1e-5
LN2 = 0.6931471805599453

K = 32
R = 32
FB = 4
E = 32
CAP = int(1.25 * N / E)
G = 16
SLOTS = E * CAP
DUMP = SLOTS
ROUNDS = CAP // 8
WG = 2 * 512 + 2 * 256 + 256 + 128
NB128 = SLOTS // 128

NBLK = T // 64
SHORT = 96
PAIRS = 8
UNROLL = 8
SWAP = [i ^ 1 for i in range(32)]
GROUPS = [[7], [6, 0], [5, 1], [4, 2], [3]]
GCUM = [1, 3, 5, 7, 8]
SBANKS = [1, 2, 7, 1, 2, 7, 1, 2, 7, 2]
PCH = [j // 2 + 1 for j in range(NBLK)]
POFF = [128 * sum(PCH[:j]) for j in range(NBLK)]
PW = 128 * sum(PCH)
CHUNKS = [(jc, j) for jc in range(TB) for j in range(NBLK) if j // 2 >= jc]
NFILL = len(CHUNKS) // 4

HID = int(C * 4 * 2 / 3)

VEC = {}
for _name, _n in (("ffn0_b1", 4), ("ffn0_b2", 1), ("scan_ba", 1), ("scan_bb", 1), ("scan_bc", 1),
                  ("r1_b", 1), ("attn2_bo", 1), ("mu_r", 1), ("mu_k", 1), ("qn_w", 1), ("kn_w", 1),
                  ("q_scale", 2), ("k_scale", 2), ("q_scale_rot", 2), ("k_scale_rot", 2),
                  ("ln_g", 2), ("ln_b", 2), ("b2", 2), ("b1a", 6), ("b1g", 6), ("slope", 8)):
    VEC[_name] = (sum(n for _, n in VEC.values()), _n)
NVEC = sum(n for _, n in VEC.values())


def adaln_blocks(nc, d, out):
    ctx = ExitStack()
    with ctx:
        def sb(name, shape, dt=F32):
            return ctx.enter_context(nc.sbuf_tensor(name, shape, dt))

        scope = [ExitStack()]

        def tmp_sb(name, shape, dt=F32):
            return scope[0].enter_context(nc.sbuf_tensor(name, shape, dt))

        def next_block():
            scope[0].close()
            scope[0] = ExitStack()

        sems = {}

        def sem(name):
            if name not in sems:
                sems[name] = ctx.enter_context(nc.semaphore(name))
            return sems[name]

        bank = [ctx.enter_context(nc.psum_tensor(f"bank{i}", [128, 512], F32)) for i in range(8)]

        x = sb("x", [C, B, T])
        h = sb("h", [C, B, TP])
        ident = sb("ident", [128, 128])
        centre = sb("centre", [128, 128])
        mean = sb("mean", [128, 128])
        vec = sb("vec", [128, NVEC])
        cond = sb("cond", [C, 16])
        cond_silu = sb("cond_silu", [C, 16])
        mod = sb("mod", [C, 4, 6, B])
        
        gate_sign = sb("gate_sign", [C, 4, 2, B])
        gate_abs = sb("gate_abs", [C, 4, 2, B])
        eps_col = sb("eps_col", [128, 1])
        rms_eps = sb("rms_eps", [128, 1])
        ln_clip = sb("ln_clip", [128, 1])
        head_sum = sb("head_sum", [128, 128])
        ln_square = sb("ln_square", [C, 2, T])
        ln_log = sb("ln_log", [C, 2, T])
        ln_rstd = sb("ln_rstd", [C, 2, T])
        ln_norm = sb("ln_norm", [C, 2, T])

        lr_u1 = sb("lr_u1", [C, R])
        lr_v1 = sb("lr_v1", [R, FB * 128])
        lr_u2 = sb("lr_u2", [128, FB, R])
        lr_v2 = sb("lr_v2", [R, C])
        scan_w = sb("scan_w", [C, 3, C])
        att_w = [sb(f"att_w{i}", [C, 3, 128]) for i in range(2)]
        rope_tab = sb("rope_tab", [128, 4, T])
        att_mask = sb("att_mask", [128, 64])
        mix_w = sb("mix_w", [C, 3, C])
        moe_w = [sb(f"moe_w{u}", [128, WG]) for u in range(2)]
        r1_c = sb("r1_c", [C, 64])
        r1_s = sb("r1_s", [6, 64])
        r2_w = sb("r2_w", [64, E])
        iota_e = sb("iota_e", [128, E])
        chunk_sum = sb("chunk_sum", [128, 128])
        zeros = sb("zeros", [128, 4 * C])
        htok = sb("htok", [128, TILES, C])

        ctx.callback(lambda: scope[0].close())

        def v(name, i=0):
            at, n = VEC[name]
            assert i < n
            return vec[:, at + i:at + i + 1]

        def gate(k, b):
            return mod[:, k // 2, 3 * (k % 2) + 2, b:b + 1]

        def scale1(k, b):
            return mod[:, k // 2, 3 * (k % 2) + 1, b:b + 1]

        def shift(k, b):
            return mod[:, k // 2, 3 * (k % 2), b:b + 1]

        def hb(b):
            return h[:, b, PAD:TP]

        def hh(b, lo, n):
            return h[:, b, PAD + lo:PAD + lo + n]

        steps = {"dve": 0, "act": 0, "pool": 0}

        def link(eng, name, ins):
            steps[name] += 1
            ins.then_inc(sem(name + "_step"), 1)
            eng.wait_ge(sem(name + "_step"), steps[name])

        LAST = 4 * 5
        block = ctx.enter_context(nc.Block())

        def x_written(k):
            if k == 4:
                return "pair_added", B * PAIRS
            if k == 6:
                return "pair_added", 2 * B * PAIRS
            return "x_ready", 4 * (k if k < 4 else k - 1)

        def ln_pe(pe, k, after_all=False, before=None, behind_two=None):
            def centred(b):
                if before:
                    before(b)
                n = 4 * k + b
                src = x[:, b, :]
                if k == 0:
                    pe.wait_ge(sem(f"x_loaded{b}"), 16)
                else:
                    name, base = ("shifted", 8 * (k - 8) + 4) if k >= 8 else x_written(k - 1)
                    pe.wait_ge(sem(name), base + (B if after_all else b + 1))
                if k >= 8:
                    src = shifted[:, b, PAD:TP]
                if n >= 3:
                    pe.wait_ge(sem("ln_normed"), n - 2)
                pe.matmul(bank[n % 3][:, :], centre[:, :], src, start=True, stop=True) \
                  .then_inc(sem("ln_centred"), 1)

            def variance(b):
                n = 4 * k + b
                pe.wait_ge(sem("ln_squared"), n + 1)
                if n:
                    pe.wait_ge(sem("ln_log"), n)
                pe.matmul(bank[3][:, :], mean[:, :], ln_square[:, n % 2, :], start=True, stop=True) \
                  .then_inc(sem("ln_variance"), 1)

            centred(0)
            for b in range(B):
                if b == 2 and behind_two:
                    behind_two()
                if b + 1 < B:
                    centred(b + 1)
                variance(b)

        def ln_act(act, k):
            nc.scalar.preload_act_table_set("natural_log_exp_and_others")

            def square(b):
                n = 4 * k + b
                act.wait_ge(sem("ln_centred"), n + 1)
                if n >= 2:
                    act.wait_ge(sem("ln_variance"), n - 1)
                nc.scalar.activation(ln_square[:, n % 2, :], bank[n % 3][:, :], ACT.Square) \
                  .then_inc(sem("ln_squared"), 1)

            square(0)
            for b in range(B):
                n = 4 * k + b
                if b + 1 < B:
                    square(b + 1)
                act.wait_ge(sem("ln_variance"), n + 1)
                if n == 0:
                    act.wait_ge(sem("filled"), 1)
                nc.scalar.activation(ln_log[:, n % 2, :], bank[3][:, :], ACT.Ln,
                                     bias=eps_col[:, 0:1]).then_inc(sem("ln_log"), 1)
                act.wait_ge(sem("ln_log"), n + 1)
                if n >= 2:
                    act.wait_ge(sem("ln_normed"), n - 1)
                nc.scalar.activation(ln_rstd[:, n % 2, :], ln_log[:, n % 2, :], ACT.Exp, scale=-0.5) \
                  .then_inc(sem("ln_rstd"), 1)

        def ln_dve(dve, k, ahead=None):
            for b in range(B):
                if ahead:
                    ahead(b)
                n = 4 * k + b
                dve.wait_ge(sem("ln_rstd"), n + 1)
                if n >= 2:
                    dve.wait_ge(sem("h_ready"), n - 1)
                nc.vector.tensor_tensor(ln_norm[:, n % 2, :], bank[n % 3][:, :], ln_rstd[:, n % 2, :],
                                        ALU.mult).then_inc(sem("ln_normed"), 1)

        def ln_pool(pool, k):
            for b in range(B):
                n = 4 * k + b
                if k == 0 and b == 0:
                    pool.wait_ge(sem("mod_ready"), 4)
                pool.wait_ge(sem("ln_normed"), n + 1)
                dst = conv_h[:, T * b:T * b + T] if k == 0 else hb(b)
                scale, bias = (scale1(k, b), shift(k, b)) if k < 8 else (v("ln_g", k - 8), v("ln_b", k - 8))
                if k >= 8:
                    dst = mlp_in[b]
                nc.gpsimd.tensor_scalar(dst, ln_norm[:, n % 2, :], scale, bias,
                                        ALU.mult, ALU.add).then_inc(sem("h_ready"), 1)

        def mod_act(act):
            act.wait_ge(sem("cond_loaded"), 16)
            nc.scalar.activation(cond_silu[:, :], cond[:, :], ACT.Silu).then_inc(sem("cond_ready"), 1)

        def mod_pe(pe):
            pe.wait_ge(sem("cond_ready"), 1)
            pe.wait_ge(sem("wmod_loaded"), 16)
            for l in range(4):
                for j in range(6):
                    at = (6 * l + j) * B
                    last = pe.matmul(bank[7][:, at:at + B], wmod[:, l, j * C:(j + 1) * C],
                                     cond_silu[:, B * l:B * l + B], start=True, stop=True)
            last.then_inc(sem("mod_raw"), 1)

        def mod_dve(dve):
            dve.wait_ge(sem("mod_raw"), 1)
            raw = bank[7][:, 0:96].rearrange("p (l j b) -> p l j b", l=4, j=6)
            for i in range(2):
                s, c, g = (mod[:, :, 3 * i + j, :] for j in range(3))
                nc.vector.tensor_copy(s, raw[:, :, 3 * i, :]).then_inc(sem("mod_ready"), 1)
                nc.vector.tensor_scalar(c, raw[:, :, 3 * i + 1, :], 1.0, None, ALU.add) \
                  .then_inc(sem("mod_ready"), 1)
                r = raw[:, :, 3 * i + 2, :]
                link(dve, "dve", nc.vector.tensor_scalar(gate_sign[:, :, i, :], r, 0.0, 2.0, ALU.is_ge, ALU.mult))
                link(dve, "dve", nc.vector.tensor_scalar(gate_abs[:, :, i, :], r, -1.0, None, ALU.mult))
                link(dve, "dve", nc.vector.tensor_tensor(gate_abs[:, :, i, :], gate_abs[:, :, i, :], r, ALU.max))
                link(dve, "dve", nc.vector.tensor_scalar(gate_abs[:, :, i, :], gate_abs[:, :, i, :], 0.25, None,
                                                         ALU.max))
                link(dve, "dve", nc.vector.scalar_tensor_tensor(g, gate_sign[:, :, i, :], -1.0,
                                                                gate_abs[:, :, i, :], ALU.add, ALU.mult))

        wmod = tmp_sb("wmod", [C, 4, 6 * C])
        conv_h = tmp_sb("conv_h", [C, N])
        conv_w = tmp_sb("conv_w", [C, 2 * K])
        conv_bias = tmp_sb("conv_bias", [128, 16, K])
        conv_mask = tmp_sb("conv_mask", [128, TB, K])
        conv_edge = tmp_sb("conv_edge", [K, K])
        logit = tmp_sb("logit", [128, 16, K])
        row_max = tmp_sb("row_max", [128, 16])
        row_sum = tmp_sb("row_sum", [128, 16])
        row_inv = tmp_sb("row_inv", [128, 16])
        prob4 = tmp_sb("prob4", [128, 16, 4, K])
        band = tmp_sb("band", [128, TILES, 128])
        edge = tmp_sb("edge", [K, TILES, K])

        def htok_pe(pe, banks, tokens):
            for b in range(B):
                for i in range(TB):
                    last = pe.transpose(banks[b][:, 128 * i:128 * i + 128], tokens(b, i), ident[:, :])
                last.then_inc(sem("htok_raw"), 1)

        def conv_pe(pe):
            pe.wait_ge(sem("h_ready"), 4)
            for r in range(K):
                half = 64 * (r % 2)
                last = pe.matmul(bank[4][half:half + 64, K * (r // 2):K * (r // 2) + K],
                                 conv_h[:, r:N:K], conv_w[:, K - r:2 * K - r], start=True, stop=True)
            last.then_inc(sem("conv_logits"), 1)
            pe.wait_ge(sem("ln_normed"), 4)
            htok_pe(pe, bank[0:4], lambda b, i: conv_h[:, T * b + 128 * i:T * b + 128 * i + 128])
            pe.wait_ge(sem("conv_prob"), 1)
            for g in range(4):
                for i in range(4):
                    last = pe.transpose(bank[4 + g][:, 128 * i:128 * i + 128],
                                        prob4[:, 4 * g + i, :, :].rearrange("p a b -> p (a b)"), ident[:, :])
                last.then_inc(sem("conv_probT"), 1)
            pe.wait_ge(sem("conv_band"), 8)
            for b in range(B):
                pe.wait_ge(sem("htok_ready"), b + 1)
                if b + 1 < B:
                    pe.wait_ge(sem("htok_ready"), b + 2)
                for i in range(TB):
                    t = TB * b + i
                    last = pe.matmul(bank[b][:, 128 * i:128 * i + 128], htok[:, t, :], band[:, t, :],
                                     start=True, stop=(i == TB - 1))
                    if i < TB - 1:
                        last = pe.matmul(bank[b][:, 128 * i + 96:128 * i + 128], htok[0:K, t + 1, :],
                                         edge[:, t, :], start=False, stop=True)
                last.then_inc(sem("pv_raw"), 1)

        def htok_act(act, base):
            for b in range(B):
                act.wait_ge(sem("htok_raw"), base + b + 1)
                nc.scalar.activation(htok[:, TB * b:TB * b + TB, :],
                                     bank[b][:, :].rearrange("p (i c) -> p i c", i=TB), ACT.Copy) \
                  .then_inc(sem("htok_ready"), 1)

        def conv_act(act):
            act.wait_ge(sem("conv_shifted"), 1)
            nc.scalar.activation(logit[:, :, :], logit[:, :, :], ACT.Exp).then_inc(sem("conv_exp"), 1)
            htok_act(act, 0)

        def conv_dve(dve):
            dve.wait_ge(sem("conv_logits"), 1)
            dve.wait_ge(sem("conv_tables"), 64)
            link(dve, "dve", nc.vector.tensor_tensor(
                logit[:, :, :], bank[4][:, :].rearrange("p (r j) -> p r j", j=K), conv_bias[:, :, :], ALU.add))
            link(dve, "dve", nc.vector.tensor_reduce(row_max[:, :], logit[:, :, :], AX_X, ALU.max))
            nc.vector.tensor_tensor(logit[:, :, :], logit[:, :, :],
                                    row_max[:, :].unsqueeze(2).to_broadcast([128, 16, K]), ALU.subtract) \
              .then_inc(sem("conv_shifted"), 1)
            dve.wait_ge(sem("conv_exp"), 1)
            link(dve, "dve", nc.vector.tensor_reduce(row_sum[:, :], logit[:, :, :], AX_X, ALU.add))
            link(dve, "dve", nc.vector.reciprocal(row_inv[:, :], row_sum[:, :]))
            for a in range(4):
                last = nc.vector.tensor_tensor(prob4[:, :, a, :], logit[:, :, :],
                                               row_inv[:, :].unsqueeze(2).to_broadcast([128, 16, K]), ALU.mult)
            last.then_inc(sem("conv_prob"), 1)
            bandv = band[:, :, :].rearrange("s t (q r) -> s t q r", r=K)
            for g in range(4):
                dve.wait_ge(sem("conv_probT"), g + 1)
                p = bank[4 + g][:, :].rearrange("s (r t q) -> s t q r", r=8, q=TB)
                m = conv_mask[:, :, 8 * g:8 * g + 8].unsqueeze(1).to_broadcast([128, TILES, TB, 8])
                nc.vector.tensor_tensor(bandv[:, :, :, 8 * g:8 * g + 8], p, m, ALU.mult) \
                  .then_inc(sem("conv_band"), 1)
                m = conv_edge[:, 8 * g:8 * g + 8].unsqueeze(1).to_broadcast([K, TILES, 8])
                nc.vector.tensor_tensor(edge[:, :, 8 * g:8 * g + 8], p[0:K, :, TB - 1, :], m, ALU.mult) \
                  .then_inc(sem("conv_band"), 1)
            for b in range(B):
                dve.wait_ge(sem("pv_raw"), b + 1)
                nc.vector.scalar_tensor_tensor(x[:, b, :], bank[b][:, :], gate(0, b), x[:, b, :],
                                               ALU.mult, ALU.add).then_inc(sem("x_ready"), 1)

        next_block()
        lr_p = tmp_sb("lr_p", [R, 2, T])
        lr_h = tmp_sb("lr_h", [128, 2, FB, T])
        lr_q = tmp_sb("lr_q", [R, 2, T])
        tmp = tmp_sb("tmp", [C, 2, T])

        def lr_pe(pe):
            def rank(b):
                pe.wait_ge(sem("h_ready"), 4 + b + 1)
                if b:
                    pe.wait_ge(sem("lr_p_ready"), b)
                pe.matmul(bank[4][0:R, :], lr_u1[:, :], hb(b), start=True, stop=True) \
                  .then_inc(sem("lr_p_raw"), 1)

            def up(b, f):
                n = FB * b + f
                if f == 0:
                    pe.wait_ge(sem("lr_p_ready"), b + 1)
                if n >= 2:
                    pe.wait_ge(sem("up_acted"), n - 1)
                pe.matmul(bank[5 + n % 2][:, :], lr_v1[:, 128 * f:128 * f + 128], lr_p[:, b % 2, :],
                          start=True, stop=True).then_inc(sem("up_raw"), 1)

            def down(b, f):
                pe.wait_ge(sem("up_acted"), FB * b + f + 1)
                if b and f == 0:
                    pe.wait_ge(sem("lr_q_ready"), b)
                last = pe.matmul(bank[7][0:R, :], lr_u2[:, f, :], lr_h[:, b % 2, f, :],
                                 start=(f == 0), stop=(f == FB - 1))
                if f == FB - 1:
                    last.then_inc(sem("lr_q_raw"), 1)

            def output(b):
                pe.wait_ge(sem("lr_q_ready"), b + 1)
                if b:
                    pe.wait_ge(sem("lr_out_read"), b)
                pe.matmul(bank[3][:, :], lr_v2[:, :], lr_q[:, b % 2, :], start=True, stop=True) \
                  .then_inc(sem("lr_out"), 1)

            pe.wait_ge(sem("early_loaded"), 96)
            rank(0)
            rank(1)
            for f in range(FB):
                up(0, f)
            pe.wait_ge(sem("ln_normed"), 8)
            for b in range(B):
                for f in range(FB):
                    if b + 1 < B:
                        up(b + 1, f)
                    down(b, f)
                    if b and f == 0:
                        output(b - 1)
                if b + 2 < B:
                    rank(b + 2)
            output(B - 1)

        def lr_act(act):
            for b in range(B):
                for f in range(FB):
                    n = FB * b + f
                    act.wait_ge(sem("up_raw"), n + 1)
                    if b >= 2 and f == 0:
                        act.wait_ge(sem("lr_q_raw"), b - 1)
                    nc.scalar.activation(lr_h[:, b % 2, f, :], bank[5 + n % 2][:, :], ACT.Gelu_apprx_tanh,
                                         bias=v("ffn0_b1", f)).then_inc(sem("up_acted"), 1)

        def lr_dve(dve):
            def p(b):
                dve.wait_ge(sem("lr_p_raw"), b + 1)
                if b >= 2:
                    dve.wait_ge(sem("up_raw"), FB * (b - 1))
                nc.vector.tensor_copy(lr_p[:, b % 2, :], bank[4][0:R, :]).then_inc(sem("lr_p_ready"), 1)

            def q(b):
                dve.wait_ge(sem("lr_q_raw"), b + 1)
                if b >= 2:
                    dve.wait_ge(sem("lr_out"), b - 1)
                nc.vector.tensor_copy(lr_q[:, b % 2, :], bank[7][0:R, :]).then_inc(sem("lr_q_ready"), 1)

            p(0)
            p(1)
            for b in range(B):
                q(b)
                if b + 2 < B:
                    p(b + 2)
                dve.wait_ge(sem("lr_out"), b + 1)
                if b >= 2:
                    dve.wait_ge(sem("x_ready"), 4 + b - 1)
                nc.vector.tensor_scalar(tmp[:, b % 2, :], bank[3][:, :], v("ffn0_b2"), gate(1, b),
                                        ALU.add, ALU.mult).then_inc(sem("lr_out_read"), 1)
                dve.wait_ge(sem("lr_out_read"), b + 1)
                nc.vector.tensor_tensor(x[:, b, :], x[:, b, :], tmp[:, b % 2, :], ALU.add) \
                  .then_inc(sem("x_ready"), 1)

        next_block()
        scan_a = tmp_sb("scan_a", [C, 2, T])
        scan_b = tmp_sb("scan_b", [C, 2, T])
        scan_c = tmp_sb("scan_c", [C, 2, T])
        scan_1a = tmp_sb("scan_1a", [C, 2, T])

        def scan_banks(b):
            return (bank[4], bank[5], bank[6]) if b % 2 == 0 else (bank[7], bank[0], bank[1])

        def scan_pe(pe):
            pe.wait_ge(sem("ln_normed"), 12)
            for b in range(B):
                pe.wait_ge(sem("h_ready"), 8 + b + 1)
                if b >= 2:
                    pe.wait_ge(sem("scan_gates"), 3 * (b - 1))
                for i in range(3):
                    pe.matmul(scan_banks(b)[i][:, :], scan_w[:, i, :], hb(b), start=True, stop=True) \
                      .then_inc(sem("scan_raw"), 1)

        def scan_act(act):
            for b in range(B):
                if b >= 2:
                    act.wait_ge(sem("x_ready"), 8 + b - 1)
                for i, (dst, f, bias) in enumerate(((scan_a, ACT.Sigmoid, "scan_ba"), (scan_b, ACT.Tanh, "scan_bb"),
                                                    (scan_c, ACT.Sigmoid, "scan_bc"))):
                    act.wait_ge(sem("scan_raw"), 3 * b + i + 1)
                    nc.scalar.activation(dst[:, b % 2, :], scan_banks(b)[i][:, :], f, bias=v(bias)) \
                      .then_inc(sem("scan_gates"), 1)

        def scan_pool(pool):
            for b in range(B):
                pool.wait_ge(sem("scan_gates"), 3 * b + 1)
                if b >= 2:
                    pool.wait_ge(sem("scan_in"), b - 1)
                nc.gpsimd.tensor_scalar(scan_1a[:, b % 2, :], scan_a[:, b % 2, :], -1.0, 1.0,
                                        ALU.mult, ALU.add).then_inc(sem("scan_1a_ready"), 1)

        def scan_dve(dve):
            for b in range(B):
                i = b % 2
                dve.wait_ge(sem("scan_gates"), 3 * b + 3)
                dve.wait_ge(sem("scan_1a_ready"), b + 1)
                nc.vector.tensor_tensor(scan_b[:, i, :], scan_1a[:, i, :], scan_b[:, i, :], ALU.mult) \
                  .then_inc(sem("scan_in"), 1)
                dve.wait_ge(sem("scan_in"), b + 1)
                link(dve, "dve", nc.vector.tensor_tensor_scan(scan_1a[:, i, :], scan_a[:, i, :], scan_b[:, i, :],
                                                              0.0, ALU.mult, ALU.add))
                link(dve, "dve", nc.vector.tensor_tensor(scan_c[:, i, :], scan_c[:, i, :], scan_1a[:, i, :], ALU.mult))
                nc.vector.scalar_tensor_tensor(x[:, b, :], scan_c[:, i, :], gate(2, b), x[:, b, :],
                                               ALU.mult, ALU.add).then_inc(sem("x_ready"), 1)

        next_block()
        bn = tmp_sb("bn", [128, TILES, 6])
        mv = tmp_sb("mv", [128, TILES, 2])
        stat = tmp_sb("stat", [128, TILES, 6])
        small = tmp_sb("small", [128, TILES, C])
        statT = tmp_sb("statT", [6, B, T])
        r_hid = tmp_sb("r_hid", [64, B, T])
        prob = tmp_sb("prob", [128, TILES, E])
        r_max = tmp_sb("r_max", [128, TILES])
        r_sum = tmp_sb("r_sum", [128, TILES])
        r_inv = tmp_sb("r_inv", [128, TILES])
        top8 = tmp_sb("top8", [128, TILES, 8])
        top8_at = tmp_sb("top8_at", [128, TILES, 8], U32)
        pick = tmp_sb("pick", [128, 2, TILES])
        onehot = tmp_sb("onehot", [128, 2, TILES, E])
        hit = tmp_sb("hit", [128, TILES, E])
        score = tmp_sb("score", [128, 4, B, E])
        scoreT = tmp_sb("scoreT", [128, T])
        rest = [tmp_sb(f"rest{i}", [128, T]) for i in range(2)]
        best = tmp_sb("best", [128, CAP])
        cand = [tmp_sb(f"cand{i}", [E, B, CAP]) for i in range(2)]
        best_all = tmp_sb("best_all", [E, CAP])
        above_last = tmp_sb("above_last", [E, CAP])
        cut = tmp_sb("cut", [E, 2])
        cut4 = tmp_sb("cut4", [128, 2])
        ones = tmp_sb("ones", [128, T])
        is_gt = tmp_sb("is_gt", [128, T])
        is_eq = tmp_sb("is_eq", [128, T])
        cum_gt = tmp_sb("cum_gt", [128, T])
        cum_eq = tmp_sb("cum_eq", [128, T])
        totals = tmp_sb("totals", [128, 2])
        offset = tmp_sb("offset", [128, 2])
        looked = tmp_sb("looked", [128, 2, TILES, E])
        place = tmp_sb("place", [128, 2, TILES])
        valid = tmp_sb("valid", [128, 2, TILES])
        slot = tmp_sb("slot", [128, 2, TILES])
        slot_u = tmp_sb("slot_u", [128, 2, TILES], U32)
        weight = tmp_sb("weight", [128, 2, TILES])
        xg = tmp_sb("xg", [128, SLOTS // 128, C])
        xgT = tmp_sb("xgT", [C, SLOTS + 128 - CAP])
        moe_silu = [tmp_sb(f"moe_silu{u}", [128, 3, 2 * CAP]) for u in range(2)]
        moe_act = [tmp_sb(f"moe_act{u}", [128, 3, 2 * CAP]) for u in range(2)]
        y_slot = [tmp_sb(f"y_slot{u}", [CAP, 2, C]) for u in range(2)]

        def up(u, q, j):
            return bank[2 * u + q][:, :].rearrange("p (j c) -> p j c", c=128)[:, j:j + 2, 0:CAP]

        y_tok = tmp_sb("y_tok", [128, 2, TILES, C])
        y_sum = htok
        early_w = y_tok[:, :, :, :].rearrange("p k t c -> p (k t c)")
        moe_w += [early_w[:, WG * u:WG * u + WG] for u in range(2)]
        xg_dram = nc.dram_tensor("xg_dram", (SLOTS, C), F32, kind="Internal").ap()
        y_dram = nc.dram_tensor("y_dram", (SLOTS + 1, C), F32, kind="Internal").ap()

        def moe_pe(pe):
            pe.wait_ge(sem("h_ready"), 16)
            pe.wait_ge(sem("ln_normed"), 16)
            pe.wait_ge(sem("x_ready"), 12)
            htok_pe(pe, bank[0:4], lambda b, i: hh(b, 128 * i, 128))
            pe.wait_ge(sem("moe_stats"), 1)
            for b in range(B):
                for i in range(TB):
                    last = pe.transpose(bank[4 + b][0:6, 128 * i:128 * i + 128], stat[:, TB * b + i, :], ident[:, :])
                last.then_inc(sem("moe_statT_raw"), 1)
            pe.wait_ge(sem("moe_loaded"), 80)
            for b in range(B):
                pe.wait_ge(sem("htok_ready"), B + b + 1)
                pe.matmul(bank[b][0:64, :], r1_c[:, :], hb(b), start=True, stop=False)
                pe.wait_ge(sem("moe_statT_ready"), b + 1)
                pe.matmul(bank[b][0:64, :], r1_s[:, :], statT[:, b, :], start=False, stop=True) \
                  .then_inc(sem("moe_hid_raw"), 1)
            for b in range(B):
                pe.wait_ge(sem("moe_hid_ready"), b + 1)
                for i in range(TB):
                    t = TB * b + i
                    last = pe.matmul(bank[4][:, E * t:E * t + E], r_hid[:, b, 128 * i:128 * i + 128], r2_w[:, :],
                                     start=True, stop=True)
            last.then_inc(sem("moe_logits"), 1)
            pe.wait_ge(sem("moe_scored"), 1)
            for g in range(4):
                last = pe.transpose(bank[5][:, 128 * g:128 * g + 128],
                                    score[:, g, :, :].rearrange("p j e -> p (j e)"), ident[:, :])
            last.then_inc(sem("moe_scoreT_raw"), 1)
            pe.wait_ge(sem("moe_totals"), 2)
            pe.matmul(bank[6][:, 0:2], chunk_sum[:, :], totals[:, :], start=True, stop=True) \
              .then_inc(sem("moe_offset_raw"), 1)
            pe.wait_ge(sem("moe_placed"), 1)
            for g in range(4):
                last = pe.transpose(bank[7][:, 128 * g:128 * g + 128], cum_gt[:, 128 * g:128 * g + 128], ident[:, :])
            last.then_inc(sem("moe_placeT"), 1)
            pe.wait_ge(sem("xg_loaded"), 16)
            for s in range(NB128 // 4):
                for i in range(4):
                    last = pe.transpose(bank[s][:, 128 * i:128 * i + 128], xg[:, 4 * s + i, :], ident[:, :])
                last.then_inc(sem("xgT_raw"), 1)
            pe.wait_ge(sem("xgT_ready"), NB128 // 4)

            def groups_pe(i, s):
                for u in range(2):
                    w = moe_w[2 * s + u]
                    pe.wait_ge(sem(f"moe_w_loaded{2 * s + u}"), i * 16 + 16)
                    at = i * (8 * CAP) + (4 * s + 2 * u) * CAP
                    for q in range(2):
                        for j in range(4):
                            last = pe.matmul(bank[2 * u + q][:, 128 * j:128 * j + 128],
                                             w[:, 512 * q + 128 * j:512 * q + 128 * j + 128],
                                             xgT[:, bass.ds(at + q * CAP, 128)],
                                             start=True, stop=True)
                        last.then_inc(sem(f"moe_up{u}"), 1)
                    for j in range(2):
                        last = pe.matmul(bank[4 + u][:, 2 * CAP * j:2 * CAP * j + 2 * CAP],
                                         w[:, 1536 + 128 * j:1536 + 128 * j + 128],
                                         xgT[:, bass.ds(at, 2 * CAP)],
                                         start=True, stop=True)
                    last.then_inc(sem(f"moe_up{u}"), 1)
                for u in range(2):
                    w = moe_w[2 * s + u]
                    pe.wait_ge(sem(f"moe_acted{u}"), i * 6 + (3 * s + 3))
                    for q in range(2):
                        y = bank[6 + u][0:CAP, C * q:C * q + C]
                        for j in range(2):
                            pe.matmul(y, moe_act[u][:, q, CAP * j:CAP * j + CAP],
                                      w[:, 1024 + 256 * q + 128 * j:1024 + 256 * q + 128 * j + 128],
                                      start=(j == 0), stop=False)
                        last = pe.matmul(y, moe_act[u][:, 2, CAP * q:CAP * q + CAP], w[:, 1792:1920],
                                         start=False, stop=True)
                    last.then_inc(sem(f"moe_y{u}"), 1)

            with pe.Fori(0, G // 4) as i:
                for s in range(2):
                    groups_pe(i, s)

        def moe_out_pe(pe, b):
            pe.wait_ge(sem("y_summed"), b + 1)
            for i in range(TB):
                last = pe.transpose(bank[4 + b][:, 128 * i:128 * i + 128], y_sum[:, TB * b + i, :], ident[:, :])
            last.then_inc(sem("moe_out"), 1)

        def moe_act_engine(act):
            htok_act(act, B)
            act.wait_ge(sem("htok_ready"), 2 * B)
            nc.scalar.activation(small[:, :, :], htok[:, :, :], ACT.Abs).then_inc(sem("moe_abs"), 1)
            act.wait_ge(sem("moe_moments"), 2)
            nc.scalar.activation(stat[:, :, 1], stat[:, :, 1], ACT.Sqrt).then_inc(sem("moe_roots"), 1)
            nc.scalar.activation(stat[:, :, 4], stat[:, :, 4], ACT.Sqrt).then_inc(sem("moe_roots"), 1)
            for b in range(B):
                act.wait_ge(sem("moe_hid_raw"), b + 1)
                nc.scalar.activation(r_hid[:, b, :], bank[b][0:64, :], ACT.Gelu, bias=v("r1_b")[0:64, :]) \
                  .then_inc(sem("moe_hid_ready"), 1)
            act.wait_ge(sem("moe_shifted"), 1)
            nc.scalar.activation(prob[:, :, :], prob[:, :, :], ACT.Exp).then_inc(sem("moe_exp"), 1)
            for s in range(NB128 // 4):
                act.wait_ge(sem("xgT_raw"), s + 1)
                nc.scalar.activation(xgT[:, 512 * s:512 * s + 512], bank[s][:, :], ACT.Copy) \
                  .then_inc(sem("xgT_ready"), 1)
            nc.scalar.preload_act_table(ACT.Silu)
            with act.Fori(0, G // 4) as i:
                for s, u in ((0, 0), (0, 1), (1, 0), (1, 1)):
                    for q in range(3):
                        act.wait_ge(sem(f"moe_up{u}"), i * 6 + (3 * s + q + 1))
                        src = up(u, q, 0) if q < 2 else bank[4 + u][:, 0:2 * CAP].rearrange("p (j c) -> p j c", j=2)
                        nc.scalar.activation(moe_silu[u][:, q, :].rearrange("p (j c) -> p j c", j=2), src, ACT.Silu) \
                          .then_inc(sem(f"moe_silued{u}"), 1)

        def moe_dve(dve):
            def L(ins):
                link(dve, "dve", ins)

            for b in range(B):
                dve.wait_ge(sem("htok_ready"), B + b + 1)
                for i in range(TB):
                    t = TB * b + i
                    last = nc.vector.bn_stats(bn[:, t, :], htok[:, t, :])
            L(last)
            for t in range(TILES):
                last = nc.vector.bn_aggr(mv[:, t, :], bn[:, t, :])
            L(last)
            nc.vector.tensor_scalar(stat[:, :, 1], mv[:, :, 1], C / (C - 1.0), None, ALU.mult) \
              .then_inc(sem("moe_moments"), 1)
            L(nc.vector.tensor_tensor(stat[:, :, 0], mv[:, :, 0], mv[:, :, 0], ALU.mult))
            L(nc.vector.tensor_tensor(stat[:, :, 4], stat[:, :, 0], mv[:, :, 1], ALU.add))
            nc.vector.tensor_scalar(stat[:, :, 4], stat[:, :, 4], float(C), None, ALU.mult) \
              .then_inc(sem("moe_moments"), 1)
            L(nc.vector.tensor_copy(stat[:, :, 0], mv[:, :, 0]))
            nc.vector.tensor_reduce(stat[:, :, 2], htok[:, :, :], AX_X, ALU.min)
            nc.vector.tensor_reduce(stat[:, :, 3], htok[:, :, :], AX_X, ALU.max)
            dve.wait_ge(sem("moe_abs"), 1)
            L(nc.vector.tensor_scalar(small[:, :, :], small[:, :, :], 1e-6, None, ALU.is_lt))
            L(nc.vector.tensor_reduce(stat[:, :, 5], small[:, :, :], AX_X, ALU.add))
            dve.wait_ge(sem("moe_roots"), 2)
            nc.vector.tensor_scalar(stat[:, :, 5], stat[:, :, 5], 1.0 / C, None, ALU.mult) \
              .then_inc(sem("moe_stats"), 1)
            for b in range(B):
                dve.wait_ge(sem("moe_statT_raw"), b + 1)
                nc.vector.tensor_copy(statT[:, b, :], bank[4 + b][0:6, :]).then_inc(sem("moe_statT_ready"), 1)

            dve.wait_ge(sem("moe_logits"), 1)
            logits = bank[4][:, :].rearrange("p (t e) -> p t e", e=E)
            L(nc.vector.tensor_reduce(r_max[:, :], logits, AX_X, ALU.max))
            nc.vector.tensor_tensor(prob[:, :, :], logits, r_max[:, :].unsqueeze(2).to_broadcast([128, TILES, E]),
                                    ALU.subtract).then_inc(sem("moe_shifted"), 1)
            dve.wait_ge(sem("moe_exp"), 1)
            L(nc.vector.tensor_reduce(r_sum[:, :], prob[:, :, :], AX_X, ALU.add))
            L(nc.vector.reciprocal(r_inv[:, :], r_sum[:, :]))
            L(nc.vector.tensor_tensor(prob[:, :, :], prob[:, :, :],
                                      r_inv[:, :].unsqueeze(2).to_broadcast([128, TILES, E]), ALU.mult))
            for t in range(TILES):
                last = nc.vector.max(top8[:, t, :], prob[:, t, :])
            L(last)
            for t in range(TILES):
                last = nc.vector.max_index(top8_at[:, t, :], top8[:, t, :], prob[:, t, :])
            L(last)
            L(nc.vector.tensor_copy(pick[:, :, :].rearrange("p k t -> p t k"), top8_at[:, :, 0:2]))
            experts = iota_e[:, :].unsqueeze(1).to_broadcast([128, TILES, E])
            for k in range(2):
                last = nc.vector.tensor_tensor(onehot[:, k, :, :], experts,
                                               pick[:, k, :].unsqueeze(2).to_broadcast([128, TILES, E]), ALU.is_equal)
            L(last)
            L(nc.vector.tensor_tensor(hit[:, :, :], onehot[:, 0, :, :], onehot[:, 1, :, :], ALU.add))
            L(nc.vector.tensor_tensor(prob[:, :, :], prob[:, :, :], hit[:, :, :], ALU.mult))
            L(nc.vector.tensor_scalar(hit[:, :, :], hit[:, :, :], -1.0, None, ALU.add))
            nc.vector.tensor_tensor(score[:, :, :, :].rearrange("p g j e -> p j g e"),
                                    prob[:, :, :].rearrange("p (j g) e -> p j g e", j=B),
                                    hit[:, :, :].rearrange("p (j g) e -> p j g e", j=B), ALU.add) \
              .then_inc(sem("moe_scored"), 1)
            L(nc.vector.tensor_tensor(r_sum[:, :], top8[:, :, 0], top8[:, :, 1], ALU.add))
            L(nc.vector.reciprocal(r_inv[:, :], r_sum[:, :]))
            for k in range(2):
                last = nc.vector.tensor_tensor(weight[:, k, :], top8[:, :, k], r_inv[:, :], ALU.mult)
            L(last)
            dve.wait_ge(sem("moe_scoreT_raw"), 1)
            L(nc.vector.tensor_copy(scoreT[:, :], bank[5][:, :]))
            for r in range(ROUNDS):
                src = scoreT if r == 0 else rest[(r - 1) % 2]
                L(nc.vector.max(best[:, 8 * r:8 * r + 8], src[:, :]))
                if r < ROUNDS - 1:
                    L(nc.vector.match_replace(rest[r % 2][:, :], best[:, 8 * r:8 * r + 8], src[:, :], -2.0))
            nc.vector.memset(xgT[:, SLOTS:], 0.0)
            nc.vector.memset(ones[:, :], 1.0).then_inc(sem("moe_best"), 1)
            dve.wait_ge(sem("moe_spread"), 16 * B)
            for r in range(ROUNDS):
                src = cand[r % 2][:, :, :].rearrange("e j c -> e (j c)")
                L(nc.vector.max(best_all[:, 8 * r:8 * r + 8], src))
                if r < ROUNDS - 1:
                    L(nc.vector.match_replace(cand[(r + 1) % 2][:, :, :].rearrange("e j c -> e (j c)"),
                                              best_all[:, 8 * r:8 * r + 8], src, -2.0))
            L(nc.vector.tensor_copy(cut[:, 0:1], best_all[:, CAP - 1:CAP]))
            L(nc.vector.tensor_scalar(above_last[:, :], best_all[:, :], cut[:, 0:1], None, ALU.is_gt))
            nc.vector.tensor_reduce(cut[:, 1:2], above_last[:, :], AX_X, ALU.add).then_inc(sem("moe_cut"), 1)
            dve.wait_ge(sem("moe_spread"), 32 * B)
            nc.vector.tensor_scalar(is_gt[:, :], scoreT[:, :], cut4[:, 0:1], None, ALU.is_gt)
            L(nc.vector.tensor_scalar(is_eq[:, :], scoreT[:, :], cut4[:, 0:1], None, ALU.is_equal))
            nc.vector.tensor_tensor_scan(cum_gt[:, :], ones[:, :], is_gt[:, :], 0.0, ALU.mult, ALU.add)
            L(nc.vector.tensor_tensor_scan(cum_eq[:, :], ones[:, :], is_eq[:, :], 0.0, ALU.mult, ALU.add))
            nc.vector.tensor_copy(totals[:, 0:1], cum_gt[:, T - 1:T]).then_inc(sem("moe_totals"), 1)
            nc.vector.tensor_copy(totals[:, 1:2], cum_eq[:, T - 1:T]).then_inc(sem("moe_totals"), 1)
            dve.wait_ge(sem("moe_offset_raw"), 1)
            nc.vector.tensor_copy(offset[:, 0:1], bank[6][:, 0:1])
            L(nc.vector.tensor_tensor(offset[:, 1:2], bank[6][:, 1:2], cut4[:, 1:2], ALU.add))
            L(nc.vector.scalar_tensor_tensor(cum_gt[:, :], cum_gt[:, :], offset[:, 0:1], is_gt[:, :], ALU.add, ALU.mult))
            L(nc.vector.scalar_tensor_tensor(cum_eq[:, :], cum_eq[:, :], offset[:, 1:2], is_eq[:, :], ALU.add, ALU.mult))
            nc.vector.tensor_tensor(cum_gt[:, :], cum_gt[:, :], cum_eq[:, :], ALU.add).then_inc(sem("moe_placed"), 1)
            dve.wait_ge(sem("moe_placeT"), 1)
            placeT = bank[7][:, :].rearrange("p (g j e) -> p j g e", g=4, j=B)
            for k in range(2):
                last = nc.vector.tensor_tensor(looked[:, k, :, :].rearrange("p (j g) e -> p j g e", j=B),
                                               onehot[:, k, :, :].rearrange("p (j g) e -> p j g e", j=B), placeT, ALU.mult)
            L(last)
            L(nc.vector.tensor_reduce(place[:, :, :], looked[:, :, :, :], AX_X, ALU.add))
            L(nc.vector.tensor_scalar(valid[:, :, :], place[:, :, :], 1.0, None, ALU.is_ge))
            L(nc.vector.scalar_tensor_tensor(valid[:, :, :], place[:, :, :], float(CAP), valid[:, :, :],
                                             ALU.is_le, ALU.mult))
            L(nc.vector.scalar_tensor_tensor(slot[:, :, :], pick[:, :, :], float(CAP), place[:, :, :],
                                             ALU.mult, ALU.add))
            L(nc.vector.scalar_tensor_tensor(slot[:, :, :], slot[:, :, :], -1.0 - DUMP, valid[:, :, :],
                                             ALU.add, ALU.mult))
            L(nc.vector.tensor_scalar(slot[:, :, :], slot[:, :, :], float(DUMP), None, ALU.add))
            nc.vector.tensor_copy(slot_u[:, :, :], slot[:, :, :]).then_inc(sem("moe_slots"), 1)
            L(nc.vector.tensor_tensor(weight[:, :, :], weight[:, :, :], valid[:, :, :], ALU.mult))

            def groups_dve(i, s):
                for u in range(2):
                    for q in range(2):
                        dve.wait_ge(sem(f"moe_silued{u}"), i * 6 + (3 * s + q + 1))
                        nc.vector.tensor_tensor(moe_act[u][:, q, :].rearrange("p (j c) -> p j c", j=2),
                                                moe_silu[u][:, q, :].rearrange("p (j c) -> p j c", j=2),
                                                up(u, q, 2), ALU.mult) \
                          .then_inc(sem(f"moe_acted{u}"), 1)
                    dve.wait_ge(sem(f"moe_silued{u}"), i * 6 + (3 * s + 3))
                    nc.vector.scalar_tensor_tensor(moe_act[u][:, 2, :], moe_silu[u][:, 2, :], 0.05,
                                                   bank[4 + u][:, 2 * CAP:4 * CAP], ALU.mult, ALU.mult) \
                      .then_inc(sem(f"moe_acted{u}"), 1)
                for u in range(2):
                    dve.wait_ge(sem(f"moe_y{u}"), i * 2 + (s + 1))
                    dve.wait_ge(sem(f"moe_stored{u}"), i * 32 + (16 * s + 16))
                    nc.vector.tensor_copy(y_slot[u][:, :, :],
                                          bank[6 + u][0:CAP, 0:2 * C].rearrange("p (q c) -> p q c", q=2)) \
                      .then_inc(sem(f"moe_y_read{u}"), 1)

            with dve.Fori(0, G // 4) as i:
                for s in range(2):
                    groups_dve(i, s)

        def moe_out_dve(dve, b):
            def L(ins):
                link(dve, "dve", ins)

            dve.wait_ge(sem(f"y_gathered{b}"), 16 * 2 * TB)
            for t in range(TB * b, TB * b + TB):
                last = nc.vector.tensor_scalar(y_sum[:, t, :], y_tok[:, 0, t, :], weight[:, 0, t:t + 1], None,
                                               ALU.mult)
            L(last)
            for t in range(TB * b, TB * b + TB):
                last = nc.vector.scalar_tensor_tensor(y_sum[:, t, :], y_tok[:, 1, t, :], weight[:, 1, t:t + 1],
                                                      y_sum[:, t, :], ALU.mult, ALU.add)
            last.then_inc(sem("y_summed"), 1)
            dve.wait_ge(sem("moe_out"), b + 1)
            nc.vector.scalar_tensor_tensor(x[:, b, :], bank[4 + b][:, :], gate(3, b), x[:, b, :],
                                           ALU.mult, ALU.add).then_inc(sem("x_ready"), 1)

        def moe_sp(sp):
            for name, dst in (("r1_c", r1_c), ("r1_s", r1_s), ("r2_w", r2_w), ("iota_e", iota_e),
                              ("chunk_sum", chunk_sum)):
                sp.dma_start(dst[:, :], d[name]).then_inc(sem("moe_loaded"), 16)
            sp.wait_ge(sem("filled"), 2)
            for s in range(NB128 // 4):
                sp.dma_start(xg_dram[512 * s:512 * s + 512, :].rearrange("(p r) c -> p (r c)", p=128),
                             zeros[:, :]).then_inc(sem("moe_zeroed"), 16)
            for u in range(2):
                sp.dma_start(y_dram[SLOTS:SLOTS + 1, 64 * u:64 * u + 64], zeros[0:1, 0:64]) \
                  .then_inc(sem(f"moe_stored{u}"), 16)
            for u in range(2):
                sp.dma_start(moe_w[u][:, :], d["moe_w"][u, :, :]).then_inc(sem(f"moe_w_loaded{u}"), 16)
            sp.wait_ge(sem("moe_best"), 1)
            for j in range(B):
                sp.dma_start(cand[0][:, j, :], best[E * j:E * j + E, :]).then_inc(sem("moe_spread"), 16)
            for u in range(2, 4):
                sp.dma_start(moe_w[u][:, :], d["moe_w"][u, :, :]).then_inc(sem(f"moe_w_loaded{u}"), 16)
            sp.wait_ge(sem("moe_cut"), 1)
            for j in range(B):
                sp.dma_start(cut4[E * j:E * j + E, :], cut[:, :]).then_inc(sem("moe_spread"), 16)
            sp.wait_ge(sem("xg_scattered"), 16 * 2 * TILES)
            sp.dma_start(xg[:, :, :], xg_dram.rearrange("(s p) c -> p s c", p=128)).then_inc(sem("xg_loaded"), 16)

            def store(i, s, u):
                sp.wait_ge(sem(f"moe_y_read{u}"), i * 2 + (s + 1))
                row = i * (8 * CAP) + (4 * s + 2 * u) * CAP
                rows = slice(row, row + 2 * CAP) if isinstance(i, int) else bass.ds(row, 2 * CAP)
                sp.dma_start(y_dram[rows, :].rearrange("(q p) c -> p q c", q=2), y_slot[u][:, :, :]) \
                  .then_inc(sem(f"moe_stored{u}"), 16)

            with sp.Fori(0, G // 4 - 1) as i:
                for s, u in ((0, 0), (0, 1), (1, 0), (1, 1)):
                    sp.wait_ge(sem(f"moe_y{u}"), i * 2 + (s + 1))
                    sp.dma_start(moe_w[2 * s + u][:, :], d["moe_w"][bass.ds(i * 4 + (4 + 2 * s + u), 1), :, :]
                                 .rearrange("o p w -> (o p) w")).then_inc(sem(f"moe_w_loaded{2 * s + u}"), 16)
                    store(i, s, u)
            for s, u in ((0, 0), (0, 1), (1, 0), (1, 1)):
                store(G // 4 - 1, s, u)

        def moe_pool(pool):
            pool.wait_ge(sem("moe_slots"), 1)
            pool.wait_ge(sem("moe_zeroed"), 16 * (NB128 // 4))
            for t in range(TILES):
                for k in range(2):
                    nc.gpsimd.indirect_dma_start(
                        xg_dram, bass.IndirectOffsetOnAxis(slot_u[:, k, t:t + 1], 0), htok[:, t, :], None,
                        bounds_check=SLOTS - 1, oob_is_err=False).then_inc(sem("xg_scattered"), 16)
            for u in range(2):
                pool.wait_ge(sem(f"moe_stored{u}"), 16 * (G // 2) + 16)
            for t in range(TILES):
                for k in range(2):
                    nc.gpsimd.indirect_dma_start(
                        y_tok[:, k, t, :], None, y_dram, bass.IndirectOffsetOnAxis(slot_u[:, k, t:t + 1], 0)) \
                      .then_inc(sem(f"y_gathered{t // TB}"), 16)

        next_block()
        q_diag = [tmp_sb(f"q_diag{i}", [128, NBLK, 128]) for i in range(2)]
        k_rope = [tmp_sb(f"k_rope{i}", [128, T]) for i in range(2)]
        rope_part = [tmp_sb(f"rope_part{i}", [128, T]) for i in range(4)]
        v_tok = [tmp_sb(f"v_tok{i}", [128, TB, 128]) for i in range(B)]
        soft = [tmp_sb(f"soft{i}", [128, PW]) for i in range(2)]
        softT = tmp_sb("softT", [128, NFILL * 512])
        neg_max = tmp_sb("neg_max", [128, 2, NBLK])
        exp_sum = tmp_sb("exp_sum", [128, 2, NBLK])
        exp_inv = tmp_sb("exp_inv", [128, 2, NBLK])
        head_out = [tmp_sb(f"head_out{i}", [128, T]) for i in range(2)]
        gate_bo = tmp_sb("gate_bo", [128, B])
        att_wo = tmp_sb("att_wo", [128, C])

        def keys(j):
            return 64 * (j + 1)

        def att_loop(eng, part):
            part(0, 0, True, True, True, True, False)
            with eng.Fori(0, PAIRS * B // UNROLL - 1) as i:
                for u in range(UNROLL):
                    part(i, u, False, True, True, True, False)
                    part(i, u + 1, True, True, True, True, True)
            i = PAIRS * B // UNROLL - 1
            for u in range(UNROLL):
                left = UNROLL - 1 - u
                part(i, u, False, left >= 1, left >= 2, True, False)
                part(i, u + 1, True, left >= 2, left >= 3, left >= 1, True)

        def att_project(pe, i, u, piece):
            b, p = u % B, u // B % 2
            pe.wait_ge(sem(f"w_loaded{p}"), i * 16 + (16 * (u // UNROLL) + 16))
            if not isinstance(i, int) or u or piece:
                pe.wait_ge(sem("proj_read"), i * (3 * UNROLL) + (3 * u + piece))
            if piece < 2:
                last = pe.matmul(bank[0][:, :], att_w[p][:, piece, :], hb(b), start=True, stop=True)
            else:
                for t in range(TB):
                    last = pe.matmul(bank[0][:, 128 * t:128 * t + 128], hh(b, 128 * t, 128), att_w[p][:, 2, :],
                                     start=True, stop=True)
            last.then_inc(sem("proj_raw"), 1)

        def att_scores(pe, i, u, g, first=False):
            par = u % 2
            if g == 0:
                pe.wait_ge(sem("roped"), i * (5 * UNROLL) + (5 * u + 5))
            back = next(k for k in range(1, 10) if SBANKS[(5 * par + g - k) % 10] == SBANKS[5 * par + g])
            units, g1 = divmod(g - back, 5)
            if not first or units == 0:
                pe.wait_ge(sem("s_exp"), i * (8 * UNROLL) + (8 * (u + units) + GCUM[g1]))
            at = 0
            for j in GROUPS[g]:
                last = pe.matmul(bank[SBANKS[5 * par + g]][:, at:at + keys(j)], q_diag[par][:, j, :],
                                 k_rope[par][:, 0:keys(j)], start=True, stop=True)
                at += keys(j)
            last.then_inc(sem("s_raw"), 1)

        def att_transpose(pe, i, u, f):
            if f == 0:
                pe.wait_ge(sem("p_normed"), i * UNROLL + (u + 1))
            if f >= 2:
                pe.wait_ge(sem("pt_ready"), i * (5 * UNROLL) + (5 * u + f - 1))
            for q in range(4 * f, 4 * f + 4):
                jc, j = CHUNKS[q]
                last = pe.transpose(bank[3 + (u + f) % 2][:, 128 * (q % 4):128 * (q % 4) + 128],
                                    soft[u % 2][:, POFF[j] + 128 * jc:POFF[j] + 128 * jc + 128], ident[:, :])
            last.then_inc(sem("pt_raw"), 1)

        def att_values(pe, i, u):
            pe.wait_ge(sem("pair_added"), i * UNROLL + (u + B))
            for half in range(2):
                pe.wait_ge(sem("pt_ready"), i * (5 * UNROLL) + (5 * u + (5 if half else 3)))
                js = range(4 * half, 4 * half + 4)
                for jc in range(2 * half + 2):
                    q = [a for a, (c, j) in enumerate(CHUNKS) if c == jc and j in js]
                    lo = 128 * (CHUNKS[q[0]][1] - 4 * half)
                    last = pe.matmul(bank[5 + half][:, lo:512], v_tok[u % B][:, jc, :],
                                     softT[:, 128 * q[0]:128 * q[-1] + 128], start=(jc == 0), stop=(jc == 2 * half + 1))
                last.then_inc(sem("pv_raw"), 1)

        def att_output(pe, i, u):
            pe.wait_ge(sem("wo_loaded"), i * (16 * UNROLL // B) + (16 * (u // B) + 16))
            pe.wait_ge(sem("pv_read"), i * (4 * UNROLL) + (4 * u + 4))
            pe.matmul(bank[5][:, :], att_wo[:, :], head_out[u % 2][:, :], start=True, stop=True) \
              .then_inc(sem("att_out"), 1)

        def att_pe(pe):
            pe.wait_ge(sem("h_ready"), 20)
            pe.wait_ge(sem("ln_normed"), 20)

            def part(i, u, early, scores, project, work, out):
                for g in range(2) if early else range(2, 5):
                    if scores:
                        att_scores(pe, i, u + 1, g)
                    if project and g % 2 == 0:
                        att_project(pe, i, u + 2, g // 2)
                    if out and g == 0:
                        att_output(pe, i, u - 1)
                    if work and g:
                        att_transpose(pe, i, u, g - 1)
                if not early:
                    att_transpose(pe, i, u, 4)
                    att_values(pe, i, u)

            for g in range(3):
                att_project(pe, 0, 0, g)
            for g in range(5):
                att_scores(pe, 0, 0, g, first=True)
                if g < 3:
                    att_project(pe, 0, 1, g)
            att_loop(pe, part)

        def att_exps(act, i, u, g):
            par = u % 2
            act.wait_ge(sem("s_max"), i * (8 * UNROLL) + (8 * u + GCUM[g]))
            at = 0
            for j in GROUPS[g]:
                nc.scalar.activation(soft[par][:, POFF[j]:POFF[j] + keys(j)],
                                     bank[SBANKS[5 * par + g]][:, at:at + keys(j)], ACT.Exp,
                                     bias=neg_max[:, par, j:j + 1], accum_out=exp_sum[:, par, j:j + 1]) \
                  .then_inc(sem("s_exp"), 1)
                at += keys(j)

        def att_v(act, i, u):
            act.wait_ge(sem("proj_raw"), i * (3 * UNROLL) + (3 * u + 3))
            nc.scalar.activation(v_tok[u % B][:, :, :], bank[0][:, :].rearrange("p (i c) -> p i c", i=TB), ACT.Copy) \
              .then_inc(sem("proj_read"), 1)

        def att_act(act):
            nc.scalar.preload_act_table_set("natural_log_exp_and_others")

            def transposed(i, u, f):
                if f == 0:
                    act.wait_ge(sem("pv_raw"), i * (2 * UNROLL) + (2 * u + B))
                act.wait_ge(sem("pt_raw"), i * (5 * UNROLL) + (5 * u + f + 1))
                nc.scalar.activation(softT[:, 512 * f:512 * f + 512], bank[3 + (u + f) % 2][:, :], ACT.Copy) \
                  .then_inc(sem("pt_ready"), 1)

            def part(i, u, early, scores, project, work, out):
                for g in range(2) if early else range(2, 5):
                    if work and g:
                        transposed(i, u, g - 1)
                    if scores:
                        att_exps(act, i, u + 1, g)
                if not early:
                    transposed(i, u, 4)
                    if project:
                        att_v(act, i, u + 2)

            att_v(act, 0, 0)
            for g in range(5):
                att_exps(act, 0, 0, g)
            att_v(act, 0, 1)
            att_loop(act, part)

        def att_rope(dve, i, u, piece, first=False):
            dve.wait_ge(sem("proj_raw"), i * (3 * UNROLL) + (3 * u + piece + 1))
            if not first:
                dve.wait_ge(sem("roped"), i * (5 * UNROLL) + (5 * u + (0 if piece else -2)))
            nc.vector.tensor_tensor(rope_part[2 * piece][:, :], bank[0][:, :], rope_tab[:, 2 * piece, :], ALU.mult)
            nc.vector.stream_shuffle(rope_part[2 * piece + 1][:, :], bank[0][:, :], SWAP) \
              .then_inc(sem("proj_read"), 1)

        def att_maxes(dve, i, u, g):
            par = u % 2
            dve.wait_ge(sem("s_raw"), i * (5 * UNROLL) + (5 * u + g + 1))
            at = 0
            for j in GROUPS[g]:
                s = bank[SBANKS[5 * par + g]][:, at:at + keys(j)]
                nc.vector.tensor_tensor(s[:, keys(j) - 64:keys(j)], s[:, keys(j) - 64:keys(j)], att_mask[:, :],
                                        ALU.add).then_inc(sem("s_masked"), 1)
                at += keys(j)
            at = 0
            for k, j in enumerate(GROUPS[g]):
                s = bank[SBANKS[5 * par + g]][:, at:at + keys(j)]
                dve.wait_ge(sem("s_masked"), i * (8 * UNROLL) + (8 * u + GCUM[g] - len(GROUPS[g]) + k + 1))
                nc.vector.tensor_reduce(neg_max[:, par, j:j + 1], s, AX_X, ALU.max, negate=True) \
                  .then_inc(sem("s_max"), 1)
                at += keys(j)

        def att_norm(dve, i, u):
            par = u % 2
            dve.wait_ge(sem("s_exp"), i * (8 * UNROLL) + (8 * u + 8))
            nc.vector.reciprocal(exp_inv[:, par, :], exp_sum[:, par, :]).then_inc(sem("s_inv"), 1)
            dve.wait_ge(sem("s_inv"), i * UNROLL + (u + 1))
            for j in range(NBLK):
                p = soft[par][:, POFF[j]:POFF[j] + keys(j)]
                last = nc.vector.tensor_scalar(p, p, exp_inv[:, par, j:j + 1], None, ALU.mult)
            last.then_inc(sem("p_normed"), 1)

        def att_heads(dve, i, u):
            for half in range(2):
                dve.wait_ge(sem("pv_raw"), i * (2 * UNROLL) + (2 * u + B + half + 1))
                for hd in range(2):
                    lo = 64 * hd
                    nc.vector.tensor_copy(
                        head_out[u % 2][lo:lo + 64, 256 * half:256 * half + 256].rearrange("p (j i) -> p j i", j=4),
                        bank[5 + half][lo:lo + 64, :].rearrange("p (j h i) -> p j h i", j=4, h=2)[:, :, hd, :]) \
                      .then_inc(sem("pv_read"), 1)

        def att_add(dve, i, u):
            b = u % B
            dve.wait_ge(sem("att_out"), i * UNROLL + (u + 1))
            dve.wait_ge(sem("pair_added"), i * UNROLL + (u + 1))
            nc.vector.scalar_tensor_tensor(x[:, b, :], bank[5][:, :], gate(4, b), x[:, b, :], ALU.mult, ALU.add) \
              .then_inc(sem("pair_added"), 1)

        def att_dve(dve):
            def part(i, u, early, scores, project, work, out):
                for g in range(2) if early else range(2, 5):
                    if scores:
                        att_maxes(dve, i, u + 1, g)
                    if project and g in (0, 2):
                        att_rope(dve, i, u + 2, g // 2)
                if out:
                    att_add(dve, i, u - 1)
                if not early:
                    if scores:
                        att_norm(dve, i, u + 1)
                    att_heads(dve, i, u)

            link(dve, "dve", nc.vector.tensor_scalar(gate_bo[:, :], mod[:, 2, 2, :], v("attn2_bo"), None, ALU.mult))
            for b in range(B):
                dve.wait_ge(sem("h_ready"), 16 + b + 1)
                nc.vector.tensor_scalar(x[:, b, :], x[:, b, :], gate_bo[:, b:b + 1], None, ALU.add) \
                  .then_inc(sem("pair_added"), 1)
            dve.wait_ge(sem("att_tables"), 32)
            for g in range(2):
                att_rope(dve, 0, 0, g, first=True)
            for g in range(5):
                att_maxes(dve, 0, 0, g)
                if g < 2:
                    att_rope(dve, 0, 1, g)
            dve.wait_ge(sem("att_zeroed"), 2 + NBLK)
            att_norm(dve, 0, 0)
            att_loop(dve, part)

        def att_sum(pool, i, u, first=False):
            par = u % 2

            def rotated(k):
                pool.wait_ge(sem("roped"), i * (5 * UNROLL) + (5 * u + k))

            if not first:
                pool.wait_ge(sem("s_raw"), i * (5 * UNROLL) + (5 * u - 5))
            pool.wait_ge(sem("proj_read"), i * (3 * UNROLL) + (3 * u + 1))
            nc.gpsimd.tensor_tensor(rope_part[1][:, :], rope_part[1][:, :], rope_tab[:, 1, :], ALU.mult) \
              .then_inc(sem("roped"), 1)
            for hd in range(2):
                lo = 64 * hd
                rotated(1 + hd)
                nc.gpsimd.tensor_tensor(q_diag[par][lo:lo + 64, :, lo:lo + 64],
                                        rope_part[0][lo:lo + 64, :].rearrange("p (j i) -> p j i", i=64),
                                        rope_part[1][lo:lo + 64, :].rearrange("p (j i) -> p j i", i=64), ALU.add) \
                  .then_inc(sem("roped"), 1)
            pool.wait_ge(sem("proj_read"), i * (3 * UNROLL) + (3 * u + 2))
            rotated(3)
            nc.gpsimd.tensor_tensor(rope_part[3][:, :], rope_part[3][:, :], rope_tab[:, 3, :], ALU.mult) \
              .then_inc(sem("roped"), 1)
            rotated(4)
            nc.gpsimd.tensor_tensor(k_rope[par][:, :], rope_part[2][:, :], rope_part[3][:, :], ALU.add) \
              .then_inc(sem("roped"), 1)

        def att_pool(pool):
            def part(i, u, early, scores, project, work, out):
                if project and not early:
                    att_sum(pool, i, u + 2)

            for i in range(2):
                nc.gpsimd.memset(q_diag[i][:, :, :], 0.0).then_inc(sem("att_zeroed"), 1)
                for j in range(0, NBLK, 2):
                    end = POFF[j] + keys(j)
                    nc.gpsimd.memset(soft[i][:, end:end + 64], 0.0).then_inc(sem("att_zeroed"), 1)
            pool.wait_ge(sem("att_zeroed"), 2 + NBLK)
            pool.wait_ge(sem("att_tables"), 32)
            att_sum(pool, 0, 0, first=True)
            att_sum(pool, 0, 1, first=True)
            att_loop(pool, part)

        def att_sp(sp):
            sp.wait_ge(sem("h_ready"), 17)
            sp.dma_start(att_wo[:, :], d["att_wo"][0, :, :]).then_inc(sem("wo_loaded"), 16)

            def next_wo(i, p):
                sp.wait_ge(sem("att_out"), i * UNROLL + (B * p + B))
                wo = d["att_wo"][i * 2 + p + 1, :, :] if isinstance(i, int) else \
                    d["att_wo"][bass.ds(i * 2 + (p + 1), 1), :, :].rearrange("o p n -> (o p) n")
                sp.dma_start(att_wo[:, :], wo).then_inc(sem("wo_loaded"), 16)

            with sp.Fori(0, PAIRS // 2 - 1) as i:
                for p in range(2):
                    sp.wait_ge(sem("proj_raw"), i * (3 * UNROLL) + (12 * p + 12))
                    sp.dma_start(att_w[p][:, :, :], d["att_w"][bass.ds(i * 2 + (p + 2), 1), :, :, :]
                                 .rearrange("o p j n -> (o p) j n")).then_inc(sem(f"w_loaded{p}"), 16)
                    next_wo(i, p)
            next_wo(PAIRS // 2 - 1, 0)

        next_block()
        mix_move = tmp_sb("mix_move", [C, 2, T])
        mix_r = tmp_sb("mix_r", [C, 2, T])
        mix_k = tmp_sb("mix_k", [C, 2, T])
        mix_gate = tmp_sb("mix_gate", [C, 2, T])
        mix_square = tmp_sb("mix_square", [C, 2, T])

        def mix_pool(pool):
            for b in range(B):
                pool.wait_ge(sem("h_ready"), 20 + b + 1)
                if b >= 2:
                    pool.wait_ge(sem("mix_in"), 2 * b - 2)
                nc.gpsimd.tensor_tensor(mix_move[:, b % 2, :], hb(b), hh(b, -1, T), ALU.subtract) \
                  .then_inc(sem("mix_moved"), 1)

        def mix_dve(dve):
            def inputs(b):
                dve.wait_ge(sem("mix_moved"), b + 1)
                if b >= 2:
                    dve.wait_ge(sem("mix_kr"), b - 1)
                for dst, mu in ((mix_r, "mu_r"), (mix_k, "mu_k")):
                    nc.vector.scalar_tensor_tensor(dst[:, b % 2, :], mix_move[:, b % 2, :], v(mu), hh(b, -1, T),
                                                   ALU.mult, ALU.add).then_inc(sem("mix_in"), 1)
                dve.wait_ge(sem("mix_in"), 2 * b + 2)

            inputs(0)
            for b in range(B):
                if b + 1 < B:
                    inputs(b + 1)
                dve.wait_ge(sem("mix_v"), b + 1)
                dve.wait_ge(sem("mix_gated"), b + 1)
                link(dve, "dve", nc.vector.tensor_tensor(mix_gate[:, b % 2, :], bank[6][:, :], mix_gate[:, b % 2, :],
                                                         ALU.mult))
                nc.vector.scalar_tensor_tensor(x[:, b, :], mix_gate[:, b % 2, :], gate(5, b), x[:, b, :],
                                               ALU.mult, ALU.add).then_inc(sem("x_ready"), 1)

        def mix_act(act):
            for b in range(B):
                if b >= 2:
                    act.wait_ge(sem("x_ready"), 16 + b - 1)
                act.wait_ge(sem("mix_kr"), b + 1)
                nc.scalar.activation(mix_square[:, b % 2, :], bank[4][:, :], ACT.Relu).then_inc(sem("mix_relued"), 1)
                act.wait_ge(sem("mix_relued"), b + 1)
                nc.scalar.activation(mix_square[:, b % 2, :], mix_square[:, b % 2, :], ACT.Square) \
                  .then_inc(sem("mix_squared"), 1)
                nc.scalar.activation(mix_gate[:, b % 2, :], bank[5][:, :], ACT.Sigmoid).then_inc(sem("mix_gated"), 1)

        def mix_pe(pe):
            pe.wait_ge(sem("early_loaded"), 96)
            for b in range(B):
                pe.wait_ge(sem("mix_in"), 2 * b + 2)
                if b:
                    pe.wait_ge(sem("mix_squared"), b)
                    pe.wait_ge(sem("mix_gated"), b)
                pe.matmul(bank[4][:, :], mix_w[:, 1, :], mix_k[:, b % 2, :], start=True, stop=True)
                pe.matmul(bank[5][:, :], mix_w[:, 0, :], mix_r[:, b % 2, :], start=True, stop=True) \
                  .then_inc(sem("mix_kr"), 1)
                pe.wait_ge(sem("mix_squared"), b + 1)
                if b:
                    pe.wait_ge(sem("x_ready"), 16 + b)
                pe.matmul(bank[6][:, :], mix_w[:, 2, :], mix_square[:, b % 2, :], start=True, stop=True) \
                  .then_inc(sem("mix_v"), 1)

        class Window:
            def __init__(self, units, start, per, loaded, tables=None, slopes=False):
                self.units, self.start, self.per = units, start, per
                self.loaded = loaded
                self.tables, self.slopes = tables, slopes
                self.ssq_reader = "win_clip" if per["win_clip"] else "win_log"

            def at(self, name, i, u, k=0):
                return i * (UNROLL * self.per[name]) + (u * self.per[name] + self.start[name] + k)

            def after(self):
                return {m: self.start[m] + self.units * c for m, c in self.per.items()}

        ROTATED = {"win_proj": 4, "win_proj_read": 2, "win_v_read": 2, "win_sq": 2, "win_ssq": 2, "win_clip": 2, "win_log": 2,
                   "win_rs": 2, "win_sum": 4, "win_q": 2, "win_k": 1, "win_s": 2, "win_biased": 2, "win_max": 2,
                   "win_exp": 8, "win_inv": 1, "win_normed": 1, "win_pt": 2, "win_pt_read": 2, "pv_raw": 2,
                   "win_pv_read": 4, "win_out": 1, "pair_added": 1}
        PLAIN = dict(ROTATED, win_proj=1, win_proj_read=0, win_v_read=0, win_sq=1, win_ssq=1, win_clip=0, win_log=1, win_rs=1,
                     win_sum=0, win_k=0)

        def win_alloc(pieces, own_kv, keys):
            a = {"q": [tmp_sb(f"win_q{i}_{pieces}", [128, NBLK, 128]) for i in range(2)],
                 "keys": keys,
                 "soft": [tmp_sb(f"win_soft{i}_{pieces}", [128, NBLK, keys]) for i in range(2)],
                 "softT": tmp_sb(f"win_softT_{pieces}", [128, NBLK * 128]),
                 "neg_max": tmp_sb(f"win_neg_max_{pieces}", [128, 2, NBLK]),
                 "sum": tmp_sb(f"win_sum_{pieces}", [128, 2, NBLK]),
                 "inv": tmp_sb(f"win_inv_{pieces}", [128, 2, NBLK]),
                 "out": [tmp_sb(f"win_out{i}_{pieces}", [128, T]) for i in range(2)],
                 "w": [tmp_sb(f"win_w{i}_{pieces}", [C, pieces, 128]) for i in range(2)],
                 "wo": tmp_sb(f"win_wo_{pieces}", [128, C]),
                 "bias": tmp_sb(f"win_bias_{pieces}", [128, NBLK, keys]),
                 "sq": tmp_sb(f"win_sq_{pieces}", [128, 2, T]),
                 "log": tmp_sb(f"win_log_{pieces}", [128, 2, T]),
                 "rs": tmp_sb(f"win_rs_{pieces}", [128, 2, T])}
            if own_kv:
                a["part"] = [tmp_sb(f"win_part{i}", [128, T]) for i in range(4)]
                a["k"] = [tmp_sb(f"win_k{i}", [128, TP]) for i in range(2)]
                a["v"] = [tmp_sb(f"win_v{i}", [128, NBLK, 128]) for i in range(B)]
            return a

        def proj_bank(W, u, piece):
            return bank[5 * ((u if W.per["win_proj"] == 1 else piece) % 2)]

        def win_loop(W, eng, part):
            for early in (True, False):
                part(0, -2, early, False, True, False, False, True)
            for early in (True, False):
                part(0, -1, early, True, True, False, False, True)
            part(0, 0, True, True, True, True, False, False)
            rounds = W.units // UNROLL
            with eng.Fori(0, rounds - 1) as i:
                for u in range(UNROLL):
                    part(i, u, False, True, True, True, False, False)
                    part(i, u + 1, True, True, True, True, True, False)
            for u in range(UNROLL):
                left = UNROLL - 1 - u
                part(rounds - 1, u, False, left >= 1, left >= 2, True, False, False)
                part(rounds - 1, u + 1, True, left >= 2, left >= 3, left >= 1, True, False)

        def win_pe(pe, W, a, tokens, keys_of, values_of):
            pieces = W.per["win_proj"]

            def project(i, u, piece, first):
                b, p = u % B, u // B % 2
                pe.wait_ge(sem(f"w_loaded{p}"), i * 16 + (16 * (u // UNROLL) + 16 + 8 * W.loaded))
                dst = proj_bank(W, u, piece)
                if pieces == 1:
                    if not first:
                        pe.wait_ge(sem("win_q"), W.at("win_q", i, u, -2))
                elif piece >= 2:
                    pe.wait_ge(sem("win_proj_read"), W.at("win_proj_read", i, u, piece - 1))
                elif u or not first:
                    pe.wait_ge(sem("win_v_read"), W.at("win_v_read", i, u, piece - 1))
                if piece < 2:
                    last = pe.matmul(dst[:, :], a["w"][p][:, piece, :], tokens(b, 0, T), start=True, stop=True)
                else:
                    for k in range(4):
                        j = 4 * (piece - 2) + k
                        last = pe.matmul(dst[:, 128 * k:128 * k + 128], tokens(b, 64 * j - 64, 128),
                                         a["w"][p][:, 2, :], start=True, stop=True)
                last.then_inc(sem("win_proj"), 1)

            def square_sum(i, u, j, first):
                pe.wait_ge(sem("win_sq"), W.at("win_sq", i, u, j + 1))
                if j == 0 and (u or not first):
                    pe.wait_ge(sem(W.ssq_reader), W.at(W.ssq_reader, i, u))
                if j and not first:
                    pe.wait_ge(sem("win_pv_read"), W.at("win_pv_read", i, u, -8))
                elif j and u:
                    pe.wait_ge(sem("win_clip"), W.at("win_clip", i, u))
                pe.matmul(bank[7 if j else 1][:, :], head_sum[:, :], a["sq"][:, j, :], start=True, stop=True) \
                  .then_inc(sem("win_ssq"), 1)

            def scores(i, u, half, first):
                if half == 0:
                    pe.wait_ge(sem("win_q"), W.at("win_q", i, u, 2))
                    if W.per["win_k"]:
                        pe.wait_ge(sem("win_k"), W.at("win_k", i, u, 1))
                if not first:
                    pe.wait_ge(sem("win_exp"), W.at("win_exp", i, u, 4 * half - 4))
                for j in range(4 * half, 4 * half + 4):
                    last = pe.matmul(bank[2 + half][:, 128 * (j % 4):128 * (j % 4) + a["keys"]], a["q"][u % 2][:, j, :],
                                     keys_of(u % UNROLL, j), start=True, stop=True)
                last.then_inc(sem("win_s"), 1)

            def transpose(i, u, half):
                if half == 0:
                    pe.wait_ge(sem("win_normed"), W.at("win_normed", i, u, 1))
                else:
                    pe.wait_ge(sem("win_pt_read"), W.at("win_pt_read", i, u, 1))
                for j in range(4 * half, 4 * half + 4):
                    last = pe.transpose(bank[4][0:a["keys"], 128 * (j % 4):128 * (j % 4) + 128],
                                        a["soft"][u % 2][:, j, :], ident[:, :])
                last.then_inc(sem("win_pt"), 1)

            def values(i, u, half, lookahead):
                if half == 0:
                    pe.wait_ge(sem("pair_added"), W.at("pair_added", i, u))
                elif lookahead and pieces > 1:
                    pe.wait_ge(sem("win_clip"), W.at("win_clip", i, u + 2, 2))
                pe.wait_ge(sem("win_pt_read"), W.at("win_pt_read", i, u, half + 1))
                for j in range(4 * half, 4 * half + 4):
                    last = pe.matmul(bank[6 + half][:, 128 * (j % 4):128 * (j % 4) + 128],
                                     values_of(u % UNROLL, j), a["softT"][0:a["keys"], 128 * j:128 * j + 128],
                                     start=True, stop=True)
                last.then_inc(sem("pv_raw"), 1)

            def output(i, u):
                pe.wait_ge(sem("wo_loaded"), i * (16 * UNROLL // B) + (16 * (u // B) + 16 + 16 * W.loaded))
                pe.wait_ge(sem("win_pv_read"), W.at("win_pv_read", i, u, 4))
                pe.matmul(bank[6][:, :], a["wo"][:, :], a["out"][u % 2][:, :], start=True, stop=True) \
                  .then_inc(sem("win_out"), 1)

            def part(i, u, early, s, p, work, out, first):
                if early:
                    if p:
                        project(i, u + 2, 0, first)
                    if s:
                        scores(i, u + 1, 0, first)
                    if p and pieces > 1:
                        project(i, u + 2, 1, first)
                    if p:
                        square_sum(i, u + 2, 0, first)
                    if out:
                        output(i, u - 1)
                    if p and pieces > 1:
                        square_sum(i, u + 2, 1, first)
                    if work:
                        transpose(i, u, 0)
                    return
                if s:
                    scores(i, u + 1, 1, first)
                if p and pieces > 1:
                    project(i, u + 2, 2, first)
                if work:
                    transpose(i, u, 1)
                    values(i, u, 0, p)
                if p and pieces > 1:
                    project(i, u + 2, 3, first)
                if work:
                    values(i, u, 1, p)

            win_loop(W, pe, part)

        def win_act(act, W, a):
            pieces = W.per["win_proj"]
            nc.scalar.preload_act_table_set("natural_log_exp_and_others")

            def square(i, u, j, first):
                act.wait_ge(sem("win_proj"), W.at("win_proj", i, u, j + 1))
                if not first:
                    act.wait_ge(sem("win_ssq"), W.at("win_ssq", i, u, j + 1 - W.per["win_ssq"]))
                nc.scalar.activation(a["sq"][:, j, :], proj_bank(W, u, j)[:, :], ACT.Square).then_inc(sem("win_sq"), 1)

            def norm(i, u, j, first):
                if W.per["win_clip"]:
                    act.wait_ge(sem("win_clip"), W.at("win_clip", i, u, j + 1))
                    nc.scalar.activation(a["log"][:, j, :], a["sq"][:, j, :], ACT.Ln).then_inc(sem("win_log"), 1)
                else:
                    act.wait_ge(sem("win_ssq"), W.at("win_ssq", i, u, j + 1))
                    nc.scalar.activation(a["log"][:, j, :], bank[1][:, :], ACT.Ln, bias=rms_eps[:, 0:1],
                                         scale=1.0 / 64).then_inc(sem("win_log"), 1)
                act.wait_ge(sem("win_log"), W.at("win_log", i, u, j + 1))
                if not first:
                    name = "win_k" if j else "win_q"
                    act.wait_ge(sem(name), W.at(name, i, u))
                bias = ln_clip[:, 0:1] if W.per["win_clip"] else 0.0
                nc.scalar.activation(a["rs"][:, j, :], a["log"][:, j, :], ACT.Exp, scale=-0.5, bias=bias) \
                  .then_inc(sem("win_rs"), 1)

            def exps(i, u, half):
                act.wait_ge(sem("win_max"), W.at("win_max", i, u, half + 1))
                for k in range(4):
                    j = 4 * half + k
                    nc.scalar.activation(a["soft"][u % 2][:, j, :], bank[2 + half][:, 128 * k:128 * k + a["keys"]], ACT.Exp,
                                         bias=a["neg_max"][:, u % 2, j:j + 1], accum_out=a["sum"][:, u % 2, j:j + 1]) \
                      .then_inc(sem("win_exp"), 1)

            def transposed(i, u, half):
                if half == 0:
                    act.wait_ge(sem("pv_raw"), W.at("pv_raw", i, u))
                act.wait_ge(sem("win_pt"), W.at("win_pt", i, u, half + 1))
                nc.scalar.activation(a["softT"][0:a["keys"], 512 * half:512 * half + 512], bank[4][0:a["keys"], :], ACT.Copy) \
                  .then_inc(sem("win_pt_read"), 1)

            def take_values(i, u, half):
                act.wait_ge(sem("win_proj"), W.at("win_proj", i, u, 3 + half))
                nc.scalar.activation(a["v"][u % B][:, 4 * half:4 * half + 4, :],
                                     proj_bank(W, u, half)[:, :].rearrange("p (i c) -> p i c", i=4), ACT.Copy) \
                  .then_inc(sem("win_v_read"), 1)

            def heads(i, u):
                act.wait_ge(sem("pv_raw"), W.at("pv_raw", i, u, 2))
                for hd in range(2):
                    dst, src = win_head(a, u, 1, hd)
                    nc.scalar.activation(dst, src, ACT.Copy).then_inc(sem("win_pv_read"), 1)

            def part(i, u, early, s, p, work, out, first):
                if early:
                    if p:
                        square(i, u + 2, 0, first)
                        if pieces > 1:
                            square(i, u + 2, 1, first)
                        norm(i, u + 2, 0, first)
                    if work:
                        transposed(i, u, 0)
                    if s:
                        exps(i, u + 1, 0)
                    if p and pieces > 1:
                        norm(i, u + 2, 1, first)
                    return
                if p and pieces > 1:
                    take_values(i, u + 2, 0)
                if work:
                    transposed(i, u, 1)
                if s:
                    exps(i, u + 1, 1)
                if p and pieces > 1:
                    take_values(i, u + 2, 1)
                if work:
                    heads(i, u)

            win_loop(W, act, part)

        def win_head(a, u, half, hd):
            lo = 64 * hd
            return (a["out"][u % 2][lo:lo + 64, 256 * half:256 * half + 256].rearrange("p (j i) -> p j i", j=4),
                    bank[6 + half][lo:lo + 64, :].rearrange("p (j h i) -> p j h i", j=4, h=2)[:, :, hd, :])

        def win_dve(dve, W, a, scales, add):
            pieces = W.per["win_proj"]

            def maxes(i, u, half):
                dve.wait_ge(sem("win_s"), W.at("win_s", i, u, half + 1))
                s = bank[2 + half][:, :].rearrange("p (j k) -> p j k", j=4)[:, :, 0:a["keys"]]
                t = a["bias"][:, 4 * half:4 * half + 4, :]
                if W.slopes:
                    slope = vec[:, bass.ds(i * (UNROLL // B) + (u // B + VEC["slope"][0]), 1)]
                    ins = nc.vector.scalar_tensor_tensor(s, t, slope, s, ALU.mult, ALU.add)
                else:
                    ins = nc.vector.tensor_tensor(s, s, t, ALU.add)
                ins.then_inc(sem("win_biased"), 1)
                dve.wait_ge(sem("win_biased"), W.at("win_biased", i, u, half + 1))
                nc.vector.tensor_reduce(a["neg_max"][:, u % 2, 4 * half:4 * half + 4], s, AX_X, ALU.max, negate=True) \
                  .then_inc(sem("win_max"), 1)

            def to_diagonal(i, u, src, weight):
                dve.wait_ge(sem("win_rs"), W.at("win_rs", i, u, 1))
                for hd in range(2):
                    lo = 64 * hd
                    out_ = a["q"][u % 2][lo:lo + 64, :, lo:lo + 64]
                    q = src[lo:lo + 64, :].rearrange("p (j i) -> p j i", i=64)
                    rs = a["rs"][lo:lo + 64, 0, :].rearrange("p (j i) -> p j i", i=64)
                    if weight is None:
                        ins = nc.vector.tensor_tensor(out_, q, rs, ALU.mult)
                    else:
                        ins = nc.vector.scalar_tensor_tensor(out_, q, weight[lo:lo + 64, :], rs, ALU.mult, ALU.mult)
                    ins.then_inc(sem("win_q"), 1)

            def rotate(i, u, piece, first):
                dve.wait_ge(sem("win_sq"), W.at("win_sq", i, u, piece + 1))
                if u or not first:
                    if piece:
                        dve.wait_ge(sem("win_k"), W.at("win_k", i, u))
                    else:
                        dve.wait_ge(sem("win_sum"), W.at("win_sum", i, u, -2))
                        dve.wait_ge(sem("win_q"), W.at("win_q", i, u))
                src = proj_bank(W, u, piece)[:, :]
                nc.vector.tensor_tensor(a["part"][2 * piece][:, :], src, W.tables[:, 2 * piece, :], ALU.mult)
                nc.vector.stream_shuffle(a["part"][2 * piece + 1][:, :], src, SWAP).then_inc(sem("win_proj_read"), 1)

            def clip(i, u, j):
                dve.wait_ge(sem("win_ssq"), W.at("win_ssq", i, u, j + 1))
                nc.vector.tensor_scalar(a["sq"][:, j, :], bank[7 if j else 1][:, :], 1e-24, 2.0 ** 30, ALU.max, ALU.mult) \
                  .then_inc(sem("win_clip"), 1)

            def inverse(i, u):
                dve.wait_ge(sem("win_exp"), W.at("win_exp", i, u, 8))
                nc.vector.reciprocal(a["inv"][:, u % 2, :], a["sum"][:, u % 2, :]).then_inc(sem("win_inv"), 1)

            def heads(i, u):
                dve.wait_ge(sem("pv_raw"), W.at("pv_raw", i, u, 1))
                for hd in range(2):
                    dst, src = win_head(a, u, 0, hd)
                    nc.vector.tensor_copy(dst, src).then_inc(sem("win_pv_read"), 1)

            def output(i, u):
                dve.wait_ge(sem("win_out"), W.at("win_out", i, u, 1))
                dve.wait_ge(sem("pair_added"), W.at("pair_added", i, u))
                add(u % B).then_inc(sem("pair_added"), 1)

            def part(i, u, early, s, p, work, out, first):
                if early:
                    if p and pieces > 1:
                        rotate(i, u + 2, 0, first)
                        clip(i, u + 2, 0)
                    if s:
                        maxes(i, u + 1, 0)
                    if p and pieces > 1:
                        rotate(i, u + 2, 1, first)
                        clip(i, u + 2, 1)
                    if out:
                        output(i, u - 1)
                    return
                if p and pieces > 1:
                    dve.wait_ge(sem("win_sum"), W.at("win_sum", i, u + 2, 2))
                    to_diagonal(i, u + 2, a["part"][0], None)
                elif p:
                    to_diagonal(i, u + 2, proj_bank(W, u + 2, 0), scales[0])
                if s:
                    maxes(i, u + 1, 1)
                    inverse(i, u + 1)
                if work:
                    heads(i, u)

            win_loop(W, dve, part)

        def win_pool(pool, W, a):
            pieces = W.per["win_proj"]

            def sum_of(i, u, j):
                swapped = a["part"][2 * j + 1][:, :]
                pool.wait_ge(sem("win_proj_read"), W.at("win_proj_read", i, u, j + 1))
                nc.gpsimd.tensor_tensor(swapped, swapped, W.tables[:, 2 * j + 1, :], ALU.mult) \
                  .then_inc(sem("win_sum"), 1)
                pool.wait_ge(sem("win_sum"), W.at("win_sum", i, u, 2 * j + 1))
                nc.gpsimd.tensor_tensor(a["part"][2 * j][:, :], a["part"][2 * j][:, :], swapped,
                                        ALU.add).then_inc(sem("win_sum"), 1)

            def key(i, u, first):
                pool.wait_ge(sem("win_sum"), W.at("win_sum", i, u, 4))
                pool.wait_ge(sem("win_rs"), W.at("win_rs", i, u, 2))
                if not first:
                    pool.wait_ge(sem("win_s"), W.at("win_s", i, u, -2))
                nc.gpsimd.tensor_tensor(a["k"][u % 2][:, PAD:TP], a["part"][2][:, :], a["rs"][:, 1, :], ALU.mult) \
                  .then_inc(sem("win_k"), 1)

            def divide(i, u):
                pool.wait_ge(sem("win_inv"), W.at("win_inv", i, u, 1))
                nc.gpsimd.tensor_tensor(a["soft"][u % 2][:, :, :], a["soft"][u % 2][:, :, :],
                                        a["inv"][:, u % 2, :].unsqueeze(2).to_broadcast([128, NBLK, a["keys"]]),
                                        ALU.mult).then_inc(sem("win_normed"), 1)

            def part(i, u, early, s, p, work, out, first):
                if not early:
                    if p and pieces > 1:
                        sum_of(i, u + 2, 0)
                        sum_of(i, u + 2, 1)
                        key(i, u + 2, first)
                    if s:
                        divide(i, u + 1)

            win_loop(W, pool, part)

        def win_sp(sp, W, a, w_of, wo_of):
            for p in range(2):
                sp.dma_start(a["w"][p][:, :, :], w_of(p)).then_inc(sem(f"w_loaded{p}"), 16)
            sp.dma_start(a["wo"][:, :], wo_of(0)).then_inc(sem("wo_loaded"), 16)

            def next_wo(i, p):
                sp.wait_ge(sem("win_out"), W.at("win_out", i, B * p + B))
                sp.dma_start(a["wo"][:, :], wo_of(i * 2 + (p + 1))).then_inc(sem("wo_loaded"), 16)

            rounds = W.units // UNROLL
            with sp.Fori(0, rounds - 1) as i:
                for p in range(2):
                    sp.wait_ge(sem("win_proj"), W.at("win_proj", i, B * p + B))
                    sp.dma_start(a["w"][p][:, :, :], w_of(i * 2 + (p + 2))).then_inc(sem(f"w_loaded{p}"), 16)
                    next_wo(i, p)
            next_wo(rounds - 1, 0)

        next_block()
        kv_k = [tmp_sb(f"kv_k{i}", [128, B, TP]) for i in range(2)]
        kv_v = [tmp_sb(f"kv_v{b}", [128, NBLK, 256]) for b in range(B)]
        kv_w = tmp_sb("kv_w", [C, 2, 256])
        kv_sq = tmp_sb("kv_sq", [128, 2, T])
        kv_log = tmp_sb("kv_log", [128, 2, T])
        kv_rs = tmp_sb("kv_rs", [128, 2, T])
        q_w8 = tmp_sb("q_w8", [128, 1])
        A6 = win_alloc(1, False, SHORT)
        start = dict({m: 0 for m in PLAIN}, pv_raw=B + 2 * B * PAIRS, pair_added=B + B * PAIRS)
        W6 = Window(PAIRS * B, start, PLAIN, PAIRS, slopes=True)

        def kv_pe(pe):
            pe.wait_ge(sem("h_ready"), 28)
            pe.wait_ge(sem("ln_normed"), 28)
            pe.wait_ge(sem("kv_loaded"), 48)

            def key(j):
                if j >= 3:
                    pe.wait_ge(sem("kv_key"), j - 2)
                pe.matmul(bank[j % 3][:, :], kv_w[:, 0, 128 * (j % 2):128 * (j % 2) + 128], hb(j // 2),
                          start=True, stop=True).then_inc(sem("kv_raw"), 1)

            def square_sum(j):
                pe.wait_ge(sem("kv_squared"), j + 1)
                if j:
                    pe.wait_ge(sem("kv_logged"), j)
                pe.matmul(bank[3][:, :], head_sum[:, :], kv_sq[:, j % 2, :], start=True, stop=True) \
                  .then_inc(sem("kv_ssq"), 1)

            def value(f):
                if f >= 4:
                    pe.wait_ge(sem("kv_v_read"), f - 3)
                for i in range(2):
                    blk = 2 * (f % 4) + i
                    last = pe.matmul(bank[4 + f % 4][0:SHORT, 256 * i:256 * i + 256], hh(f // 4, 64 * blk + 64 - SHORT, SHORT),
                                     kv_w[:, 1, :], start=True, stop=True)
                last.then_inc(sem("kv_v_raw"), 1)

            key(0)
            key(1)
            square_sum(0)
            for j in range(2 * B):
                if j + 2 < 2 * B:
                    key(j + 2)
                value(2 * j)
                if j + 1 < 2 * B:
                    square_sum(j + 1)
                value(2 * j + 1)

        def kv_act(act):
            def square(j):
                act.wait_ge(sem("kv_raw"), j + 1)
                if j >= 2:
                    act.wait_ge(sem("kv_ssq"), j - 1)
                nc.scalar.activation(kv_sq[:, j % 2, :], bank[j % 3][:, :], ACT.Square).then_inc(sem("kv_squared"), 1)

            square(0)
            for j in range(2 * B):
                if j + 1 < 2 * B:
                    square(j + 1)
                act.wait_ge(sem("kv_ssq"), j + 1)
                nc.scalar.activation(kv_log[:, j % 2, :], bank[3][:, :], ACT.Ln, bias=rms_eps[:, 0:1],
                                     scale=1.0 / 64).then_inc(sem("kv_logged"), 1)
                act.wait_ge(sem("kv_logged"), j + 1)
                if j >= 2:
                    act.wait_ge(sem("kv_key"), j - 1)
                nc.scalar.activation(kv_rs[:, j % 2, :], kv_log[:, j % 2, :], ACT.Exp, scale=-0.5) \
                  .then_inc(sem("kv_rs_ready"), 1)
                for f in (2 * j, 2 * j + 1):
                    act.wait_ge(sem("kv_v_raw"), f + 1)
                    nc.scalar.activation(kv_v[f // 4][0:SHORT, 2 * (f % 4):2 * (f % 4) + 2, :],
                                         bank[4 + f % 4][0:SHORT, :].rearrange("p (i c) -> p i c", i=2), ACT.Copy) \
                      .then_inc(sem("kv_v_read"), 1)

        def kv_dve(dve):
            link(dve, "dve", nc.vector.tensor_scalar(q_w8[:, :], v("qn_w"), 0.125, None, ALU.mult))
            for i in range(2):
                link(dve, "dve", nc.vector.memset(A6["q"][i][:, :, :], 0.0))
                link(dve, "dve", nc.vector.memset(kv_k[i][:, :, 0:PAD], 0.0))
            for j in range(2 * B):
                dve.wait_ge(sem("kv_rs_ready"), j + 1)
                nc.vector.scalar_tensor_tensor(kv_k[j % 2][:, j // 2, PAD:TP], bank[j % 3][:, :], v("kn_w"),
                                               kv_rs[:, j % 2, :], ALU.mult, ALU.mult).then_inc(sem("kv_key"), 1)
            dve.wait_ge(sem("win_bias_loaded"), 16)

        def alibi_pe(pe):
            pe.wait_ge(sem("kv_key"), 2 * B)
            pe.wait_ge(sem("kv_v_read"), 4 * B)
            win_pe(pe, W6, A6, tokens=lambda b, lo, n: hh(b, lo, n),
                   keys_of=lambda u, j: kv_k[u // B][:, u % B, 64 * j + 128 - SHORT:64 * j + 128],
                   values_of=lambda u, j: kv_v[u % B][0:SHORT, j, 128 * (u // B):128 * (u // B) + 128])

        def alibi_dve(dve):
            win_dve(dve, W6, A6, [q_w8[:, 0:1]],
                    lambda b: nc.vector.scalar_tensor_tensor(x[:, b, :], bank[6][:, :], gate(6, b), x[:, b, :],
                                                             ALU.mult, ALU.add))

        def alibi_sp(sp):
            sp.wait_ge(sem("h_ready"), 25)
            sp.dma_start(kv_w[:, 0, :], d["kv_w"][:, 0, :]).then_inc(sem("kv_loaded"), 16)
            sp.dma_start(kv_w[:, 1, :], d["kv_w"][:, 1, :]).then_inc(sem("kv_loaded"), 16)
            sp.dma_start(A6["bias"][:, :, :], d["alibi_rel"]).then_inc(sem("win_bias_loaded"), 16)

            def one(name, i):
                return d[name][i, :, :] if isinstance(i, int) else \
                    d[name][bass.ds(i, 1), :, :].rearrange("o p n -> (o p) n")

            win_sp(sp, W6, A6, lambda i: one("alibi_wq", i).rearrange("p (j n) -> p j n", j=1),
                   lambda i: one("alibi_wo", i))

        next_block()
        shifted = tmp_sb("shifted", [C, B, TP])
        A7 = win_alloc(3, True, 128)
        qk_tab = tmp_sb("qk_tab", [128, 4, T])
        scaled_tab = tmp_sb("scaled_tab", [128, 4, T])
        w1 = tmp_sb("w1", [C, 2, 2 * HID])
        w2 = tmp_sb("w2", [128, 2, 3, C])
        mlp_gelu = [tmp_sb(f"mlp_gelu{i}", [128, T]) for i in range(2)]
        mlp_hid = A7["part"][0:3]
        mlp_in = [A7["v"][b][:, :, :].rearrange("p j c -> p (j c)")[:, 0:T] for b in range(B)]
        layers = []
        for l in range(2):
            layers.append(Window(4 * B, (layers[-1] if l else W6).after(), ROTATED, 2 * PAIRS + 4 * l, tables=scaled_tab))

        def shift_dve(dve, b):
            nc.vector.tensor_copy(shifted[0:64, b, PAD:TP], h[0:64, b, PAD:TP])
            nc.vector.tensor_copy(shifted[64:128, b, PAD:TP], h[64:128, b, PAD - 1:TP - 1]) \
              .then_inc(sem("shifted"), 1)

        def scale_tables(dve, l):
            for j, name in enumerate(("q_scale", "q_scale_rot", "k_scale", "k_scale_rot")):
                link(dve, "dve", nc.vector.tensor_scalar(scaled_tab[:, j, :], qk_tab[:, j, :], v(name, l), None, ALU.mult))

        def local_pe(pe, l):
            pe.wait_ge(sem("shifted"), 8 * l + B)
            if l == 0:
                pe.wait_ge(sem("ln_normed"), 32)
                pe.wait_ge(sem("local_cleared"), 5)
            win_pe(pe, layers[l], A7, tokens=lambda b, lo, n: shifted[:, b, PAD + lo:PAD + lo + n],
                   keys_of=lambda u, j: A7["k"][u % 2][:, 64 * j:64 * j + 128],
                   values_of=lambda u, j: A7["v"][u % B][:, j, :])

        def local_dve(dve, l):
            win_dve(dve, layers[l], A7, None,
                    lambda b: nc.vector.tensor_tensor(hb(b), hb(b), bank[6][:, :], ALU.add))

        def clear_pool(pool):
            nc.gpsimd.memset(shifted[:, :, 0:PAD], 0.0).then_inc(sem("local_cleared"), 1)
            for i in range(2):
                nc.gpsimd.memset(A7["k"][i][:, 0:PAD], 0.0).then_inc(sem("local_cleared"), 1)
                nc.gpsimd.memset(A7["q"][i][:, :, :], 0.0).then_inc(sem("local_cleared"), 1)

        def local_sp(sp):
            sp.wait_ge(sem("h_ready"), 29)
            sp.dma_start(A7["bias"][:, :, :], d["local_mask"]).then_inc(sem("win_bias_loaded"), 16)
            sp.dma_start(qk_tab[:, :, :], d["qk_tab"]).then_inc(sem("local_loaded"), 16)
            sp.dma_start(w1[:, :, :], d["local_w1"]).then_inc(sem("local_loaded"), 16)
            sp.dma_start(w2[:, :, :, :], d["local_w2"]).then_inc(sem("local_loaded"), 16)

            def one(name, l, i):
                return d[name][l, i, :, :] if isinstance(i, int) else \
                    d[name][l, bass.ds(i, 1), :, :].rearrange("o p n -> (o p) n")

            for l in range(2):
                if l:
                    sp.wait_ge(sem("win_out"), layers[0].after()["win_out"])
                win_sp(sp, layers[l], A7, lambda i: one("local_w", l, i).rearrange("p (j n) -> p j n", j=3),
                       lambda i: one("local_wo", l, i))

        def mlp_pe(pe, l):
            pe.wait_ge(sem("local_loaded"), 48)
            pe.wait_ge(sem("ln_normed"), 4 * (9 + l))

            def up(f):
                b, c = divmod(f, 3)
                n = min(128, HID - 128 * c)
                if c == 0:
                    pe.wait_ge(sem("h_ready"), 4 * (8 + l) + b + 1)
                if f >= 2:
                    pe.wait_ge(sem("mlp_hidden"), 12 * l + f - 1)
                for half in range(2):
                    lo = HID * half + 128 * c
                    last = pe.matmul(bank[4 + 2 * (f % 2) + half][0:n, :], w1[:, l, lo:lo + n], mlp_in[b],
                                     start=True, stop=True)
                last.then_inc(sem("up_raw"), 1)

            def down(f):
                b, c = divmod(f, 3)
                n = min(128, HID - 128 * c)
                pe.wait_ge(sem("mlp_hidden"), 12 * l + f + 1)
                pe.matmul(bank[b][:, :], w2[0:n, l, c, :], mlp_hid[c][0:n, :], start=(c == 0), stop=(c == 2)) \
                  .then_inc(sem("mlp_hid_read"), 1)

            up(0)
            for f in range(3 * B):
                if f + 1 < 3 * B:
                    up(f + 1)
                down(f)

        def mlp_act(act, l):
            for f in range(12 * l, 12 * l + 12):
                c = f % 3
                n = min(128, HID - 128 * c)
                act.wait_ge(sem("up_raw"), FB * B + f + 1)
                if f >= 2:
                    act.wait_ge(sem("mlp_hidden"), f - 1)
                nc.scalar.activation(mlp_gelu[f % 2][0:n, :], bank[5 + 2 * (f % 2)][0:n, :], ACT.Gelu,
                                     bias=v("b1g", 3 * l + c)[0:n, :]).then_inc(sem("up_acted"), 1)

        def mlp_dve(dve, l, then):
            def update(b):
                dve.wait_ge(sem("mlp_hid_read"), 12 * l + 3 * b + 3)
                link(dve, "dve", nc.vector.scalar_tensor_tensor(hb(b), bank[b][:, :], v("b2", l), hb(b),
                                                                ALU.add, ALU.add))
                then(b)

            for b in range(B):
                for c in range(3):
                    f = 12 * l + 3 * b + c
                    n = min(128, HID - 128 * c)
                    dve.wait_ge(sem("up_acted"), FB * B + f + 1)
                    if b:
                        dve.wait_ge(sem("mlp_hid_read"), f - 2)
                    nc.vector.scalar_tensor_tensor(mlp_hid[c][0:n, :], bank[4 + 2 * (f % 2)][0:n, :],
                                                   v("b1a", 3 * l + c)[0:n, :], mlp_gelu[f % 2][0:n, :],
                                                   ALU.add, ALU.mult).then_inc(sem("mlp_hidden"), 1)
                    if b and c == 0:
                        update(b - 1)
            update(B - 1)

        def final_dve(dve, b):
            nc.vector.scalar_tensor_tensor(x[:, b, :], hb(b), gate(7, b), x[:, b, :], ALU.mult, ALU.add) \
              .then_inc(sem("x_ready"), 1)

        @block.sync
        def _(sp):
            sp.dma_start(cond[:, :], d["cond"]).then_inc(sem("cond_loaded"), 16)
            sp.dma_start(centre[:, :], d["centre"]).then_inc(sem("ln_loaded"), 16)
            sp.dma_start(x[:, 0, :], d["x"][:, 0, :]).then_inc(sem("x_loaded0"), 16)
            sp.dma_start(mean[:, :], d["mean"]).then_inc(sem("ln_loaded"), 16)
            for b in range(1, B):
                sp.dma_start(x[:, b, :], d["x"][:, b, :]).then_inc(sem(f"x_loaded{b}"), 16)
            sp.dma_start(wmod[:, :, :], d["wmod"]).then_inc(sem("wmod_loaded"), 16)
            sp.dma_start(ident[:, :], d["ident"]).then_inc(sem("consts"), 16)
            sp.dma_start(vec[:, :], d["vec"]).then_inc(sem("consts"), 16)
            sp.dma_start(conv_w[:, :], d["conv_w"]).then_inc(sem("consts"), 16)
            for p in range(2):
                sp.dma_start(conv_bias[64 * p:64 * p + 64, :, :],
                             d["conv_bias"][p:p + 1, :, :].to_broadcast([64, 16, K])).then_inc(sem("conv_tables"), 16)
            sp.dma_start(conv_mask[:, :, :], d["conv_mask"]).then_inc(sem("conv_tables"), 16)
            sp.dma_start(conv_edge[:, :], d["conv_edge"]).then_inc(sem("conv_tables"), 16)
            sp.dma_start(head_sum[:, :], d["head_sum"]).then_inc(sem("kv_loaded"), 16)
            sp.dma_start(lr_u1[:, :], d["lr_u1"]).then_inc(sem("early_loaded"), 16)
            sp.dma_start(lr_v1[:, :], d["lr_v1"]).then_inc(sem("early_loaded"), 16)
            sp.dma_start(lr_u2[:, :, :], d["lr_u2"]).then_inc(sem("early_loaded"), 16)
            sp.dma_start(lr_v2[:, :], d["lr_v2"]).then_inc(sem("early_loaded"), 16)
            sp.dma_start(scan_w[:, :, :], d["scan_w"]).then_inc(sem("early_loaded"), 16)
            sp.dma_start(mix_w[:, :, :], d["mix_w"]).then_inc(sem("early_loaded"), 16)
            for p in range(2):
                sp.dma_start(att_w[p][:, :, :], d["att_w"][p, :, :, :]).then_inc(sem(f"w_loaded{p}"), 16)
            sp.dma_start(rope_tab[:, :, :], d["rope_tab"]).then_inc(sem("att_tables"), 16)
            sp.dma_start(att_mask[:, :], d["att_mask"]).then_inc(sem("att_tables"), 16)
            moe_sp(sp)
            att_sp(sp)
            alibi_sp(sp)
            local_sp(sp)
            for b in range(B):
                sp.wait_ge(sem("x_ready"), LAST + b + 1)
                sp.dma_start(out[:, b, :], x[:, b, :]).then_inc(sem("stored"), 16)
            sp.wait_ge(sem("stored"), 16 * B)

        @block.gpsimd
        def _(pool):
            nc.gpsimd.memset(rms_eps[:, :], 0.01)
            nc.gpsimd.memset(ln_clip[:, :], 15.0 * LN2)
            nc.gpsimd.memset(eps_col[:, :], EPS).then_inc(sem("filled"), 1)
            nc.gpsimd.memset(zeros[:, :], 0.0).then_inc(sem("filled"), 1)
            nc.gpsimd.memset(h[:, :, 0:PAD], 0.0)
            ln_pool(pool, 0)
            ln_pool(pool, 1)
            ln_pool(pool, 2)
            scan_pool(pool)
            ln_pool(pool, 3)
            moe_pool(pool)
            ln_pool(pool, 4)
            att_pool(pool)
            ln_pool(pool, 5)
            mix_pool(pool)
            ln_pool(pool, 6)
            win_pool(pool, W6, A6)
            ln_pool(pool, 7)
            clear_pool(pool)
            pool.wait_ge(sem("local_cleared"), 5)
            for l in range(2):
                win_pool(pool, layers[l], A7)
                ln_pool(pool, 8 + l)

        @block.scalar
        def _(act):
            mod_act(act)
            ln_act(act, 0)
            conv_act(act)
            act.wait_ge(sem("consts"), 48)
            ln_act(act, 1)
            lr_act(act)
            ln_act(act, 2)
            scan_act(act)
            ln_act(act, 3)
            moe_act_engine(act)
            ln_act(act, 4)
            att_act(act)
            ln_act(act, 5)
            mix_act(act)
            ln_act(act, 6)
            kv_act(act)
            win_act(act, W6, A6)
            ln_act(act, 7)
            for l in range(2):
                win_act(act, layers[l], A7)
                ln_act(act, 8 + l)
                mlp_act(act, l)

        @block.vector
        def _(dve):
            ln_dve(dve, 0, ahead=lambda b: mod_dve(dve) if b == 2 else None)
            conv_dve(dve)
            dve.wait_ge(sem("consts"), 48)
            ln_dve(dve, 1)
            lr_dve(dve)
            ln_dve(dve, 2)
            scan_dve(dve)
            ln_dve(dve, 3)
            moe_dve(dve)
            moe_out_dve(dve, 0)
            ln_dve(dve, 4, ahead=lambda b: moe_out_dve(dve, b + 1) if b + 1 < B else None)
            att_dve(dve)
            ln_dve(dve, 5)
            mix_dve(dve)
            ln_dve(dve, 6)
            kv_dve(dve)
            alibi_dve(dve)
            ln_dve(dve, 7)
            for b in range(B):
                dve.wait_ge(sem("h_ready"), 28 + b + 1)
                shift_dve(dve, b)
            dve.wait_ge(sem("win_bias_loaded"), 32)
            dve.wait_ge(sem("local_loaded"), 48)
            dve.wait_ge(sem("local_cleared"), 5)
            scale_tables(dve, 0)
            for l in range(2):
                local_dve(dve, l)
                dve.wait_ge(sem("pair_added"), layers[l].after()["pair_added"])
                for b in range(B):
                    shift_dve(dve, b)
                if l == 0:
                    scale_tables(dve, 1)
                ln_dve(dve, 8 + l)
                mlp_dve(dve, l, (lambda b: final_dve(dve, b)) if l else (lambda b: shift_dve(dve, b)))

        @block.tensor
        def _(pe):
            pe.wait_ge(sem("ln_loaded"), 32)
            ln_pe(pe, 0, behind_two=lambda: mod_pe(pe))
            pe.wait_ge(sem("consts"), 48)
            conv_pe(pe)
            ln_pe(pe, 1, after_all=True)
            lr_pe(pe)
            ln_pe(pe, 2, after_all=True)
            scan_pe(pe)
            ln_pe(pe, 3, after_all=True)
            moe_pe(pe)
            ln_pe(pe, 4, before=lambda b: moe_out_pe(pe, b))
            att_pe(pe)
            ln_pe(pe, 5)
            mix_pe(pe)
            ln_pe(pe, 6)
            kv_pe(pe)
            alibi_pe(pe)
            ln_pe(pe, 7, after_all=True)
            for l in range(2):
                local_pe(pe, l)
                ln_pe(pe, 8 + l, after_all=True)
                mlp_pe(pe, l)


def _layouts(a):
    f = np.float32
    d = {"x": a["L0_attn_x"].transpose(2, 0, 1)}
    d["cond"] = np.concatenate([a[f"L{i}_c"] for i in range(4)], 0).T
    d["wmod"] = np.stack([a[f"L{i}_wmod"] for i in range(4)], 1)
    d["ident"] = np.eye(128, dtype=f)
    d["centre"] = (np.eye(C) - 1.0 / C).astype(f)
    d["mean"] = np.full((C, C), 1.0 / C, f)
    vec = np.zeros((128, NVEC), f)

    def put(name, *cols):
        for i, col in enumerate(cols):
            vec[:len(col), VEC[name][0] + i] = col

    put("ffn0_b1", *a["L0_ffn_b1"].reshape(4, 128))
    put("ffn0_b2", a["L0_ffn_b2"])
    for n in ("ba", "bb", "bc"):
        put("scan_" + n, a["L1_attn_" + n])
    put("r1_b", a["L1_ffn_r1_b"])
    put("attn2_bo", a["L2_attn_bo"])
    put("mu_r", a["L2_ffn_mu_r"])
    put("mu_k", a["L2_ffn_mu_k"])
    put("qn_w", np.tile(a["L3_attn_q_norm_w"], 2))
    put("kn_w", np.tile(a["L3_attn_k_norm_w"], 2))
    couples = np.arange(64).reshape(2, 32).T.reshape(-1)
    for l in range(2):
        for n in ("q_scale", "k_scale"):
            s = a["L3_ffn_" + n][l]
            vec[:, VEC[n][0] + l] = np.tile(s[couples], 2)
            vec[:, VEC[n + "_rot"][0] + l] = np.tile(s[couples[np.arange(64) ^ 1]], 2)
    put("ln_g", *a["L3_ffn_ln_g"])
    put("ln_b", *a["L3_ffn_ln_b"])
    put("b2", *a["L3_ffn_b2"])
    for l in range(2):
        for j in range(3):
            n = min(128, HID - 128 * j)
            vec[:n, VEC["b1a"][0] + 3 * l + j] = a["L3_ffn_b1"][l, 128 * j:128 * j + n]
            vec[:n, VEC["b1g"][0] + 3 * l + j] = a["L3_ffn_b1"][l, HID + 128 * j:HID + 128 * j + n]
    for p in range(8):
        vec[:, VEC["slope"][0] + p] = np.repeat(2.0 ** (-0.5 * (2 * p + 1 + np.arange(2))), 64)
    d["vec"] = vec
    j = np.arange(32)
    d["conv_w"] = a["L0_attn_W"].T[:, np.tile(j, 2)]
    res = np.arange(32).reshape(16, 2).T
    d["conv_bias"] = a["L0_attn_b"][(j[None, None, :] - res[:, :, None]) % 32]
    s = np.arange(128)[:, None, None] - 32 * np.arange(4)[None, :, None] - j[None, None, :]
    d["conv_mask"] = ((s >= 0) & (s < 32)).astype(f)
    d["conv_edge"] = (j[:, None] < j[None, :]).astype(f)
    d["lr_u1"], d["lr_v1"], d["lr_v2"] = a["L0_ffn_U1"], a["L0_ffn_V1"], a["L0_ffn_V2"]
    d["lr_u2"] = a["L0_ffn_U2"].reshape(4, 128, 32).transpose(1, 0, 2)
    d["scan_w"] = np.stack([a["L1_attn_W" + n].T for n in "abc"], 1)
    r1 = a["L1_ffn_r1_w"].T
    d["r1_c"], d["r1_s"], d["r2_w"] = r1[:C], r1[C:], a["L1_ffn_r2_w"].T
    d["iota_e"] = np.tile(np.arange(32, dtype=f), (128, 1))
    p = np.arange(128)
    d["chunk_sum"] = ((p[:, None] % 32 == p[None, :] % 32) & (p[:, None] // 32 < p[None, :] // 32)).astype(f)
    up = a["L1_ffn_w_up"].transpose(0, 2, 1).reshape(16, 2, C, 512).transpose(0, 2, 1, 3).reshape(16, C, 1024)
    down = a["L1_ffn_w_down"].transpose(0, 2, 1).reshape(16, 2, 2, 128, C).transpose(0, 3, 1, 2, 4).reshape(16, 128, 512)
    d["moe_w"] = np.concatenate([up, down, a["L1_ffn_a_up"].transpose(0, 2, 1), a["L1_ffn_a_down"].transpose(0, 2, 1)], 2)
    def pairs(w):
        return w.reshape(C, 8, 128).transpose(1, 0, 2)

    d["att_w"] = np.stack([pairs(a["L2_attn_W" + n]) for n in "qkv"], 2)
    d["att_wo"] = a["L2_attn_Wo"].reshape(8, 128, C)
    inv = (1.0 / (np.float32(10000.0) ** (np.arange(0, 64, 2, dtype=f) / f(64)))).astype(f)
    ang = (np.arange(T, dtype=f)[None, :] * inv[:, None]).astype(f).astype(np.float64)
    cos, sin = (np.tile(np.repeat(t(ang), 2, 0), (2, 1)) for t in (np.cos, np.sin))
    sin = sin * np.where(np.arange(128) % 2 == 0, -1.0, 1.0)[:, None]
    d["rope_tab"] = np.stack([cos / 8, sin / 8, cos, sin], 1).astype(f)
    i64 = np.arange(128) % 64
    d["att_mask"] = np.where(np.arange(64)[None, :] <= i64[:, None], 0.0, -1e30).astype(f)
    d["mix_w"] = np.stack([a["L2_ffn_W_" + n].T for n in "rkv"], 1)
    d["head_sum"] = (p[:, None] // 64 == p[None, :] // 64).astype(f)
    d["kv_w"] = np.stack([a["L3_attn_wk"].T, a["L3_attn_wv"].T], 1)
    d["alibi_wq"] = pairs(a["L3_attn_wq"].T)
    d["alibi_wo"] = a["L3_attn_wo"].T.reshape(8, 128, C)
    qi, kj = i64[:, None, None], np.arange(128)[None, None, :]
    rel = kj - 64 - qi + 0 * np.arange(8)[None, :, None]
    there = (kj >= 64) | (np.arange(8)[None, :, None] > 0)
    d["alibi_rel"] = np.where((rel <= 0) & (rel >= -16) & there, rel, -1e30).astype(f)[:, :, 128 - SHORT:]
    d["local_mask"] = np.where((rel <= 0) & (rel >= -64) & there, 0.0, -1e30).astype(f)
    w = a["L3_ffn_wqkv"].reshape(2, C, 3, 4, 128).transpose(2, 0, 3, 1, 4)
    c2 = np.concatenate([couples, 64 + couples])
    d["local_w"] = np.stack([w[0][..., c2], w[1][..., c2], w[2]], 3).reshape(2, 4, C, 384)
    d["local_wo"] = a["L3_ffn_wo"].reshape(2, 4, 128, C)
    d["local_w1"] = a["L3_ffn_w1"].transpose(1, 0, 2)
    w2 = np.zeros((128, 2, 3, C), f)
    for j in range(3):
        n = min(128, HID - 128 * j)
        w2[:n, :, j, :] = a["L3_ffn_w2"][:, 128 * j:128 * j + n, :].transpose(1, 0, 2)
    d["local_w2"] = w2
    idx = np.arange(0, 64, 2, dtype=f)
    t = np.arange(T, dtype=f)
    ang = (t[None, :] * inv[:, None]).astype(f).astype(np.float64)
    base = ((idx + f(0.4 * 64)) / f(1.4 * 64)).astype(np.float64)
    sc = base[:, None] ** ((t[None, :].astype(np.float64) - T // 2) / 32.0)
    cos, sin, sc = (np.tile(np.repeat(t, 2, 0), (2, 1)) for t in (np.cos(ang), np.sin(ang), sc))
    sin = sin * np.where(p % 2 == 0, -1.0, 1.0)[:, None]
    d["qk_tab"] = np.stack([8 * cos * sc, 8 * sin * sc, cos / sc, sin / sc], 1).astype(f)
    return d


def kernel(**inputs):
    import concourse.bacc as _bacc
    from concourse.bass_utils import run_bass_kernel_spmd as _run

    nc = _bacc.Bacc("TRN2", target_bir_lowering=False, num_devices=1)
    arrays, aps = {}, {}
    for name, a in _layouts({k: np.asarray(val) for k, val in inputs.items()}).items():
        a = np.ascontiguousarray(a)
        arrays["in_" + name] = a
        aps[name] = nc.dram_tensor("in_" + name, a.shape, mybir.dt.from_np(a.dtype), kind="ExternalInput").ap()
    out = nc.dram_tensor("out_x", (C, B, T), F32, kind="ExternalOutput").ap()
    adaln_blocks(nc, aps, out)
    r = _run(nc, [arrays], core_ids=[0])
    return np.ascontiguousarray(r.results[0]["out_x"].transpose(1, 2, 0))
```
